# Optimizing a Trainium2 kernel written in Bass

```python
import numpy as np
import jax
import jax.numpy as jnp

def _softmax(x, axis=-1):
    return jax.nn.softmax(x, axis=axis)

def _gelu(x):
    return jax.nn.gelu(x, approximate=True)

def _silu(x):
    return jax.nn.silu(x)

def _sigmoid(x):
    return jax.nn.sigmoid(x)

def _layernorm(x, axis=-1, eps=1e-05):
    m = jnp.mean(x, axis=axis, keepdims=True)
    v = jnp.var(x, axis=axis, keepdims=True)
    return (x - m) / jnp.sqrt(v + eps)

def _scatter_add(tgt, idx, src, axis=0):
    return tgt.at[idx].add(src)

def _segment_sum(src, seg, n):
    return jax.ops.segment_sum(src, seg, n)
kernel_name = 'mk_decoder_preln_d1_seqx_r8_2e1750'

def setup_inputs(seed: int=0):
    np.random.seed(seed)
    _w = jnp.asarray

    def _rec_inputs():
        import jax
        import jax.numpy as jnp
        _rk = jax.random.key(seed)
        x = 7.22e-05 + 1 * jax.random.normal(jax.random.fold_in(_rk, 1), (16, 128, 256), jnp.float32)
        _lenS = 128 - jax.random.randint(jax.random.fold_in(_rk, 7), (16,), 0, max(1, 128 // 4) + 1, jnp.int32)
        _lenS2 = 128 - jax.random.randint(jax.random.fold_in(_rk, 8), (16,), 0, max(1, 128 // 4) + 1, jnp.int32)
        _ctx_512P = jax.random.normal(jax.random.fold_in(_rk, 11), (16, 16, 64), jnp.float32)
        _ctx_512c = jax.random.dirichlet(jax.random.fold_in(_rk, 511), 0.3 * jnp.ones((16,), jnp.float32), (16, 128))
        _ctx_512t = jnp.einsum('bsk,bkd->bsd', _ctx_512c, _ctx_512P)
        _ctx_512t = _ctx_512t * jax.lax.rsqrt(jnp.mean(jnp.square(_ctx_512t)) + 1e-12) * 0.953939
        ctx_512 = -0.000514642 + 1.00011 * (_ctx_512t + 0.3 * jax.random.normal(jax.random.fold_in(_rk, 611), (16, 128, 64), jnp.float32))
        return (x, ctx_512)
    x, ctx_512 = _rec_inputs()

    def _L0_attn_setup():
        import jax, jax.numpy as jnp
        import numpy as np
        D_IN = 256
        D_OUT = 256
        NUM_HEADS = 16
        NUM_KV_GROUPS = 4
        GROUP_SIZE = NUM_HEADS // NUM_KV_GROUPS
        HEAD_DIM = D_OUT // NUM_HEADS
        key = jax.random.key(seed)
        ks = jax.random.split(key, 6)
        b, n = (2, 256)
        x = jax.random.normal(ks[0], (b, n, D_IN), dtype=jnp.float32)
        Wq = jax.random.normal(ks[1], (D_IN, D_OUT), dtype=jnp.float32) * (1.0 / np.sqrt(D_IN))
        Wk = jax.random.normal(ks[2], (D_IN, NUM_KV_GROUPS * HEAD_DIM), dtype=jnp.float32) * (1.0 / np.sqrt(D_IN))
        Wv = jax.random.normal(ks[3], (D_IN, NUM_KV_GROUPS * HEAD_DIM), dtype=jnp.float32) * (1.0 / np.sqrt(D_IN))
        Wo = jax.random.normal(ks[4], (D_OUT, D_OUT), dtype=jnp.float32) * (1.0 / np.sqrt(D_OUT))
        bo = jax.random.normal(ks[5], (D_OUT,), dtype=jnp.float32) * 0.01
        return {'x': x, 'Wq': Wq, 'Wk': Wk, 'Wv': Wv, 'Wo': Wo, 'bo': bo}
    _L0_attn_all = _L0_attn_setup()
    _L0_attn_in = {k: v for k, v in _L0_attn_all.items() if k in ('Wq', 'Wk', 'Wv', 'Wo', 'bo')}
    del _L0_attn_all

    def _L0_xattn_setup():
        import jax, jax.numpy as jnp
        import numpy as np
        N_HEADS = 16
        N_KV_HEADS = 4
        ROPE_THETA = 10000.0
        EPS = 1e-05

        def _rms_norm(x, w):
            var = jnp.mean(x * x, axis=-1, keepdims=True)
            return x * jax.lax.rsqrt(var + EPS) * w

        def _rope_sin_cos(T, head_dim, dtype):
            inv_freq = 1.0 / ROPE_THETA ** (jnp.arange(0, head_dim, 2, dtype=jnp.float32) / head_dim)
            t = jnp.arange(T, dtype=jnp.float32)
            freqs = jnp.outer(t, inv_freq)
            emb = jnp.concatenate([freqs, freqs], -1)
            return (jnp.sin(emb).astype(dtype)[None, None], jnp.cos(emb).astype(dtype)[None, None])

        def _rotate_half(x):
            h = x.shape[-1] // 2
            x1, x2 = (x[..., :h], x[..., h:])
            return jnp.concatenate([-x2, x1], axis=-1)
        key = jax.random.key(seed)
        ks = jax.random.split(key, 6)
        B, T, C = (2, 256, 256)
        Ckv = C // N_HEADS * N_KV_HEADS
        return {'q': jax.random.normal(ks[0], (B, T, C), jnp.float32), 'k': jax.random.normal(ks[1], (B, T, Ckv), jnp.float32), 'v': jax.random.normal(ks[2], (B, T, Ckv), jnp.float32), 'q_norm_w': jnp.ones((C,), jnp.float32), 'k_norm_w': jnp.ones((Ckv,), jnp.float32), 'w_out': jax.random.normal(ks[3], (C, C), jnp.float32) * C ** (-0.5)}
    _L0_xattn_all = _L0_xattn_setup()
    _L0_xattn_in = {k: v for k, v in _L0_xattn_all.items() if k in ('q_norm_w', 'k_norm_w', 'w_out')}
    del _L0_xattn_all

    def _L0_ffn_setup():
        import jax, jax.numpy as jnp
        import numpy as np
        B, S, H = (4, 256, 256)
        INTER = 512
        E = 8
        TOPK = 2
        SHARED_I = INTER * 2

        def moe_forward(hidden_states, router_w, w1, w2, w_gate, w_up, w_down):
            b, s, h = hidden_states.shape
            x = hidden_states.reshape(-1, h)
            T = x.shape[0]
            logits = x @ router_w
            top_logits, top_indices = jax.lax.top_k(logits, TOPK)
            scores = jax.nn.softmax(top_logits, axis=-1)
            flat_idx = top_indices.reshape(-1)
            sorted_pos = jnp.argsort(flat_idx, stable=True)
            permuted = x[sorted_pos // TOPK]
            expert_ids = flat_idx[sorted_pos]
            out = jnp.zeros((T * TOPK, h), x.dtype)
            for e in range(E):
                mask = (expert_ids == e)[:, None]
                f1 = permuted * mask @ w1[e]
                g, u = jnp.split(f1, 2, axis=-1)
                act = jax.nn.silu(g) * u
                out = out + jnp.where(mask, act @ w2[e], 0.0)
            unperm = jnp.zeros_like(out).at[sorted_pos].set(out)
            combined = (unperm.reshape(T, TOPK, h) * scores[..., None]).sum(axis=1)
            shared = jax.nn.silu(x @ w_gate) * (x @ w_up) @ w_down
            return (combined + shared).reshape(b, s, h)
        key = jax.random.key(seed)
        ks = jax.random.split(key, 7)
        s = 0.02
        return {'hidden_states': jax.random.normal(ks[0], (B, S, H), jnp.float32), 'router_w': jax.random.normal(ks[1], (H, E), jnp.float32) * s, 'w1': jax.random.normal(ks[2], (E, H, 2 * INTER), jnp.float32) * s, 'w2': jax.random.normal(ks[3], (E, INTER, H), jnp.float32) * s, 'w_gate': jax.random.normal(ks[4], (H, SHARED_I), jnp.float32) * s, 'w_up': jax.random.normal(ks[5], (H, SHARED_I), jnp.float32) * s, 'w_down': jax.random.normal(ks[6], (SHARED_I, H), jnp.float32) * s}
    _L0_ffn_all = _L0_ffn_setup()
    _L0_ffn_in = {k: v for k, v in _L0_ffn_all.items() if k in ('router_w', 'w1', 'w2', 'w_gate', 'w_up', 'w_down')}
    del _L0_ffn_all
    return {'x': x, 'ctx_512': ctx_512, 'L0_attn_Wq': _L0_attn_in['Wq'], 'L0_attn_Wk': _L0_attn_in['Wk'], 'L0_attn_Wv': _L0_attn_in['Wv'], 'L0_attn_Wo': _L0_attn_in['Wo'], 'L0_attn_bo': _L0_attn_in['bo'], 'L0_xattn_q_norm_w': _L0_xattn_in['q_norm_w'], 'L0_xattn_k_norm_w': _L0_xattn_in['k_norm_w'], 'L0_xattn_w_out': _L0_xattn_in['w_out'], 'L0_ffn_router_w': _L0_ffn_in['router_w'], 'L0_ffn_w1': _L0_ffn_in['w1'], 'L0_ffn_w2': _L0_ffn_in['w2'], 'L0_ffn_w_gate': _L0_ffn_in['w_gate'], 'L0_ffn_w_up': _L0_ffn_in['w_up'], 'L0_ffn_w_down': _L0_ffn_in['w_down']}

def reference(x, ctx_512, L0_attn_Wq, L0_attn_Wk, L0_attn_Wv, L0_attn_Wo, L0_attn_bo, L0_xattn_q_norm_w, L0_xattn_k_norm_w, L0_xattn_w_out, L0_ffn_router_w, L0_ffn_w1, L0_ffn_w2, L0_ffn_w_gate, L0_ffn_w_up, L0_ffn_w_down):
    import jax
    import jax.numpy as jnp

    def _L0_attn_ref(x, Wq, Wk, Wv, Wo, bo):
        import jax, jax.numpy as jnp
        import numpy as np
        D_IN = 256
        D_OUT = 256
        NUM_HEADS = 16
        NUM_KV_GROUPS = 4
        GROUP_SIZE = NUM_HEADS // NUM_KV_GROUPS
        HEAD_DIM = D_OUT // NUM_HEADS
        b, n, _ = x.shape
        q = (x @ Wq).reshape(b, n, NUM_KV_GROUPS, GROUP_SIZE, HEAD_DIM)
        k = (x @ Wk).reshape(b, n, NUM_KV_GROUPS, HEAD_DIM)
        v = (x @ Wv).reshape(b, n, NUM_KV_GROUPS, HEAD_DIM)
        scale = 1.0 / np.sqrt(HEAD_DIM).astype(np.float32)
        scores = jnp.einsum('bqgsd,bkgd->bgsqk', q, k) * scale
        causal = jnp.arange(n)[:, None] < jnp.arange(n)[None, :]
        scores = jnp.where(causal, -jnp.inf, scores)
        attn = jax.nn.softmax(scores, axis=-1)
        ctx = jnp.einsum('bgsqk,bkgd->bqgsd', attn, v)
        ctx = ctx.reshape(b, n, D_OUT)
        return ctx @ Wo + bo

    def _L0_xattn_ref(q, k, v, q_norm_w, k_norm_w, w_out):
        import jax, jax.numpy as jnp
        import numpy as np
        N_HEADS = 16
        N_KV_HEADS = 4
        ROPE_THETA = 10000.0
        EPS = 1e-05

        def _rms_norm(x, w):
            var = jnp.mean(x * x, axis=-1, keepdims=True)
            return x * jax.lax.rsqrt(var + EPS) * w

        def _rope_sin_cos(T, head_dim, dtype):
            inv_freq = 1.0 / ROPE_THETA ** (jnp.arange(0, head_dim, 2, dtype=jnp.float32) / head_dim)
            t = jnp.arange(T, dtype=jnp.float32)
            freqs = jnp.outer(t, inv_freq)
            emb = jnp.concatenate([freqs, freqs], -1)
            return (jnp.sin(emb).astype(dtype)[None, None], jnp.cos(emb).astype(dtype)[None, None])

        def _rotate_half(x):
            h = x.shape[-1] // 2
            x1, x2 = (x[..., :h], x[..., h:])
            return jnp.concatenate([-x2, x1], axis=-1)
        B, T, C = q.shape
        hd = C // N_HEADS
        g = N_HEADS // N_KV_HEADS
        q = _rms_norm(q, q_norm_w)
        k = _rms_norm(k, k_norm_w)
        q = q.reshape(B, T, N_HEADS, hd).transpose(0, 2, 1, 3)
        k = k.reshape(B, T, N_KV_HEADS, hd).transpose(0, 2, 1, 3)
        v = v.reshape(B, T, N_KV_HEADS, hd).transpose(0, 2, 1, 3)
        sin, cos = _rope_sin_cos(T, hd, q.dtype)
        q = q * cos + _rotate_half(q) * sin
        k = k * cos + _rotate_half(k) * sin
        qg = q.reshape(B, N_KV_HEADS, g, T, hd)
        scale = 1.0 / jnp.sqrt(jnp.asarray(hd, q.dtype))
        scores = jnp.einsum('bgnqd,bgkd->bgnqk', qg, k) * scale
        causal = jnp.tril(jnp.ones((T, T), bool))
        scores = jnp.where(causal, scores, jnp.asarray(-1e+30, scores.dtype))
        attn = jax.nn.softmax(scores, axis=-1)
        out = jnp.einsum('bgnqk,bgkd->bgnqd', attn, v)
        out = out.reshape(B, N_HEADS, T, hd).transpose(0, 2, 1, 3).reshape(B, T, C)
        return out @ w_out.T

    def _L0_ffn_ref(hidden_states, router_w, w1, w2, w_gate, w_up, w_down):
        import jax, jax.numpy as jnp
        import numpy as np
        B, S, H = (4, 256, 256)
        INTER = 512
        E = 8
        TOPK = 2
        SHARED_I = INTER * 2

        def moe_forward(hidden_states, router_w, w1, w2, w_gate, w_up, w_down):
            b, s, h = hidden_states.shape
            x = hidden_states.reshape(-1, h)
            T = x.shape[0]
            logits = x @ router_w
            top_logits, top_indices = jax.lax.top_k(logits, TOPK)
            scores = jax.nn.softmax(top_logits, axis=-1)
            flat_idx = top_indices.reshape(-1)
            sorted_pos = jnp.argsort(flat_idx, stable=True)
            permuted = x[sorted_pos // TOPK]
            expert_ids = flat_idx[sorted_pos]
            out = jnp.zeros((T * TOPK, h), x.dtype)
            for e in range(E):
                mask = (expert_ids == e)[:, None]
                f1 = permuted * mask @ w1[e]
                g, u = jnp.split(f1, 2, axis=-1)
                act = jax.nn.silu(g) * u
                out = out + jnp.where(mask, act @ w2[e], 0.0)
            unperm = jnp.zeros_like(out).at[sorted_pos].set(out)
            combined = (unperm.reshape(T, TOPK, h) * scores[..., None]).sum(axis=1)
            shared = jax.nn.silu(x @ w_gate) * (x @ w_up) @ w_down
            return (combined + shared).reshape(b, s, h)
        return moe_forward(hidden_states, router_w, w1, w2, w_gate, w_up, w_down)
    x = x + _L0_attn_ref(_layernorm(x, axis=-1), L0_attn_Wq, L0_attn_Wk, L0_attn_Wv, L0_attn_Wo, L0_attn_bo)
    x = x + _L0_xattn_ref(_layernorm(x, axis=-1), ctx_512, ctx_512, L0_xattn_q_norm_w, L0_xattn_k_norm_w, L0_xattn_w_out)
    x = x + _L0_ffn_ref(_layernorm(x, axis=-1), L0_ffn_router_w, L0_ffn_w1, L0_ffn_w2, L0_ffn_w_gate, L0_ffn_w_up, L0_ffn_w_down)
    return x

_drawn_inputs = setup_inputs


def setup_inputs(seed=0):
    import zlib

    import numpy as np

    out = dict(_drawn_inputs(seed))
    spreads = {'L0_xattn_q_norm_w': (1.0, 0.2), 'L0_xattn_k_norm_w': (1.0, 0.2)}
    factors = {'L0_attn_bo': 6.242,
     'L0_ffn_router_w': 4.609,
     'L0_ffn_w1': 3.966,
     'L0_ffn_w2': 3.962,
     'L0_ffn_w_gate': 3.129,
     'L0_ffn_w_up': 3.093,
     'L0_ffn_w_down': 3.097}
    for name, (base, spread) in spreads.items():
        noise = np.random.default_rng([zlib.crc32(name.encode()), seed]).standard_normal(out[name].shape)
        drawn = base * np.exp(spread * noise) if base else spread * noise
        out[name] = jnp.asarray(drawn.astype(out[name].dtype))
    for name, factor in factors.items():
        out[name] = (out[name] * factor).astype(out[name].dtype)
    return out
```

```python
from contextlib import ExitStack

import numpy as np
import concourse.bass as bass
from concourse import mybir

ALU = mybir.AluOpType
ACT = mybir.ActivationFunctionType
AX = mybir.AxisListType
F32 = mybir.dt.float32
F32R = mybir.dt.float32r
BF16 = mybir.dt.bfloat16
F16 = mybir.dt.float16
I32 = mybir.dt.int32

P = 128
D = 256
HEADS, GROUPS, HD = 16, 4, 16
KVD = GROUPS * HD
QKV = D + 2 * KVD
EPS = 1e-5
SCALE = 1.0 / HD ** 0.5
MASKED = -1e30
EXPERTS, INTER, TOPK = 8, 512, 2
SHARED = 2 * INTER
KT = D // P
FT = INTER // P
FLIGHT = 4

SLOTS = 6
STACK = SLOTS * HD
BLOCK = 2 + STACK
VCOLS = 1 + 3 * HD
KV = 2 * GROUPS
HALF = HEADS // 2

WEIGHT, ROW_ID, ROW = D, D + 1, D + 2

L_PRIORITY = 0
L_FULL = L_PRIORITY + EXPERTS


def constants(B, TILES):
    t = np.arange(P)
    ident = np.eye(P)
    causal = np.where(t[:, None] < t[None, :], MASKED, 0.0)
    earlier = (t[:, None] < t[None, :]) * 1.0
    first = (t[:, None] == 0) * np.ones((1, P))
    squares = np.stack([ident, causal, earlier, first], 1).astype(np.float32)
    freq = np.outer(t.astype(np.float32), (1.0 / 10000.0 ** (np.arange(0, HD, 2, dtype=np.float32) / HD)).astype(np.float32))
    cos = np.concatenate([np.cos(freq), np.cos(freq)], 1)
    sin = np.concatenate([-np.sin(freq), np.sin(freq)], 1)
    rope = np.stack([cos, sin], 1).astype(np.float32)
    row = np.concatenate([
        EXPERTS - np.arange(EXPERTS), 128.0 * np.arange(B), np.arange(TILES),
        np.tile((np.arange(B) > 0) * 1.0, EXPERTS), np.ones(EXPERTS)]).astype(np.float32)
    lanes = np.broadcast_to(row, (P, row.size)).copy()
    token = P * np.arange(B)[None, :] + t[:, None]
    row_ids = (TOPK * token[:, None, :] + np.arange(TOPK)[None, :, None]).astype(np.int32)
    return squares, rope, lanes, row_ids


def decoder_layer(nc, a, out):
    x, ctx_512 = a["x"], a["ctx_512"]
    B = x.shape[0]
    PAIRS = B // 2
    CHOICES = B * P * TOPK
    TILES = CHOICES // P + EXPERTS
    assert TILES % FLIGHT == 0 and B % 2 == 0
    NO_ROW = CHOICES
    dispatched = nc.dram_tensor("dispatched", (TILES * P, ROW), F32, kind="Internal").ap()
    combined = nc.dram_tensor("combined", (CHOICES, D), F32, kind="Internal").ap()

    L_IOTA = L_FULL + B
    L_CARRY = L_IOTA + TILES
    L_ONES = L_CARRY + EXPERTS * B

    top = ExitStack()

    def maker(scope):
        def sb(name, shape, dt):
            return scope.enter_context(nc.sbuf_tensor(name, shape, dt))
        return sb

    sb = maker(top)
    tokens = sb("tokens", [P, B, D], F32)
    over_shared = [nc.sbuf_base]
    wgu_hi = sb("wgu_hi", [P, KT, 2, 2, INTER], F32R)
    wgu_lo = sb("wgu_lo", [P, KT, 2, 2, INTER], F32R)
    wd_hi = sb("wd_hi", [P, 2, FT, D], F32R)
    wd_lo = sb("wd_lo", [P, 2, FT, D], F32R)
    rt_hi = sb("rt_hi", [P, KT, D], F32R)
    rt_lo = sb("rt_lo", [P, KT, D], F32R)
    squares = sb("squares", [P, 4, P], F32)
    identity, earlier_fp = squares[:, 0], squares[:, 2]
    lane = sb("lane", [P, L_ONES + EXPERTS], F32)
    bstats = sb("bstats", [P, 2, 6], F32)
    moments = sb("moments", [P, 2, 2], F32)
    variance = sb("variance", [P, 2, 1], F32)
    rstd = sb("rstd", [P, 2, 1], F32)
    minus_half = sb("minus_half", [P, B], F32)
    xn = [sb(f"xn{s}", [P, D], F32) for s in range(2)]
    actT_hi = [sb(f"actT_hi{s}", [P, KT, P], F32R) for s in range(2)]
    actT_lo = [sb(f"actT_lo{s}", [P, KT, P], F32R) for s in range(2)]

    phase_a = ExitStack()
    sb = maker(phase_a)
    wqkv_hi = sb("wqkv_hi", [P, KT, QKV], F32R)
    wqkv_lo = sb("wqkv_lo", [P, KT, QKV], F32R)
    wproj_hi = sb("wproj_hi", [P, 2, KT, D], F32R)
    wproj_lo = sb("wproj_lo", [P, 2, KT, D], F32R)
    bias_hi = sb("bias_hi", [P, D], F32R)
    bias_lo = sb("bias_lo", [P, D], F32R)
    first_row = sb("first_row", [P, P], F32R)
    raw = sb("raw", [P, KT * 2 * SHARED + FT * 2 * D], F32)
    raw_qkv = sb("raw_qkv", [P, KT, QKV], F32)
    raw_proj = sb("raw_proj", [P, 2, KT, D], F32)
    raw_bias = sb("raw_bias", [P, D], F32)
    raw_router = sb("raw_router", [P, KT, EXPERTS], F32)
    mask_bf = sb("mask_bf", [P, 4, P], BF16)
    ident_bf = sb("ident_bf", [P, P], BF16)
    rope = sb("rope", [P, 2, HD], F32)
    norm_w = sb("norm_w", [P, D + KVD], F32)
    cos_w = sb("cos_w", [P, D + KVD], F32)
    sin_w = sb("sin_w", [P, D + KVD], F32)
    cross_kv = sb("cross_kv", [P, B, KV, BLOCK], BF16)
    stack = [sb(f"stack{s}", [P, HEADS + KV, BLOCK], BF16) for s in range(2)]
    remainder = [sb(f"remainder{a}", [P, QKV], F32) for a in range(2)]
    cross_stack = sb("cross_stack", [P, HEADS, BLOCK], BF16)
    q_fp = sb("q_fp", [P, D], F32)
    q_sin = sb("q_sin", [P, D], F32)
    qT = [sb(f"qT{a}", [P, HEADS, P], BF16) for a in range(2)]
    kT = [sb(f"kT{a}", [P, GROUPS, P], BF16) for a in range(2)]
    row_max = [sb(f"row_max{u}", [P, HALF], F32) for u in range(2)]
    prob = [sb(f"prob{u}", [P, HALF, P], F32) for u in range(2)]
    prob_hi = [sb(f"prob_hi{u}", [P, HALF, P], F16) for u in range(2)]
    prob_lo = [sb(f"prob_lo{u}", [P, HALF, P], F16) for u in range(2)]
    heads = [sb(f"heads{a}", [P, HEADS, HD], F32) for a in range(2)]
    denom = [sb(f"denom{a}", [P, HEADS], F32) for a in range(2)]
    mixed = [sb(f"mixed{a}", [P, HEADS, HD], F32) for a in range(2)]
    ctx_sb = sb("ctx_sb", [P, B, KVD], F32)
    k_rstd = sb("k_rstd", [P, B], F32)
    empty_rows = sb("empty_rows", [P, ROW], F32)
    phase_a.close()
    kv_fp = raw[:, 0:B * 2 * KVD].rearrange("p (b n) -> p b n", b=B)
    kv_a = raw[:, B * 2 * KVD:2 * B * 2 * KVD].rearrange("p (b n) -> p b n", b=B)
    kv_b = raw[:, 2 * B * 2 * KVD:3 * B * 2 * KVD].rearrange("p (b n) -> p b n", b=B)
    raw_gu = raw[:, 0:KT * 2 * SHARED]
    raw_d = raw[:, KT * 2 * SHARED:]

    phase_c = ExitStack()
    sb = maker(phase_c)
    rows = sb("rows", [P, B, ROW], F32)
    w1_sb = sb("w1_sb", [P, EXPERTS, KT, 2, INTER], F32)
    w2_sb = sb("w2_sb", [P, EXPERTS, FT, D], F32)
    logits = sb("logits", [P, B, EXPERTS], F32)
    silu = [sb(f"silu{u}", [P, INTER], F32) for u in range(2)]
    hT_hi = [sb(f"hT_hi{u}", [P, FT, P], F32R) for u in range(2)]
    hT_lo = [sb(f"hT_lo{u}", [P, FT, P], F32R) for u in range(2)]
    phase_c.close()

    def over(name, shape, dt):
        words = int(np.prod(shape[1:]))
        t = nc.alloc_sbuf_tensor_at(name, shape, dt, offset=over_shared[0])
        over_shared[0] += -(-words * mybir.dt.size(dt) // 32) * 32
        return t

    tile_in = [over(f"tile_in{u}", [P, ROW], F32) for u in range(FLIGHT)]
    tile_out = [over(f"tile_out{u}", [P, D], F32) for u in range(FLIGHT)]
    best = [over(f"best{k}", [P, B], F32) for k in range(2)]
    hit = over("hit", [P, B, EXPERTS], F32)
    pick = [over(f"pick{k}", [P, B, EXPERTS], F32) for k in range(2)]
    top_priority = over("top_priority", [P, B], F32)
    masked_logits = over("masked_logits", [P, B, EXPERTS], F32)
    weight = [over(f"weight{k}", [P, B], F32) for k in range(2)]
    ratio = over("ratio", [P, B], F32)
    chosen = over("chosen", [P, B, EXPERTS], BF16)
    ones_bf = over("ones_bf", [P, P], BF16)
    earlier_bf = over("earlier_bf", [P, P], BF16)
    upto = over("upto", [P, EXPERTS, B], F32)
    begun = over("begun", [P, EXPERTS, B], F32)
    n_tiles = over("n_tiles", [P, EXPERTS], F32)
    end_tile = over("end_tile", [P, EXPERTS], F32)
    start_row = over("start_row", [P, EXPERTS], F32)
    place = over("place", [P, EXPERTS, B], F32)
    where_fp = [over(f"where_fp{k}", [P, B], F32) for k in range(2)]
    where = [over(f"where{k}", [P, B], I32) for k in range(2)]
    passed = over("passed", [P, TILES, EXPERTS], F32)
    tile_expert_fp = over("tile_expert_fp", [P, TILES], F32)
    tile_expert = over("tile_expert", [P, TILES], I32)
    row_id_sb = over("row_id_sb", [P, TOPK, B], I32)
    xT_fp = [over(f"xT_fp{u}", [P, KT, P], F32) for u in range(2)]
    hT_fp = [over(f"hT_fp{u}", [P, FT, P], F32) for u in range(2)]
    QUARTERS, QB = 4, B // 4
    products = w1_sb[:].rearrange("p e k g n -> p (e k g n)")[:, 0:B * TOPK * D].rearrange(
        "p (c b k n) -> p c b k n", c=QUARTERS, b=QB, k=TOPK)

    psum_a = ExitStack()
    ps_scores = psum_a.enter_context(nc.psum_tensor("ps_scores", [P, HALF, P], F32))
    ps_probs = psum_a.enter_context(nc.psum_tensor("ps_probs", [P, HALF, P], F32))
    ps_stack = psum_a.enter_context(nc.psum_tensor("ps_stack", [P, HALF, P], BF16))
    ps_heads = psum_a.enter_context(nc.psum_tensor("ps_heads", [P, 512], F32))
    ps_proj = psum_a.enter_context(nc.psum_tensor("ps_proj", [P, 512], F32))
    ps_actT = psum_a.enter_context(nc.psum_tensor("ps_actT", [P, 4, P], F32))
    psum_a.close()
    psum_c = ExitStack()
    ps_gu = [psum_c.enter_context(nc.psum_tensor(f"ps_gu{u}", [P, 2, INTER], F32)) for u in range(2)]
    ps_hT = psum_c.enter_context(nc.psum_tensor("ps_hT", [P, FT, P], F32))
    ps_y = psum_c.enter_context(nc.psum_tensor("ps_y", [P, 512], F32))
    ps_router = psum_c.enter_context(nc.psum_tensor("ps_router", [P, 512], F32))
    ps_xT = psum_c.enter_context(nc.psum_tensor("ps_xT", [P, 4, P], F32))
    psum_c.close()

    sems = ExitStack()

    def sem(name):
        return sems.enter_context(nc.semaphore(name))

    lane_loaded, squares_loaded, x_loaded, rest_loaded, qkv_loaded, consts_loaded, attn_loaded, ctx_loaded, shared_loaded = map(
        sem, ["lane_loaded", "squares_loaded", "x_loaded", "rest_loaded", "qkv_loaded", "consts_loaded", "attn_loaded", "ctx_loaded", "shared_loaded"])
    empty_made, emptied = sem("empty_made"), sem("emptied")
    filled_act, unread = sem("filled_act"), sem("unread")
    filled, hi_made, lo_made, kv_step, kv_var, kv_pow, kv_src, kv_h, kv_r, kv_m, kv_l = map(sem, [
        "filled", "hi_made", "lo_made", "kv_step", "kv_var", "kv_pow", "kv_src", "kv_h", "kv_r", "kv_m", "kv_l"])
    shared_hi, shared_lo, a_ends, b_ends = map(sem, ["shared_hi", "shared_lo", "a_ends", "b_ends"])
    def each(names, n):
        return [[sem(f"{name}{i}") for i in range(n)] for name in names]

    stats_done, moments_done, var_eps, rstd_done, xn_done = each(
        ["stats_done", "moments_done", "var_eps", "rstd_done", "xn_done"], 2)
    act_turned, act_hi_done, act_lo_done, projected, proj_read = each([
        "act_turned", "act_hi_done", "act_lo_done", "projected", "proj_read"], 3)
    parts_h, parts_m, parts_l, stack_turned, stack_kept = each([
        "parts_h", "parts_m", "parts_l", "stack_turned", "stack_kept"], 2)
    q_rest, rope_step, q_done = map(sem, ["q_rest", "rope_step", "q_done"])
    scored, max_done, shifted, exp_done, probs_turned, prob_hi_done, prob_lo_done = each([
        "scored", "max_done", "shifted", "exp_done", "probs_turned", "prob_hi_done", "prob_lo_done"], 2)
    heads_done, heads_summed, heads_read, mixed_done = each([
        "heads_done", "heads_summed", "heads_read", "mixed_done"], 2)

    b_stats, b_moments, b_var, b_rstd, b_xn, b_kept = map(sem, ["b_stats", "b_moments", "b_var", "b_rstd", "b_xn", "b_kept"])
    b_turned, b_hi, b_lo, b_routed, b_logits = map(sem, ["b_turned", "b_hi", "b_lo", "b_routed", "b_logits"])
    b_gu, b_silu, b_gated, b_hturned, b_hhi, b_hlo, b_down, b_added = map(
        sem, ["b_gu", "b_silu", "b_gated", "b_hturned", "b_hhi", "b_hlo", "b_down", "b_added"])
    ones_made, r_step, r_exp, r_in, r_ranked, r_ready, r_meta = map(
        sem, ["ones_made", "r_step", "r_exp", "r_in", "r_ranked", "r_ready", "r_meta"])
    r_sent, experts_loaded, ids_loaded = map(sem, ["r_sent", "experts_loaded", "ids_loaded"])
    c_loaded = [sem(f"c_loaded{u}") for u in range(FLIGHT)]
    c_stored = [sem(f"c_stored{u}") for u in range(FLIGHT)]
    c_turned, c_kept, c_gu, c_silu, c_gated, c_hturned, c_hkept, c_down, c_scaled = map(sem, [
        "c_turned", "c_kept", "c_gu", "c_silu", "c_gated", "c_hturned", "c_hkept", "c_down", "c_scaled"])
    pairs_loaded = [sem(f"pairs_loaded{c}") for c in range(QUARTERS)]
    pairs_added, result_stored = sem("pairs_added"), sem("result_stored")

    A_OVER = B
    B_OVER = B + 1

    block = nc.Block()
    block.__enter__()

    def wait_alone(engine, semaphore, value):
        engine.wait_ge(semaphore, value)
        engine.sem_inc(unread, 1)

    def b_unit(b, c):
        return 2 * b + c

    def over_elements(engine, step):
        with engine.Fori(0, PAIRS - 1) as it:
            for s in range(2):
                step(2 * it + s, s, 2)
        step(B - 2, 0, 1)
        step(B - 1, 1, 0)

    def phase_b_tensor(pe):
        def turn(b, s):
            pe.wait_ge(b_xn, b + 1)
            pe.wait_ge(b_lo, b + 1)
            for t in range(KT):
                mm = pe.transpose(ps_xT[:, t], xn[s][:, t * P:(t + 1) * P], identity)
            mm.then_inc(b_turned, 1)

        def route(b, s):
            pe.wait_ge(b_lo, b + 2)
            pe.wait_ge(b_logits, b + 1)
            for t in range(KT):
                mm = three_products(pe, ps_router[:, 0:D], actT_hi[s][:, t], actT_lo[s][:, t],
                                    rt_hi[:, t], rt_lo[:, t], t == 0, t == KT - 1)
            mm.then_inc(b_routed, 1)

        def gate_up(b, s, c):
            pe.wait_ge(b_lo, b + 2)
            pe.wait_ge(b_gated, b_unit(b, c) + 1)
            for g in range(2):
                for t in range(KT):
                    mm = three_products(pe, ps_gu[c][:, g], actT_hi[s][:, t], actT_lo[s][:, t],
                                        wgu_hi[:, t, c, g], wgu_lo[:, t, c, g], t == 0, t == KT - 1)
            mm.then_inc(b_gu, 1)

        def turn_hidden(b, c):
            m = b_unit(b, c)
            pe.wait_ge(b_gated, m + 3)
            pe.wait_ge(b_hlo, m + 1)
            for t in range(FT):
                mm = pe.transpose(ps_hT[:, t], silu[c][:, t * P:(t + 1) * P], identity)
            mm.then_inc(b_hturned, 1)

        def down(b, c):
            m = b_unit(b, c)
            pe.wait_ge(b_hlo, m + 2)
            if c == 0:
                pe.wait_ge(b_added, b + 1)
            for t in range(FT):
                mm = three_products(pe, ps_y[:, 0:D], hT_hi[c][:, t], hT_lo[c][:, t],
                                    wd_hi[:, c, t], wd_lo[:, c, t], c == 0 and t == 0, c == 1 and t == FT - 1)
            if c == 1:
                mm.then_inc(b_down, 1)

        def step(b, s, following):
            turn_hidden(b, 0)
            gate_up(b, s, 1)
            if following:
                turn(b + 1, 1 - s)
            down(b, 0)
            turn_hidden(b, 1)
            if following:
                gate_up(b + 1, 1 - s, 0)
                route(b + 1, 1 - s)
            down(b, 1)

        pe.wait_ge(proj_read[2], A_OVER)
        pe.wait_ge(shared_lo, 2 * B)
        turn(0, 0)
        gate_up(0, 0, 0)
        route(0, 0)
        over_elements(pe, step)

    def phase_b_scalar(act):
        S = nc.scalar

        def keep_row(b, s):
            act.wait_ge(b_xn, b + 1)
            S.copy(rows[:, bass.ds(b, 1), 0:D], xn[s][:].unsqueeze(1)).then_inc(b_kept, 1)

        def act_hi(b, s):
            act.wait_ge(b_turned, b + 1)
            S.copy(actT_hi[s][:], ps_xT[:, 0:KT]).then_inc(b_hi, 1)

        def gate(b, c):
            act.wait_ge(b_gu, b_unit(b, c) + 1)
            S.activation(silu[c][:], ps_gu[c][:, 0], ACT.Silu).then_inc(b_silu, 1)

        def hidden_hi(b, c):
            act.wait_ge(b_hturned, b_unit(b, c) + 1)
            S.copy(hT_hi[c][:], ps_hT[:]).then_inc(b_hhi, 1)

        def step(b, s, following):
            gate(b, 0)
            hidden_hi(b, 0)
            if following:
                act_hi(b + 1, 1 - s)
            gate(b, 1)
            hidden_hi(b, 1)
            if following:
                keep_row(b + 1, 1 - s)

        act.wait_ge(proj_read[2], A_OVER)
        keep_row(0, 0)
        act_hi(0, 0)
        over_elements(act, step)

    def phase_b_vector(dve):
        V = nc.vector

        def stats(b, s):
            V.bn_stats(bstats[:, s], tokens[:, bass.ds(b, 1), :]).then_inc(b_stats, 1)
            wait_alone(dve, b_stats, b + 1)
            V.bn_aggr(moments[:, s], bstats[:, s]).then_inc(b_moments, 1)

        def normalise(b, s, turned):
            dve.wait_ge(b_rstd, b + 1)
            if turned:
                dve.wait_ge(b_kept, b - 1)
            V.tensor_scalar(xn[s][:].unsqueeze(1), tokens[:, bass.ds(b, 1), :], moments[:, s, 0:1], rstd[:, s],
                            ALU.subtract, ALU.mult).then_inc(b_xn, 1)

        def act_lo(b, s):
            dve.wait_ge(b_hi, b + 1)
            V.tensor_tensor(actT_lo[s][:], ps_xT[:, 0:KT], actT_hi[s][:].bitcast(F32), ALU.subtract).then_inc(b_lo, 1)

        def keep_logits(b):
            dve.wait_ge(b_routed, b + 1)
            V.tensor_copy(logits[:, bass.ds(b, 1), :], ps_router[:, 0:EXPERTS].unsqueeze(1)).then_inc(b_logits, 1)

        def gated(b, c):
            dve.wait_ge(b_silu, b_unit(b, c) + 1)
            V.tensor_tensor(silu[c][:], silu[c][:], ps_gu[c][:, 1], ALU.mult).then_inc(b_gated, 1)

        def hidden_lo(b, c):
            dve.wait_ge(b_hhi, b_unit(b, c) + 1)
            V.tensor_tensor(hT_lo[c][:], ps_hT[:], hT_hi[c][:].bitcast(F32), ALU.subtract).then_inc(b_hlo, 1)

        def add(b):
            dve.wait_ge(b_down, b + 1)
            V.tensor_tensor(tokens[:, bass.ds(b, 1), :], tokens[:, bass.ds(b, 1), :], ps_y[:, 0:D].unsqueeze(1),
                            ALU.add).then_inc(b_added, 1)

        def step(b, s, following):
            if following == 2:
                stats(b + 2, s)
            hidden_lo(b, 0)
            if following:
                act_lo(b + 1, 1 - s)
            gated(b, 1)
            if following == 2:
                normalise(b + 2, s, True)
            hidden_lo(b, 1)
            if following:
                gated(b + 1, 0)
                keep_logits(b + 1)
            add(b)

        for credit, n in ((b_lo, 1), (b_logits, 1), (b_gated, 2), (b_hlo, 1), (b_added, 1)):
            dve.nop().then_inc(credit, n)
        dve.wait_ge(proj_read[2], A_OVER)
        for b in range(2):
            stats(b, b)
        for b in range(2):
            normalise(b, b, False)
        act_lo(0, 0)
        gated(0, 0)
        keep_logits(0)
        over_elements(dve, step)

    def phase_b_pool(pool):
        G = nc.gpsimd

        def scale(b, s):
            wait_alone(pool, b_moments, b + 1)
            G.tensor_scalar(variance[:, s], moments[:, s, 1:2], EPS, None, ALU.add).then_inc(b_var, 1)
            pool.wait_ge(b_var, b + 1)
            G.tensor_tensor(rstd[:, s], variance[:, s], minus_half[:, 0:1], ALU.pow).then_inc(b_rstd, 1)

        pool.wait_ge(proj_read[2], A_OVER)
        with pool.Fori(0, PAIRS) as it:
            for s in range(2):
                scale(2 * it + s, s)

    def routing_vector(dve):
        V = nc.vector
        done = 0

        def then(ins):
            nonlocal done
            ins.then_inc(r_step, 1)
            done += 1
            dve.wait_ge(r_step, done)

        def over_experts(v):
            return v.unsqueeze(2).to_broadcast([P, B, EXPERTS])

        priority = lane[:, L_PRIORITY:L_FULL].unsqueeze(1).to_broadcast([P, B, EXPERTS])
        dve.wait_ge(b_logits, B + 1)
        dve.wait_ge(lane_loaded, 16)
        V.memset(ones_bf[:], 1.0).then_inc(ones_made, 1)
        then(V.tensor_copy(earlier_bf[:], earlier_fp))
        source = logits
        for k in range(TOPK):
            then(V.tensor_reduce(best[k][:], source[:], AX.X, ALU.max))
            then(V.tensor_tensor(hit[:], source[:], over_experts(best[k][:]), ALU.is_ge))
            then(V.tensor_tensor(hit[:], hit[:], priority, ALU.mult))
            then(V.tensor_reduce(top_priority[:], hit[:], AX.X, ALU.max))
            then(V.tensor_tensor(pick[k][:], hit[:], over_experts(top_priority[:]), ALU.is_ge))
            if k == 0:
                then(V.scalar_tensor_tensor(masked_logits[:], pick[0][:], -3e38, logits[:], ALU.mult, ALU.add))
                source = masked_logits
        then(V.tensor_tensor(ratio[:], best[1][:], best[0][:], ALU.subtract))
        V.tensor_tensor(chosen[:], pick[0][:], pick[1][:], ALU.add).then_inc(r_in, 1)
        dve.wait_ge(r_exp, 1)
        then(V.tensor_scalar(weight[0][:], ratio[:], 1.0, None, ALU.add))
        then(V.reciprocal(weight[0][:], weight[0][:]))
        then(V.tensor_tensor(weight[1][:], ratio[:], weight[0][:], ALU.mult))
        dve.wait_ge(r_ranked, 1)
        ranks = ps_router[:, 0:B * EXPERTS].rearrange("p (b e) -> p e b", e=EXPERTS)
        totals = ps_router[:, B * EXPERTS:2 * B * EXPERTS].rearrange("p (b e) -> p e b", e=EXPERTS)
        then(V.tensor_copy(place[:], totals))
        flat = lambda v: v.rearrange("p e b -> p (e b)")
        then(V.tensor_tensor_scan(flat(upto[:]), lane[:, L_CARRY:L_ONES], flat(place[:]), 0.0, ALU.mult, ALU.add))
        full = lane[:, L_FULL:L_IOTA].unsqueeze(1).to_broadcast([P, EXPERTS, B])
        then(V.tensor_tensor(begun[:], upto[:, :, B - 1:B].to_broadcast([P, EXPERTS, B]), full, ALU.is_gt))
        then(V.tensor_reduce(n_tiles[:], begun[:], AX.X, ALU.add))
        then(V.tensor_scalar(n_tiles[:], n_tiles[:], 1.0, None, ALU.max))
        then(V.tensor_tensor_scan(end_tile[:], lane[:, L_ONES:], n_tiles[:], 0.0, ALU.mult, ALU.add))
        then(V.tensor_tensor(start_row[:], end_tile[:], n_tiles[:], ALU.subtract))
        then(V.tensor_scalar(start_row[:], start_row[:], float(P), None, ALU.mult))
        then(V.tensor_tensor(place[:], upto[:], place[:], ALU.subtract))
        then(V.tensor_tensor(place[:], place[:], ranks, ALU.add))
        then(V.tensor_tensor(place[:], place[:], start_row[:].unsqueeze(2).to_broadcast([P, EXPERTS, B]), ALU.add))
        for k in range(TOPK):
            then(V.tensor_tensor(hit[:], pick[k][:], place[:].rearrange("p e b -> p b e"), ALU.mult))
            then(V.tensor_reduce(where_fp[k][:], hit[:], AX.X, ALU.add))
            then(V.tensor_copy(where[k][:], where_fp[k][:]))
        ends = end_tile[:].unsqueeze(1).to_broadcast([P, TILES, EXPERTS])
        tiles = lane[:, L_IOTA:L_CARRY].unsqueeze(2).to_broadcast([P, TILES, EXPERTS])
        then(V.tensor_tensor(passed[:], ends, tiles, ALU.is_le))
        then(V.tensor_reduce(tile_expert_fp[:], passed[:], AX.X, ALU.add))
        then(V.tensor_scalar(tile_expert_fp[:], tile_expert_fp[:], float(EXPERTS - 1), None, ALU.min))
        V.tensor_copy(tile_expert[:], tile_expert_fp[:]).then_inc(r_ready, 1)
        dve.wait_ge(ids_loaded, 16)
        dve.wait_ge(b_kept, B)
        for k in range(TOPK):
            if k > 0:
                dve.wait_ge(r_sent, 16 * B)
            V.tensor_copy(rows[:, :, WEIGHT], weight[k][:])
            V.tensor_copy(rows[:, :, ROW_ID].bitcast(I32), row_id_sb[:, k]).then_inc(r_meta, 1)

    def routing_tensor(pe):
        pe.wait_ge(r_in, 1)
        m = chosen[:].rearrange("p b e -> p (b e)")
        pe.matmul(ps_router[:, 0:B * EXPERTS], earlier_bf[:], m, start=True, stop=True)
        pe.matmul(ps_router[:, B * EXPERTS:2 * B * EXPERTS], ones_bf[:], m, start=True, stop=True).then_inc(r_ranked, 1)

    def routing_scalar(act):
        act.wait_ge(r_step, 13)
        nc.scalar.activation(ratio[:], ratio[:], ACT.Exp).then_inc(r_exp, 1)

    def routing_pool(pool):
        pool.wait_ge(emptied, 16)
        for k in range(TOPK):
            pool.wait_ge(r_meta, k + 1)
            for b in range(B):
                pool.indirect_dma_start(dispatched, bass.IndirectOffsetOnAxis(ap=where[k][:, b:b + 1], axis=0),
                                        rows[:, b], None, bounds_check=TILES * P - 1, oob_is_err=False).then_inc(r_sent, 16)

    def over_tiles(engine, step, registers=None):
        def experts_from(i):
            return registers(i) if registers else [None] * (FLIGHT + 1)

        with engine.Fori(0, TILES // FLIGHT - 1) as it:
            e = experts_from(FLIGHT * it)
            for u in range(FLIGHT):
                step(FLIGHT * it + u, u, it, e[u:], 2)
        e = experts_from(TILES - FLIGHT)
        for u in range(FLIGHT):
            step(TILES - FLIGHT + u, u, TILES // FLIGHT - 1, e[u:], min(2, FLIGHT - 1 - u))

    def phase_c_sync(sp):
        sp.wait_ge(r_sent, 16 * B * TOPK)
        for u in range(FLIGHT):
            sp.dma_start(tile_in[u][:], dispatched[u * P:(u + 1) * P, :]).then_inc(c_loaded[u], 16)
        with sp.Fori(1, TILES // FLIGHT) as it:
            for u in range(FLIGHT):
                sp.wait_ge(c_stored[u], 16 * it)
                sp.dma_start(tile_in[u][:], dispatched[bass.ds((FLIGHT * it + u) * P, P), :]).then_inc(c_loaded[u], 16)

    def phase_c_tensor(pe):
        def turn(i, u, loads):
            pe.wait_ge(c_loaded[u], 16 * loads)
            pe.wait_ge(c_kept, i + 1)
            for t in range(KT):
                mm = pe.transpose(ps_xT[:, t], tile_in[u][:, t * P:(t + 1) * P], identity)
            mm.then_inc(c_turned, 1)

        def gate_up(i, u, e):
            v = u % 2
            pe.wait_ge(c_kept, i + 2)
            pe.wait_ge(c_gated, i + 1)
            for g in range(2):
                for t in range(KT):
                    mm = pe.matmul(ps_gu[v][:, g], xT_fp[v][:, t], w1_sb[:, bass.ds(e, 1), t, g],
                                   start=t == 0, stop=t == KT - 1)
            mm.then_inc(c_gu, 1)

        def turn_hidden(i, u):
            v = u % 2
            pe.wait_ge(c_gated, i + 3)
            pe.wait_ge(c_hkept, i + 1)
            for t in range(FT):
                mm = pe.transpose(ps_hT[:, t], silu[v][:, t * P:(t + 1) * P], identity)
            mm.then_inc(c_hturned, 1)

        def down(i, u, e):
            v = u % 2
            pe.wait_ge(c_hkept, i + 2)
            pe.wait_ge(c_scaled, i + 1)
            for t in range(FT):
                mm = pe.matmul(ps_y[:, 0:D], hT_fp[v][:, t], w2_sb[:, bass.ds(e, 1), t], start=t == 0, stop=t == FT - 1)
            mm.then_inc(c_down, 1)

        def registers(i):
            n = FLIGHT + 1 if not isinstance(i, int) else FLIGHT
            return [pe.value_load(tile_expert[0:1, bass.ds(i + j, 1)], min_val=0, max_val=EXPERTS - 1) for j in range(n)]

        def step(i, u, r, e, following):
            turn_hidden(i, u)
            if following:
                gate_up(i + 1, u + 1, e[1])
            if following == 2:
                turn(i + 2, (u + 2) % FLIGHT, r + (u + 2) // FLIGHT + 1)
            down(i, u, e[0])

        pe.wait_ge(r_ready, 1)
        pe.wait_ge(experts_loaded, 16 * 2 * EXPERTS)
        first = registers(0)[0]
        turn(0, 0, 1)
        gate_up(0, 0, first)
        turn(1, 1, 1)
        over_tiles(pe, step, registers)

    def phase_c_scalar(act):
        S = nc.scalar

        def step(i, u, r, e, following):
            act.wait_ge(c_gu, i + 1)
            S.activation(silu[u % 2][:], ps_gu[u % 2][:, 0], ACT.Silu).then_inc(c_silu, 1)

        over_tiles(act, step)

    def phase_c_vector(dve):
        V = nc.vector
        for credit, n in ((c_kept, 1), (c_hkept, 1), (c_gated, 2), (c_scaled, 1)):
            dve.nop().then_inc(credit, n)

        def keep_x(i, u):
            dve.wait_ge(c_turned, i + 1)
            V.tensor_copy(xT_fp[u % 2][:], ps_xT[:, 0:KT]).then_inc(c_kept, 1)

        def gated(i, u):
            dve.wait_ge(c_silu, i + 1)
            V.tensor_tensor(silu[u % 2][:], silu[u % 2][:], ps_gu[u % 2][:, 1], ALU.mult).then_inc(c_gated, 1)

        def keep_h(i, u):
            dve.wait_ge(c_hturned, i + 1)
            V.tensor_copy(hT_fp[u % 2][:], ps_hT[:]).then_inc(c_hkept, 1)

        def scale(i, u):
            dve.wait_ge(c_down, i + 1)
            V.tensor_scalar(tile_out[u][:], ps_y[:, 0:D], tile_in[u][:, WEIGHT:WEIGHT + 1], None, ALU.mult).then_inc(c_scaled, 1)

        def step(i, u, r, e, following):
            keep_h(i, u)
            if following == 2:
                keep_x(i + 2, u + 2)
            if following:
                gated(i + 1, u + 1)
            scale(i, u)

        keep_x(0, 0)
        gated(0, 0)
        keep_x(1, 1)
        over_tiles(dve, step)
        for c in range(QUARTERS):
            dve.wait_ge(pairs_loaded[c], 16)
            for k in range(TOPK):
                mine = tokens[:, c * QB:(c + 1) * QB]
                V.tensor_tensor(mine, mine, products[:, c, :, k], ALU.add).then_inc(pairs_added, 1)
                dve.wait_ge(pairs_added, TOPK * c + k + 1)

    def phase_c_pool(pool):
        last_row = pool.to_reg(CHOICES - 1)
        with pool.Fori(0, TILES // FLIGHT) as it:
            for u in range(FLIGHT):
                wait_alone(pool, c_scaled, FLIGHT * it + u + 2)
                pool.indirect_dma_start(combined, bass.IndirectOffsetOnAxis(ap=tile_in[u][:, ROW_ID:ROW].bitcast(I32), axis=0),
                                        tile_out[u][:], None, bounds_check=last_row, oob_is_err=False).then_inc(c_stored[u], 16)

    def exists(element):
        return 0 <= element < B

    def over_iterations(engine, iteration):
        for nb in range(-1, 3):
            iteration(nb, nb)
        with engine.Fori(0, (B - 4) // 2) as it:
            for j in range(2):
                iteration(2 * it + 3 + j, 3 + j)
        for nb in range(B - 1, B + 3):
            iteration(nb, nb)

    def unit_at(b, nb, i):
        if i < 0:
            b, nb, i = b - 1, nb - 1, i + 4
        a = i // 2
        return (a, b - 2 * a, nb - 2 * a, i % 2) if exists(nb - 2 * a) else None

    def unit_before(b, nb, i):
        for back in range(1, 4):
            if unit_at(b, nb, i - back):
                return unit_at(b, nb, i - back)
        return None

    def wait_unit(engine, semaphores, unit):
        if unit:
            a, e, _, u = unit
            engine.wait_ge(semaphores[a], 2 * e + u + 1)

    STACKS = [(0, 0, 2), (1, -2, 0), (1, -2, 1), (1, -2, 2), (0, 1, 0), (0, 1, 1)]
    PROJECTIONS = [(1, -1), (0, 1), (2, -3)]

    def user_before(order, now, b, nb):
        i = order.index(now)
        for back in range(1, 2 * len(order)):
            who = order[(i - back) % len(order)]
            turns = -((i - back) // len(order))
            if exists(nb - turns + who[1]):
                return who, b - turns + who[1]
        return None, None

    flat_gu = [w[:].rearrange("p k u g n -> p (k u g n)") for w in (wgu_hi, wgu_lo)]
    flat_d = [w[:].rearrange("p u k n -> p (u k n)") for w in (wd_hi, wd_lo)]
    n_gu, n_d = KT * 2 * SHARED // B, FT * 2 * D // B
    SHARES = [(flat_gu[0], raw_gu, n_gu), (flat_d[0], raw_d, n_d)]
    LOW_SHARES = [(flat_gu[1], flat_gu[0], raw_gu, n_gu), (flat_d[1], flat_d[0], raw_d, n_d)]

    @block.sync
    def _(sp):
        sp.dma_start(squares[:], a["squares"]).then_inc(squares_loaded, 16)
        sp.dma_start(tokens[:, 0:2], x[0:2].rearrange("b t d -> t b d")).then_inc(x_loaded, 16)
        for w, c0, n in (("wq", 0, D), ("wk", D, KVD), ("wv", D + KVD, KVD)):
            sp.dma_start(raw_qkv[:, :, c0:c0 + n], a[w].rearrange("(k p) n -> p k n", p=P)).then_inc(qkv_loaded, 16)
        sp.dma_start(ctx_sb[:], ctx_512.rearrange("b t d -> t b d")).then_inc(ctx_loaded, 16)
        sp.dma_start(rope[:], a["rope"]).then_inc(consts_loaded, 16)
        sp.dma_start(norm_w[:, 0:D], a["q_norm"].partition_broadcast(P)).then_inc(consts_loaded, 16)
        sp.dma_start(norm_w[:, D:], a["k_norm"].partition_broadcast(P)).then_inc(consts_loaded, 16)
        for i, w in enumerate(("wo", "w_out_t")):
            sp.dma_start(raw_proj[:, i], a[w].rearrange("(k p) n -> p k n", p=P)).then_inc(attn_loaded, 16)
        sp.dma_start(raw_bias[:], a["bo"].partition_broadcast(P)).then_inc(attn_loaded, 16)
        sp.dma_start(raw_router[:], a["router"].rearrange("(k p) n -> p k n", p=P)).then_inc(attn_loaded, 16)
        sp.dma_start(tokens[:, 2:], x[2:].rearrange("b t d -> t b d")).then_inc(rest_loaded, 16)
        sp.dma_start(lane[:], a["lanes"]).then_inc(lane_loaded, 16)
        sp.wait_ge(empty_made, 2)
        sp.dma_start(dispatched.rearrange("(t p) n -> p t n", p=P),
                     empty_rows[:].unsqueeze(1).to_broadcast([P, TILES, ROW])).then_inc(emptied, 16)
        sp.wait_ge(kv_l, 1)
        gu = raw_gu.rearrange("p (k u g n) -> p k u g n", k=KT, u=2, g=2)
        for k in range(KT):
            for g, w in enumerate(("w_gate", "w_up")):
                sp.dma_start(gu[:, k, :, g], a[w][k * P:(k + 1) * P].rearrange("p (u n) -> p u n", u=2)).then_inc(shared_loaded, 16)
        sp.dma_start(raw_d.rearrange("p (k n) -> p k n", n=D), a["w_down"].rearrange("(k p) n -> p k n", p=P)).then_inc(shared_loaded, 16)
        sp.wait_ge(proj_read[2], A_OVER)
        sp.wait_ge(shared_lo, 2 * B)
        for e in range(EXPERTS):
            sp.dma_start(w1_sb[:, e], a["w1"][e].rearrange("(k p) (g n) -> p k g n", p=P, g=2)).then_inc(experts_loaded, 16)
            sp.dma_start(w2_sb[:, e], a["w2"][e].rearrange("(k p) n -> p k n", p=P)).then_inc(experts_loaded, 16)
        sp.wait_ge(b_added, B_OVER)
        sp.dma_start(row_id_sb[:], a["row_ids"]).then_inc(ids_loaded, 16)
        phase_c_sync(sp)
        for u in range(FLIGHT):
            sp.wait_ge(c_stored[u], 16 * (TILES // FLIGHT))
        for c in range(QUARTERS):
            sp.dma_start(products[:, c].rearrange("p b k n -> p b (k n)"), combined.rearrange("(c b p k) n -> c p b (k n)", c=QUARTERS, p=P, k=TOPK)[c]).then_inc(pairs_loaded[c], 16)
        for c in range(QUARTERS):
            sp.wait_ge(pairs_added, TOPK * (c + 1))
            sp.dma_start(out[c * QB:(c + 1) * QB].rearrange("b t d -> t b d"), tokens[:, c * QB:(c + 1) * QB]).then_inc(result_stored, 16)
        sp.wait_ge(result_stored, 16 * QUARTERS)

    def three_products(pe, dst, xh, xl, wh, wl, start, stop):
        pe.matmul(dst, xh, wh, start=start, stop=False)
        pe.matmul(dst, xh, wl, start=False, stop=False)
        return pe.matmul(dst, xl, wh, start=False, stop=stop)

    @block.tensor
    def _(pe):
        def turn(k, src):
            for t in range(KT):
                mm = pe.transpose(ps_actT[:, t], src[:, t * P:(t + 1) * P], identity)
            mm.then_inc(act_turned[k], 1)

        def turn_heads(k, e):
            pe.wait_ge(mixed_done[k - 1], e + 1)
            turn(k, mixed[k - 1][:].rearrange("p h d -> p (h d)"))

        def turn_tokens(e):
            pe.wait_ge(xn_done[0], e + 1)
            turn(0, xn[0])

        def project(k, b, nb):
            now = [p for p in PROJECTIONS if p[0] == k][0]
            before, e_before = user_before(PROJECTIONS, now, b, nb)
            pe.wait_ge(act_lo_done[k], b + now[1] + 1)
            if before:
                pe.wait_ge(proj_read[before[0]], e_before + 1)
            s = k % 2
            if k == 0:
                for t in range(KT):
                    mm = three_products(pe, ps_proj[:, 0:QKV], actT_hi[s][:, t], actT_lo[s][:, t],
                                        wqkv_hi[:, t], wqkv_lo[:, t], t == 0, t == KT - 1)
            else:
                if k == 1:
                    pe.matmul(ps_proj[:, 0:D], first_row[:], bias_hi[:], start=True, stop=False)
                    pe.matmul(ps_proj[:, 0:D], first_row[:], bias_lo[:], start=False, stop=False)
                for t in range(KT):
                    mm = three_products(pe, ps_proj[:, 0:D], actT_hi[s][:, t], actT_lo[s][:, t],
                                        wproj_hi[:, k - 1, t], wproj_lo[:, k - 1, t],
                                        k == 2 and t == 0, t == KT - 1)
            mm.then_inc(projected[k], 1)

        def turn_stack(a, offset, g, b, nb):
            if not exists(nb + offset):
                return
            e = b + offset
            before, e_before = user_before(STACKS, (a, offset, g), b, nb)
            if a == 0 or g > 0:
                pe.wait_ge(parts_l[a], e + 1)
            if before:
                pe.wait_ge(stack_kept[before[0]], 3 * e_before + before[2] + 1)
            first, n = ((HEADS, GROUPS), (0, HALF), (HALF, HALF))[g]
            for h in range(n):
                if a == 0:
                    src = stack[(nb + offset) % 2][:, first + h, 2:BLOCK]
                elif g == 0:
                    src = cross_kv[:, bass.ds(e, 1), h, 2:BLOCK]
                else:
                    src = cross_stack[:, first + h, 2:BLOCK]
                mm = pe.transpose(ps_stack[0:STACK, h], src, ident_bf[:])
            mm.then_inc(stack_turned[a], 1)

        def score(b, nb, i):
            unit = unit_at(b, nb, i)
            if not unit:
                return
            a, e, _, u = unit
            pe.wait_ge(stack_kept[a], 3 * e + u + 2)
            wait_unit(pe, shifted, unit_before(b, nb, i))
            for j in range(2):
                pe.matmul(ps_scores[:, 4 * j:4 * j + 4], ident_bf[:], mask_bf[:], start=True, stop=False,
                          skip_group_check=True)
                for n in range(4):
                    h = HALF * u + 4 * j + n
                    mm = pe.matmul(ps_scores[:, 4 * j + n], qT[a][0:STACK, h], kT[a][0:STACK, h // 4],
                                   start=False, stop=n == 3, skip_group_check=True)
            mm.then_inc(scored[a], 1)

        def turn_probs(b, nb, i):
            unit = unit_at(b, nb, i)
            if not unit:
                return
            a, _, _, u = unit
            wait_unit(pe, exp_done, unit)
            wait_unit(pe, prob_lo_done, unit_before(b, nb, i))
            for n in range(HALF):
                mm = pe.transpose(ps_probs[:, n], prob[u][:, n], identity)
            mm.then_inc(probs_turned[a], 1)

        def mix(b, nb, i):
            unit = unit_at(b, nb, i)
            if not unit:
                return
            a, e, ne, u = unit
            wait_unit(pe, prob_lo_done, unit)
            wait_unit(pe, heads_read, unit_before(b, nb, i))
            for n in range(HALF):
                group = GROUPS + (HALF * u + n) // 4
                v = stack[ne % 2][:, HEADS + group, 1:1 + VCOLS] if a == 0 else cross_kv[:, bass.ds(e, 1), group, 1:1 + VCOLS]
                dst = ps_heads[:, n * VCOLS:(n + 1) * VCOLS]
                pe.matmul(dst, prob_hi[u][:, n], v, start=True, stop=False)
                mm = pe.matmul(dst, prob_lo[u][:, n], v, start=False, stop=True)
            mm.then_inc(heads_done[a], 1)

        def iteration(b, nb):
            if nb == 1:
                pe.wait_ge(lo_made, 4)
            if nb == 2:
                pe.wait_ge(kv_l, 1)
            score(b, nb, 0)
            turn_stack(0, 0, 2, b, nb)
            turn_probs(b, nb, -1)
            if exists(nb - 1):
                turn_heads(1, b - 1)
            mix(b, nb, -2)
            turn_stack(1, -2, 0, b, nb)
            score(b, nb, 1)
            turn_probs(b, nb, 0)
            if exists(nb - 1):
                project(1, b, nb)
            if exists(nb + 1):
                turn_tokens(b + 1)
            mix(b, nb, -1)
            turn_stack(1, -2, 1, b, nb)
            if exists(nb + 1):
                project(0, b, nb)
            score(b, nb, 2)
            turn_probs(b, nb, 1)
            turn_stack(1, -2, 2, b, nb)
            if exists(nb - 3):
                turn_heads(2, b - 3)
            mix(b, nb, 0)
            score(b, nb, 3)
            turn_probs(b, nb, 2)
            if exists(nb - 3):
                project(2, b, nb)
            turn_stack(0, 1, 0, b, nb)
            mix(b, nb, 1)
            turn_stack(0, 1, 1, b, nb)

        pe.wait_ge(squares_loaded, 16)
        pe.wait_ge(lo_made, 1)
        pe.wait_ge(filled, 6)
        pe.wait_ge(filled_act, 3)
        over_iterations(pe, iteration)
        phase_b_tensor(pe)
        routing_tensor(pe)
        phase_c_tensor(pe)

    @block.vector
    def _(dve):
        V = nc.vector

        V.memset(minus_half[:], -0.5).then_inc(filled, 1)
        V.memset(empty_rows[:, 0:ROW_ID], 0.0).then_inc(empty_made, 1)
        V.memset(empty_rows[:, ROW_ID:ROW].bitcast(I32), NO_ROW).then_inc(empty_made, 1)
        V.memset(cross_kv[:, :, :, 0:2], 1.0).then_inc(filled, 1)
        for s in range(2):
            V.memset(stack[s][:, :, 0:2], 1.0).then_inc(filled, 1)
        V.memset(rt_hi[:].bitcast(F32), 0.0).then_inc(filled, 1)
        V.memset(rt_lo[:].bitcast(F32), 0.0).then_inc(filled, 1)
        dve.wait_ge(filled, 6)
        dve.wait_ge(hi_made, 1)
        V.tensor_tensor(wqkv_lo[:], raw_qkv[:], wqkv_hi[:].bitcast(F32), ALU.subtract).then_inc(lo_made, 1)

        def ctx_squares():
            dve.wait_ge(ctx_loaded, 16)
            V.tensor_tensor(kv_a[:, :, 0:KVD], ctx_sb[:], ctx_sb[:], ALU.mult).then_inc(kv_step, 1)
            dve.wait_ge(kv_step, 1)
            V.tensor_reduce(k_rstd[:], kv_a[:, :, 0:KVD], AX.X, ALU.add).then_inc(kv_var, 1)

        def rotary_weights():
            dve.wait_ge(consts_loaded, 16 * 3)
            w_view = norm_w[:].rearrange("p (h n) -> p h n", n=HD)
            w_swap = norm_w[:].rearrange("p (h t e) -> p h t e", t=2, e=HD // 2)[:, :, ::-1, :]
            n_heads = HEADS + GROUPS
            V.tensor_tensor(cos_w[:].rearrange("p (h n) -> p h n", n=HD), w_view,
                            rope[:, 0:1, :].to_broadcast([P, n_heads, HD]), ALU.mult).then_inc(kv_step, 1)
            V.tensor_tensor(sin_w[:].rearrange("p (h t e) -> p h t e", t=2, e=HD // 2), w_swap,
                            rope[:, 1:2, :].rearrange("p o (t e) -> p o t e", t=2).to_broadcast([P, n_heads, 2, HD // 2]),
                            ALU.mult).then_inc(kv_step, 1)

        def low_weights():
            dve.wait_ge(hi_made, 4)
            V.tensor_tensor(wproj_lo[:], raw_proj[:], wproj_hi[:].bitcast(F32), ALU.subtract).then_inc(lo_made, 1)
            V.tensor_tensor(bias_lo[:], raw_bias[:], bias_hi[:].bitcast(F32), ALU.subtract).then_inc(lo_made, 1)
            V.tensor_tensor(rt_lo[:, :, 0:EXPERTS], raw_router[:], rt_hi[:, :, 0:EXPERTS].bitcast(F32), ALU.subtract).then_inc(lo_made, 1)

        def ctx_cosines():
            dve.wait_ge(kv_pow, 2)
            dve.wait_ge(kv_step, 3)
            V.tensor_tensor(kv_b[:, :, 0:KVD], ctx_sb[:], k_rstd[:].unsqueeze(2).to_broadcast([P, B, KVD]), ALU.mult).then_inc(kv_step, 1)
            dve.wait_ge(kv_step, 4)
            ck = cos_w[:, D:].unsqueeze(1).to_broadcast([P, B, KVD])
            V.tensor_tensor(kv_a[:, :, 0:KVD], kv_b[:, :, 0:KVD], ck, ALU.mult).then_inc(kv_step, 1)

        def ctx_sines():
            swapped = kv_b[:, :, 0:KVD].rearrange("p b (g t e) -> p b g t e", g=GROUPS, t=2)[:, :, :, ::-1, :]
            for g in range(GROUPS):
                sk = sin_w[:, D + g * HD:D + (g + 1) * HD].rearrange("p (t e) -> p t e", t=2)
                V.tensor_tensor(kv_a[:, :, KVD + g * HD:KVD + (g + 1) * HD].rearrange("p b (t e) -> p b t e", t=2),
                                swapped[:, :, g], sk.unsqueeze(1).to_broadcast([P, B, 2, HD // 2]),
                                ALU.mult).then_inc(kv_step, 1)
            dve.wait_ge(kv_step, 9)
            V.tensor_tensor(kv_fp[:, :, 0:KVD], kv_a[:, :, 0:KVD], kv_a[:, :, KVD:], ALU.add).then_inc(kv_src, 1)

        blocks = cross_kv[:].rearrange("p b g n -> p (b g) n")
        rest = kv_b.rearrange("p b (g n) -> p (b g) n", n=HD)

        def ctx_rest():
            dve.wait_ge(kv_h, 1)
            V.tensor_tensor(rest, kv_fp.rearrange("p b (g n) -> p (b g) n", n=HD), blocks[:, :, 2:2 + HD], ALU.subtract).then_inc(kv_r, 1)

        def ctx_last():
            dve.wait_ge(kv_m, 1)
            V.tensor_tensor(blocks[:, :, 2 + 2 * HD:2 + 3 * HD], rest, blocks[:, :, 2 + HD:2 + 2 * HD], ALU.subtract).then_inc(kv_l, 1)

        def setup_beside(nb, slot):
            if (nb, slot) == (-1, 1):
                ctx_squares()
            elif (nb, slot) == (-1, 3):
                rotary_weights()
                low_weights()
            elif (nb, slot) == (0, 0):
                dve.wait_ge(rest_loaded, 16)
                ctx_cosines()
            elif (nb, slot) == (0, 1):
                ctx_sines()
            elif (nb, slot) == (0, 3):
                ctx_rest()
            elif (nb, slot) == (1, 2):
                ctx_last()

        def norm_stats(a, e):
            V.bn_stats(bstats[:, a], tokens[:, bass.ds(e, 1), :]).then_inc(stats_done[a], 1)

        def norm_moments(a, e):
            wait_alone(dve, stats_done[a], e + 1)
            V.bn_aggr(moments[:, a], bstats[:, a]).then_inc(moments_done[a], 1)

        def normalise(a, e):
            dve.wait_ge(rstd_done[a], e + 1)
            V.tensor_scalar(xn[a][:].unsqueeze(1), tokens[:, bass.ds(e, 1), :], moments[:, a, 0:1], rstd[:, a],
                            ALU.subtract, ALU.mult).then_inc(xn_done[a], 1)

        def act_lo(k, e):
            dve.wait_ge(act_hi_done[k], e + 1)
            V.tensor_tensor(actT_lo[k % 2][:], ps_actT[:, 0:KT], actT_hi[k % 2][:].bitcast(F32), ALU.subtract).then_inc(act_lo_done[k], 1)

        def add_projected(k, e):
            dve.wait_ge(projected[k], e + 1)
            mine = tokens[:, bass.ds(e, 1), :]
            V.tensor_tensor(mine, mine, ps_proj[:, 0:D].unsqueeze(1), ALU.add).then_inc(proj_read[k], 1)

        def take_remainder(e, s):
            dve.wait_ge(parts_h[0], e + 1)
            V.tensor_tensor(remainder[0][:].rearrange("p (h n) -> p h n", n=HD),
                            ps_proj[:, 0:QKV].rearrange("p (h n) -> p h n", n=HD),
                            stack[s][:, :, 2:2 + HD], ALU.subtract).then_inc(proj_read[0], 1)

        def shift(b, nb, i):
            unit = unit_at(b, nb, i)
            if not unit:
                return
            a, _, _, u = unit
            wait_unit(dve, scored, unit)
            V.tensor_reduce(row_max[u][:], ps_scores[:], AX.X, ALU.max).then_inc(max_done[a], 1)
            wait_unit(dve, max_done, unit)
            V.tensor_tensor(prob[u][:], ps_scores[:], row_max[u][:].unsqueeze(2).to_broadcast([P, HALF, P]),
                            ALU.subtract).then_inc(shifted[a], 1)

        def probs_lo(b, nb, i):
            unit = unit_at(b, nb, i)
            if not unit:
                return
            a, _, _, u = unit
            wait_unit(dve, prob_hi_done, unit)
            V.tensor_tensor(prob_lo[u][:], ps_probs[:], prob_hi[u][:], ALU.subtract).then_inc(prob_lo_done[a], 1)

        def sum_parts(b, nb, i):
            unit = unit_at(b, nb, i)
            if not unit:
                return
            a, e, _, u = unit
            wait_unit(dve, heads_done, unit)
            o = ps_heads[:, 0:HALF * VCOLS].rearrange("p (h c) -> p h c", c=VCOLS)
            V.tensor_reduce(heads[a][:, HALF * u:HALF * (u + 1)],
                            o[:, :, 1:].rearrange("p h (c d) -> p h d c", c=3), AX.X, ALU.add).then_inc(heads_summed[a], 1)
            V.reciprocal(denom[a][:, HALF * u:HALF * (u + 1)], o[:, :, 0]).then_inc(heads_read[a], 1)

        def finish_heads(a, e):
            dve.wait_ge(heads_summed[a], 2 * e + 2)
            dve.wait_ge(heads_read[a], 2 * e + 2)
            V.tensor_tensor(mixed[a][:], heads[a][:], denom[a][:].unsqueeze(2).to_broadcast([P, HEADS, HD]),
                            ALU.mult).then_inc(mixed_done[a], 1)

        def iteration(b, nb):
            if exists(nb + 1):
                norm_stats(0, b + 1)
            shift(b, nb, 0)
            if exists(nb + 1):
                norm_moments(0, b + 1)
            probs_lo(b, nb, -1)
            if exists(nb - 1):
                act_lo(1, b - 1)
            sum_parts(b, nb, -2)
            if exists(nb + 1):
                normalise(0, b + 1)
            setup_beside(nb, 0)
            shift(b, nb, 1)
            if exists(nb - 1):
                add_projected(1, b - 1)
            if exists(nb + 1):
                act_lo(0, b + 1)
            if exists(nb - 1):
                wait_alone(dve, proj_read[1], b)
                norm_stats(1, b - 1)
            probs_lo(b, nb, 0)
            if exists(nb - 1):
                norm_moments(1, b - 1)
            sum_parts(b, nb, -1)
            setup_beside(nb, 1)
            shift(b, nb, 2)
            if exists(nb - 3):
                finish_heads(1, b - 3)
            if exists(nb + 1):
                take_remainder(b + 1, (nb + 1) % 2)
            probs_lo(b, nb, 1)
            if exists(nb - 1):
                normalise(1, b - 1)
            sum_parts(b, nb, 0)
            if exists(nb - 3):
                act_lo(2, b - 3)
            setup_beside(nb, 2)
            shift(b, nb, 3)
            probs_lo(b, nb, 2)
            sum_parts(b, nb, 1)
            if exists(nb - 3):
                add_projected(2, b - 3)
            if exists(nb):
                finish_heads(0, b)
            setup_beside(nb, 3)

        dve.wait_ge(x_loaded, 16)
        over_iterations(dve, iteration)
        phase_b_vector(dve)
        routing_vector(dve)
        phase_c_vector(dve)

    @block.scalar
    def _(act):
        S = nc.scalar
        act.wait_ge(squares_loaded, 16)
        S.copy(ident_bf[:], identity).then_inc(filled_act, 1)
        S.copy(mask_bf[:], squares[:, 1:2].to_broadcast([P, 4, P])).then_inc(filled_act, 1)
        S.copy(first_row[:], squares[:, 3]).then_inc(filled_act, 1)
        act.wait_ge(qkv_loaded, 16 * 3)
        S.copy(wqkv_hi[:], raw_qkv[:]).then_inc(hi_made, 1)

        def high_weights():
            act.wait_ge(attn_loaded, 16 * 4)
            S.copy(wproj_hi[:], raw_proj[:]).then_inc(hi_made, 1)
            S.copy(bias_hi[:], raw_bias[:]).then_inc(hi_made, 1)
            act.wait_ge(filled, 6)
            S.copy(rt_hi[:, :, 0:EXPERTS], raw_router[:]).then_inc(hi_made, 1)

        fp = kv_fp.rearrange("p b (g n) -> p (b g) n", n=HD)
        rest = kv_b.rearrange("p b (g n) -> p (b g) n", n=HD)
        slots = cross_kv[:].rearrange("p b g n -> p (b g) n")[:, :, 2:].rearrange("p r (c n) -> p r c n", n=HD)
        two = lambda v: v.unsqueeze(2).to_broadcast([P, B * KV, 2, HD])

        def ctx_values():
            act.wait_ge(ctx_loaded, 16)
            S.copy(kv_fp[:, :, KVD:], ctx_sb[:]).then_inc(kv_src, 1)

        def ctx_high():
            act.wait_ge(kv_src, 2)
            S.copy(slots[:, :, 0::3], two(fp))
            S.copy(slots[:, :, 5], fp).then_inc(kv_h, 1)

        def ctx_middle():
            act.wait_ge(kv_r, 1)
            S.copy(slots[:, :, 1::3], two(rest)).then_inc(kv_m, 1)

        def setup_beside(nb, slot):
            if (nb, slot) == (-1, 2):
                high_weights()
                ctx_values()
            elif (nb, slot) == (0, 2):
                ctx_high()
            elif (nb, slot) == (1, 1):
                ctx_middle()

        def act_hi(k, e):
            act.wait_ge(act_turned[k], e + 1)
            S.copy(actT_hi[k % 2][:], ps_actT[:, 0:KT]).then_inc(act_hi_done[k], 1)

        def in_slots(blocks):
            return blocks[:, :, 2:].rearrange("p h (c n) -> p h c n", n=HD)

        def high_parts_self(e, s):
            act.wait_ge(projected[0], e + 1)
            q = ps_proj[:, 0:D].rearrange("p (h n) -> p h n", n=HD)
            kv = ps_proj[:, D:QKV].rearrange("p (h n) -> p h n", n=HD)
            in_kv, in_q = in_slots(stack[s][:, HEADS:]), in_slots(stack[s][:, 0:HEADS])
            S.copy(in_kv[:, :, 0::3], kv.unsqueeze(2).to_broadcast([P, KV, 2, HD]))
            S.copy(in_kv[:, :, 5], kv)
            S.copy(in_q[:, :, 0:3], q.unsqueeze(2).to_broadcast([P, HEADS, 3, HD])).then_inc(parts_h[0], 1)

        def middle_parts_self(e, s):
            act.wait_ge(proj_read[0], e + 1)
            r = remainder[0][:].rearrange("p (h n) -> p h n", n=HD)
            in_kv, in_q = in_slots(stack[s][:, HEADS:]), in_slots(stack[s][:, 0:HEADS])
            S.copy(in_kv[:, :, 1::3], r[:, HEADS:].unsqueeze(2).to_broadcast([P, KV, 2, HD]))
            S.copy(in_q[:, :, 3:5], r[:, 0:HEADS].unsqueeze(2).to_broadcast([P, HEADS, 2, HD])).then_inc(parts_m[0], 1)

        def high_parts_cross(e):
            act.wait_ge(q_done, e + 1)
            q = q_fp[:].rearrange("p (h n) -> p h n", n=HD)
            S.copy(in_slots(cross_stack)[:, :, 0:3], q.unsqueeze(2).to_broadcast([P, HEADS, 3, HD])).then_inc(parts_h[1], 1)

        def middle_parts_cross(e):
            act.wait_ge(q_rest, e + 1)
            r = remainder[1][:, 0:D].rearrange("p (h n) -> p h n", n=HD)
            S.copy(in_slots(cross_stack)[:, :, 3:5], r.unsqueeze(2).to_broadcast([P, HEADS, 2, HD])).then_inc(parts_m[1], 1)

        def keep_stack(a, offset, g, b, nb):
            if not exists(nb + offset):
                return
            act.wait_ge(stack_turned[a], 3 * (b + offset) + g + 1)
            if g == 0:
                S.copy(kT[a][0:STACK], ps_stack[0:STACK, 0:GROUPS]).then_inc(stack_kept[a], 1)
            else:
                S.copy(qT[a][0:STACK, HALF * (g - 1):HALF * g], ps_stack[0:STACK]).then_inc(stack_kept[a], 1)

        def exponentials(b, nb, i):
            unit = unit_at(b, nb, i)
            if not unit:
                return
            a, _, _, u = unit
            wait_unit(act, shifted, unit)
            S.activation(prob[u][:], prob[u][:], ACT.Exp, scale=SCALE).then_inc(exp_done[a], 1)

        def probs_hi(b, nb, i):
            unit = unit_at(b, nb, i)
            if not unit:
                return
            a, _, _, u = unit
            wait_unit(act, probs_turned, unit)
            S.copy(prob_hi[u][:], ps_probs[:]).then_inc(prob_hi_done[a], 1)

        def share(b, nb):
            if nb == 0:
                act.wait_ge(shared_loaded, 16 * 5)
            for hi, src, n in SHARES:
                S.copy(hi[:, bass.ds(n * b, n)], src[:, bass.ds(n * b, n)]).then_inc(shared_hi, 1)

        def iteration(b, nb):
            keep_stack(0, 0, 2, b, nb)
            probs_hi(b, nb, -1)
            if exists(nb - 1):
                act_hi(1, b - 1)
            exponentials(b, nb, 0)
            keep_stack(1, -2, 0, b, nb)
            if exists(nb - 2):
                middle_parts_cross(b - 2)
            if exists(nb - 3):
                share(b - 3, nb - 3)
            setup_beside(nb, 0)
            probs_hi(b, nb, 0)
            if exists(nb + 1):
                act_hi(0, b + 1)
            keep_stack(1, -2, 1, b, nb)
            exponentials(b, nb, 1)
            setup_beside(nb, 1)
            if exists(nb + 1):
                high_parts_self(b + 1, (nb + 1) % 2)
            probs_hi(b, nb, 1)
            keep_stack(1, -2, 2, b, nb)
            exponentials(b, nb, 2)
            if exists(nb - 3):
                act_hi(2, b - 3)
            if exists(nb + 1):
                middle_parts_self(b + 1, (nb + 1) % 2)
            setup_beside(nb, 2)
            keep_stack(0, 1, 0, b, nb)
            probs_hi(b, nb, 2)
            keep_stack(0, 1, 1, b, nb)
            exponentials(b, nb, 3)
            if exists(nb - 1):
                high_parts_cross(b - 1)

        over_iterations(act, iteration)
        phase_b_scalar(act)
        routing_scalar(act)
        phase_c_scalar(act)

    @block.gpsimd
    def _(pool):
        G = nc.gpsimd
        pool.wait_ge(filled, 6)

        def ctx_scale():
            pool.wait_ge(kv_var, 1)
            G.tensor_scalar(k_rstd[:], k_rstd[:], 1.0 / KVD, EPS, ALU.mult, ALU.add).then_inc(kv_pow, 1)
            pool.wait_ge(kv_pow, 1)
            G.tensor_tensor(k_rstd[:], k_rstd[:], minus_half[:], ALU.pow).then_inc(kv_pow, 1)

        def norm_scale(a, e, mul, add):
            wait_alone(pool, moments_done[a], e + 1)
            G.tensor_scalar(variance[:, a], moments[:, a, 1:2], mul, add, ALU.mult, ALU.add).then_inc(var_eps[a], 1)
            pool.wait_ge(var_eps[a], e + 1)
            G.tensor_tensor(rstd[:, a], variance[:, a], minus_half[:, 0:1], ALU.pow).then_inc(rstd_done[a], 1)

        def low_parts(a, e, blocks):
            pool.wait_ge(parts_m[a], e + 1)
            r = remainder[a][:].rearrange("p (h n) -> p h n", n=HD)
            if a == 0:
                kv = blocks[:, HEADS:]
                G.tensor_tensor(kv[:, :, 2 + 2 * HD:2 + 3 * HD], r[:, HEADS:], kv[:, :, 2 + 4 * HD:2 + 5 * HD], ALU.subtract)
            q = blocks[:, 0:HEADS]
            G.tensor_tensor(q[:, :, 2 + 5 * HD:2 + 6 * HD], r[:, 0:HEADS], q[:, :, 2 + 4 * HD:2 + 5 * HD], ALU.subtract).then_inc(parts_l[a], 1)

        def rotate(e):
            pool.wait_ge(xn_done[1], e + 1)
            G.tensor_tensor(q_fp[:], xn[1][:], cos_w[:, 0:D], ALU.mult).then_inc(rope_step, 1)
            half = lambda v: v.rearrange("p (h t e) -> p h t e", t=2, e=HD // 2)
            G.tensor_tensor(half(q_sin[:]), half(xn[1][:])[:, :, ::-1, :], half(sin_w[:, 0:D]), ALU.mult).then_inc(rope_step, 1)
            pool.wait_ge(rope_step, 2 * e + 2)
            G.tensor_tensor(q_fp[:], q_fp[:], q_sin[:], ALU.add).then_inc(q_done, 1)

        def rest_of_q(e):
            pool.wait_ge(parts_h[1], e + 1)
            G.tensor_tensor(remainder[1][:, 0:D].rearrange("p (h n) -> p h n", n=HD),
                            q_fp[:].rearrange("p (h n) -> p h n", n=HD),
                            cross_stack[:, :, 2:2 + HD], ALU.subtract).then_inc(q_rest, 1)

        def share(b):
            pool.wait_ge(shared_hi, 2 * b + 2)
            for lo, hi, src, n in LOW_SHARES:
                G.tensor_tensor(lo[:, bass.ds(n * b, n)], src[:, bass.ds(n * b, n)],
                                hi[:, bass.ds(n * b, n)].bitcast(F32), ALU.subtract).then_inc(shared_lo, 1)

        def iteration(b, nb):
            if exists(nb + 1):
                norm_scale(0, b + 1, 1.0, EPS)
            if exists(nb - 2):
                low_parts(1, b - 2, cross_stack)
            if exists(nb - 3):
                share(b - 3)
            if exists(nb - 1):
                norm_scale(1, b - 1, 1.0 + EPS, EPS * EPS)
            if exists(nb + 1):
                low_parts(0, b + 1, stack[(nb + 1) % 2])
            if nb == -1:
                ctx_scale()
            if nb == 1:
                pool.wait_ge(kv_step, 3)
            if exists(nb - 1):
                rotate(b - 1)
                rest_of_q(b - 1)

        over_iterations(pool, iteration)
        phase_b_pool(pool)
        routing_pool(pool)
        phase_c_pool(pool)

    block.__exit__(None, None, None)
    sems.close()
    top.close()


_INS = {"x": "x", "ctx_512": "ctx_512", "wq": "L0_attn_Wq", "wk": "L0_attn_Wk", "wv": "L0_attn_Wv", "wo": "L0_attn_Wo",
        "bo": "L0_attn_bo", "q_norm": "L0_xattn_q_norm_w", "k_norm": "L0_xattn_k_norm_w",
        "w_out_t": "L0_xattn_w_out", "router": "L0_ffn_router_w", "w1": "L0_ffn_w1", "w2": "L0_ffn_w2",
        "w_gate": "L0_ffn_w_gate", "w_up": "L0_ffn_w_up", "w_down": "L0_ffn_w_down"}


def kernel(**inputs):
    import concourse.bacc as bacc
    from concourse.bass_utils import run_bass_kernel_spmd

    arrays = {}
    for name, source in _INS.items():
        w = np.asarray(inputs[source])
        arrays[name] = np.ascontiguousarray(w.T if name == "w_out_t" else w)
    B = arrays["x"].shape[0]
    tiles = B * TOPK + EXPERTS
    arrays["squares"], arrays["rope"], arrays["lanes"], arrays["row_ids"] = constants(B, tiles)
    nc = bacc.Bacc("TRN2", target_bir_lowering=False, num_devices=1)
    aps = {name: nc.dram_tensor(f"in_{name}", v.shape, mybir.dt.from_np(v.dtype), kind="ExternalInput").ap()
           for name, v in arrays.items()}
    out = nc.dram_tensor("out", arrays["x"].shape, F32, kind="ExternalOutput").ap()
    decoder_layer(nc, aps, out)
    ran = run_bass_kernel_spmd(nc, [{f"in_{name}": v for name, v in arrays.items()}], core_ids=[0])
    return ran.results[0]["out"]
```

```python
from contextlib import ExitStack

import numpy as np
import concourse.bass as bass
from concourse import mybir

ALU = mybir.AluOpType
ACT = mybir.ActivationFunctionType
AX = mybir.AxisListType
F32 = mybir.dt.float32
F32R = mybir.dt.float32r
BF16 = mybir.dt.bfloat16
F16 = mybir.dt.float16
I32 = mybir.dt.int32

P = 128
D = 256
HEADS, GROUPS, HD = 16, 4, 16
KVD = GROUPS * HD
QKV = D + 2 * KVD
EPS = 1e-5
SCALE = 1.0 / HD ** 0.5
MASKED = -1e30
EXPERTS, INTER, TOPK = 8, 512, 2
SHARED = 2 * INTER
KT = D // P
FT = INTER // P
FLIGHT = 4
BESIDE_ROUTING = 4

SLOTS = 6
STACK = SLOTS * HD
BLOCK = 2 + STACK
VCOLS = 1 + 3 * HD
KV = 2 * GROUPS
HALF = HEADS // 2

WEIGHT, ROW_ID, ROW = D, D + 1, D + 2

L_PRIORITY = 0
L_FULL = L_PRIORITY + EXPERTS


def constants(B, TILES):
    t = np.arange(P)
    ident = np.eye(P)
    causal = np.where(t[:, None] < t[None, :], MASKED, 0.0)
    earlier = (t[:, None] < t[None, :]) * 1.0
    first = (t[:, None] == 0) * np.ones((1, P))
    squares = np.stack([ident, causal, earlier, first], 1).astype(np.float32)
    freq = np.outer(t.astype(np.float32), (1.0 / 10000.0 ** (np.arange(0, HD, 2, dtype=np.float32) / HD)).astype(np.float32))
    cos = np.concatenate([np.cos(freq), np.cos(freq)], 1)
    sin = np.concatenate([-np.sin(freq), np.sin(freq)], 1)
    rope = np.stack([cos, sin], 1).astype(np.float32)
    row = np.concatenate([
        EXPERTS - np.arange(EXPERTS), 128.0 * np.arange(B), np.arange(TILES),
        np.tile((np.arange(B) > 0) * 1.0, EXPERTS), np.ones(EXPERTS)]).astype(np.float32)
    lanes = np.broadcast_to(row, (P, row.size)).copy()
    token = P * np.arange(B)[None, :] + t[:, None]
    row_ids = (TOPK * token[:, None, :] + np.arange(TOPK)[None, :, None]).astype(np.int32)
    return squares, rope, lanes, row_ids


def decoder_layer(nc, a, out):
    x, ctx_512 = a["x"], a["ctx_512"]
    B = x.shape[0]
    PAIRS = B // 2
    CHOICES = B * P * TOPK
    TILES = CHOICES // P + EXPERTS
    assert TILES % FLIGHT == 0 and B % 2 == 0
    NO_ROW = CHOICES
    dispatched = nc.dram_tensor("dispatched", (TILES * P, ROW), F32, kind="Internal").ap()
    combined = nc.dram_tensor("combined", (CHOICES, D), F32, kind="Internal").ap()

    L_IOTA = L_FULL + B
    L_CARRY = L_IOTA + TILES
    L_ONES = L_CARRY + EXPERTS * B

    top = ExitStack()

    def maker(scope):
        def sb(name, shape, dt):
            return scope.enter_context(nc.sbuf_tensor(name, shape, dt))
        return sb

    sb = maker(top)
    tokens = sb("tokens", [P, B, D], F32)
    over_shared = [nc.sbuf_base]
    wgu_hi = sb("wgu_hi", [P, KT, 2, 2, INTER], F32R)
    wgu_lo = sb("wgu_lo", [P, KT, 2, 2, INTER], F32R)
    wd_hi = sb("wd_hi", [P, 2, FT, D], F32R)
    wd_lo = sb("wd_lo", [P, 2, FT, D], F32R)
    rt_hi = sb("rt_hi", [P, KT, D], F32R)
    rt_lo = sb("rt_lo", [P, KT, D], F32R)
    squares = sb("squares", [P, 4, P], F32)
    identity, earlier_fp = squares[:, 0], squares[:, 2]
    lane = sb("lane", [P, L_ONES + EXPERTS], F32)
    bstats = sb("bstats", [P, 2, 6], F32)
    moments = sb("moments", [P, 2, 2], F32)
    variance = sb("variance", [P, 2, 1], F32)
    rstd = sb("rstd", [P, 2, 1], F32)
    minus_half = sb("minus_half", [P, B], F32)
    xn = [sb(f"xn{s}", [P, D], F32) for s in range(2)]
    actT_hi = [sb(f"actT_hi{s}", [P, KT, P], F32R) for s in range(2)]
    actT_lo = [sb(f"actT_lo{s}", [P, KT, P], F32R) for s in range(2)]

    phase_a = ExitStack()
    sb = maker(phase_a)
    wqkv_hi = sb("wqkv_hi", [P, KT, QKV], F32R)
    wqkv_lo = sb("wqkv_lo", [P, KT, QKV], F32R)
    wproj_hi = sb("wproj_hi", [P, 2, KT, D], F32R)
    wproj_lo = sb("wproj_lo", [P, 2, KT, D], F32R)
    bias_hi = sb("bias_hi", [P, D], F32R)
    bias_lo = sb("bias_lo", [P, D], F32R)
    first_row = sb("first_row", [P, P], F32R)
    raw = sb("raw", [P, KT * 2 * SHARED + FT * 2 * D], F32)
    raw_qkv = sb("raw_qkv", [P, KT, QKV], F32)
    raw_proj = sb("raw_proj", [P, 2, KT, D], F32)
    raw_bias = sb("raw_bias", [P, D], F32)
    raw_router = sb("raw_router", [P, KT, EXPERTS], F32)
    mask_bf = sb("mask_bf", [P, 4, P], BF16)
    ident_bf = sb("ident_bf", [P, P], BF16)
    rope = sb("rope", [P, 2, HD], F32)
    norm_w = sb("norm_w", [P, D + KVD], F32)
    cos_w = sb("cos_w", [P, D + KVD], F32)
    sin_w = sb("sin_w", [P, D + KVD], F32)
    cross_kv = sb("cross_kv", [P, B, KV, BLOCK], BF16)
    stack = [sb(f"stack{s}", [P, HEADS + KV, BLOCK], BF16) for s in range(2)]
    remainder = [sb(f"remainder{a}", [P, QKV], F32) for a in range(2)]
    cross_stack = sb("cross_stack", [P, HEADS, BLOCK], BF16)
    q_fp = sb("q_fp", [P, D], F32)
    q_sin = sb("q_sin", [P, D], F32)
    qT = [sb(f"qT{a}", [P, HEADS, P], BF16) for a in range(2)]
    kT = [sb(f"kT{a}", [P, GROUPS, P], BF16) for a in range(2)]
    row_max = [sb(f"row_max{u}", [P, HALF], F32) for u in range(2)]
    prob = [sb(f"prob{u}", [P, HALF, P], F32) for u in range(2)]
    prob_hi = [sb(f"prob_hi{u}", [P, HALF, P], F16) for u in range(2)]
    prob_lo = [sb(f"prob_lo{u}", [P, HALF, P], F16) for u in range(2)]
    heads = [sb(f"heads{a}", [P, HEADS, HD], F32) for a in range(2)]
    denom = [sb(f"denom{a}", [P, HEADS], F32) for a in range(2)]
    mixed = [sb(f"mixed{a}", [P, HEADS, HD], F32) for a in range(2)]
    ctx_sb = sb("ctx_sb", [P, B, KVD], F32)
    k_rstd = sb("k_rstd", [P, B], F32)
    empty_rows = sb("empty_rows", [P, ROW], F32)
    phase_a.close()
    kv_fp = raw[:, 0:B * 2 * KVD].rearrange("p (b n) -> p b n", b=B)
    kv_a = raw[:, B * 2 * KVD:2 * B * 2 * KVD].rearrange("p (b n) -> p b n", b=B)
    kv_b = raw[:, 2 * B * 2 * KVD:3 * B * 2 * KVD].rearrange("p (b n) -> p b n", b=B)
    raw_gu = raw[:, 0:KT * 2 * SHARED]
    raw_d = raw[:, KT * 2 * SHARED:]

    phase_c = ExitStack()
    sb = maker(phase_c)
    rows = sb("rows", [P, B, ROW], F32)
    w1_sb = sb("w1_sb", [P, EXPERTS, KT, 2, INTER], F32)
    w2_sb = sb("w2_sb", [P, EXPERTS, FT, D], F32)
    logits = sb("logits", [P, B, EXPERTS], F32)
    silu = [sb(f"silu{u}", [P, INTER], F32) for u in range(2)]
    hT_hi = [sb(f"hT_hi{u}", [P, FT, P], F32R) for u in range(2)]
    hT_lo = [sb(f"hT_lo{u}", [P, FT, P], F32R) for u in range(2)]
    best = [sb(f"best{k}", [P, B], F32) for k in range(2)]
    hit = sb("hit", [P, B, EXPERTS], F32)
    pick = [sb(f"pick{k}", [P, B, EXPERTS], F32) for k in range(2)]
    top_priority = sb("top_priority", [P, B], F32)
    masked_logits = sb("masked_logits", [P, B, EXPERTS], F32)
    weight = [sb(f"weight{k}", [P, B], F32) for k in range(2)]
    ratio = sb("ratio", [P, B], F32)
    chosen = sb("chosen", [P, B, EXPERTS], BF16)
    ones_bf = sb("ones_bf", [P, P], BF16)
    earlier_bf = sb("earlier_bf", [P, P], BF16)
    counts = sb("counts", [P, 3, EXPERTS, B], F32)
    upto, begun, place = (counts[:, i] for i in range(3))
    n_tiles = sb("n_tiles", [P, EXPERTS], F32)
    end_tile = sb("end_tile", [P, EXPERTS], F32)
    start_row = sb("start_row", [P, EXPERTS], F32)
    where_fp = [sb(f"where_fp{k}", [P, B], F32) for k in range(2)]
    where = [sb(f"where{k}", [P, B], I32) for k in range(2)]
    assert TILES <= 3 * B
    passed = counts[:].rearrange("p i e b -> p (i e b)")[:, 0:TILES * EXPERTS].rearrange("p (t e) -> p t e", e=EXPERTS)
    tile_expert_fp = sb("tile_expert_fp", [P, TILES], F32)
    tile_expert = sb("tile_expert", [P, TILES], I32)
    row_id_sb = sb("row_id_sb", [P, TOPK, B], I32)
    phase_c.close()

    def over(name, shape, dt):
        words = int(np.prod(shape[1:]))
        t = nc.alloc_sbuf_tensor_at(name, shape, dt, offset=over_shared[0])
        over_shared[0] += -(-words * mybir.dt.size(dt) // 32) * 32
        return t

    tile_in = [over(f"tile_in{u}", [P, ROW], F32) for u in range(FLIGHT)]
    tile_out = [over(f"tile_out{u}", [P, D], F32) for u in range(FLIGHT)]
    xT_fp = [over(f"xT_fp{u}", [P, KT, P], F32) for u in range(2)]
    hT_fp = [over(f"hT_fp{u}", [P, FT, P], F32) for u in range(2)]
    QUARTERS, QB = 4, B // 4
    products = w1_sb[:].rearrange("p e k g n -> p (e k g n)")[:, 0:B * TOPK * D].rearrange(
        "p (c b k n) -> p c b k n", c=QUARTERS, b=QB, k=TOPK)

    psum_a = ExitStack()
    ps_scores = psum_a.enter_context(nc.psum_tensor("ps_scores", [P, HALF, P], F32))
    ps_probs = psum_a.enter_context(nc.psum_tensor("ps_probs", [P, HALF, P], F32))
    ps_stack = psum_a.enter_context(nc.psum_tensor("ps_stack", [P, HALF, P], BF16))
    ps_heads = psum_a.enter_context(nc.psum_tensor("ps_heads", [P, 512], F32))
    ps_proj = psum_a.enter_context(nc.psum_tensor("ps_proj", [P, 512], F32))
    ps_actT = psum_a.enter_context(nc.psum_tensor("ps_actT", [P, 4, P], F32))
    psum_a.close()
    psum_c = ExitStack()
    ps_gu = [psum_c.enter_context(nc.psum_tensor(f"ps_gu{u}", [P, 2, INTER], F32)) for u in range(2)]
    ps_hT = psum_c.enter_context(nc.psum_tensor("ps_hT", [P, FT, P], F32))
    ps_y = psum_c.enter_context(nc.psum_tensor("ps_y", [P, 512], F32))
    ps_router = psum_c.enter_context(nc.psum_tensor("ps_router", [P, 512], F32))
    ps_xT = psum_c.enter_context(nc.psum_tensor("ps_xT", [P, 4, P], F32))
    psum_c.close()

    sems = ExitStack()

    def sem(name):
        return sems.enter_context(nc.semaphore(name))

    lane_loaded, squares_loaded, x_loaded, rest_loaded, qkv_loaded, consts_loaded, attn_loaded, ctx_loaded, shared_loaded = map(
        sem, ["lane_loaded", "squares_loaded", "x_loaded", "rest_loaded", "qkv_loaded", "consts_loaded", "attn_loaded", "ctx_loaded", "shared_loaded"])
    empty_made, emptied = sem("empty_made"), sem("emptied")
    filled_act, unread = sem("filled_act"), sem("unread")
    filled, hi_made, lo_made, kv_step, kv_var, kv_pow, kv_src, kv_h, kv_r, kv_m, kv_l = map(sem, [
        "filled", "hi_made", "lo_made", "kv_step", "kv_var", "kv_pow", "kv_src", "kv_h", "kv_r", "kv_m", "kv_l"])
    shared_hi, shared_lo, a_ends, b_ends = map(sem, ["shared_hi", "shared_lo", "a_ends", "b_ends"])
    def each(names, n):
        return [[sem(f"{name}{i}") for i in range(n)] for name in names]

    stats_done, moments_done, var_eps, rstd_done, xn_done = each(
        ["stats_done", "moments_done", "var_eps", "rstd_done", "xn_done"], 2)
    act_turned, act_hi_done, act_lo_done, projected, proj_read = each([
        "act_turned", "act_hi_done", "act_lo_done", "projected", "proj_read"], 3)
    parts_h, parts_m, parts_l, stack_turned, stack_kept = each([
        "parts_h", "parts_m", "parts_l", "stack_turned", "stack_kept"], 2)
    q_rest, rope_step, q_done = map(sem, ["q_rest", "rope_step", "q_done"])
    scored, max_done, shifted, exp_done, probs_turned, prob_hi_done, prob_lo_done = each([
        "scored", "max_done", "shifted", "exp_done", "probs_turned", "prob_hi_done", "prob_lo_done"], 2)
    heads_done, heads_summed, heads_read, mixed_done = each([
        "heads_done", "heads_summed", "heads_read", "mixed_done"], 2)

    n_stats, n_moments, n_var, n_rstd, n_xn, n_kept = map(sem, ["n_stats", "n_moments", "n_var", "n_rstd", "n_xn", "n_kept"])
    n_turned, n_hi, n_lo, n_routed, n_logits = map(sem, ["n_turned", "n_hi", "n_lo", "n_routed", "n_logits"])
    b_xn, b_turned, b_hi, b_lo = map(sem, ["b_xn", "b_turned", "b_hi", "b_lo"])
    b_gu, b_silu, b_gated, b_hturned, b_hhi, b_hlo, b_down, b_added = map(
        sem, ["b_gu", "b_silu", "b_gated", "b_hturned", "b_hhi", "b_hlo", "b_down", "b_added"])
    ones_made, r_step, r_exp, r_in, r_ranked, r_ready, r_meta, r_placed = map(
        sem, ["ones_made", "r_step", "r_exp", "r_in", "r_ranked", "r_ready", "r_meta", "r_placed"])
    r_sent, experts_loaded, ids_loaded = map(sem, ["r_sent", "experts_loaded", "ids_loaded"])
    c_loaded = [sem(f"c_loaded{u}") for u in range(FLIGHT)]
    c_stored = [sem(f"c_stored{u}") for u in range(FLIGHT)]
    c_turned, c_kept, c_gu, c_silu, c_gated, c_hturned, c_hkept, c_down, c_scaled = map(sem, [
        "c_turned", "c_kept", "c_gu", "c_silu", "c_gated", "c_hturned", "c_hkept", "c_down", "c_scaled"])
    pairs_loaded = [sem(f"pairs_loaded{c}") for c in range(QUARTERS)]
    pairs_added, result_stored = sem("pairs_added"), sem("result_stored")

    A_OVER = B
    B_OVER = B + 1

    block = nc.Block()
    block.__enter__()

    def wait_alone(engine, semaphore, value):
        engine.wait_ge(semaphore, value)
        engine.sem_inc(unread, 1)

    def over_elements(engine, step, first=0):
        for b in range(first):
            step(b, b % 2, 2)
        with engine.Fori(first // 2, PAIRS - 1) as it:
            for s in range(2):
                step(2 * it + s, s, 2)
        step(B - 2, 0, 1)
        step(B - 1, 1, 0)

    all_stats = silu[0][:, 0:6 * B].rearrange("p (b n) -> p b n", n=6)
    all_moments = silu[0][:, 6 * B:8 * B].rearrange("p (b n) -> p b n", n=2)
    all_rstd = silu[0][:, 8 * B:9 * B]

    def router_tensor(pe):
        def turn(b, s):
            pe.wait_ge(n_xn, b + 1)
            for t in range(KT):
                mm = pe.transpose(ps_xT[:, t], xn[s][:, t * P:(t + 1) * P], identity)
            mm.then_inc(n_turned, 1)

        def step(b, s, following):
            pe.wait_ge(n_lo, b + 1)
            if following:
                turn(b + 1, 1 - s)
            pe.wait_ge(n_logits, b + 1)
            for t in range(KT):
                mm = three_products(pe, ps_gu[s][:, 0, 0:D], actT_hi[s][:, t], actT_lo[s][:, t],
                                    rt_hi[:, t], rt_lo[:, t], t == 0, t == KT - 1)
            mm.then_inc(n_routed, 1)

        pe.wait_ge(proj_read[2], A_OVER)
        turn(0, 0)
        over_elements(pe, step)

    def router_scalar(act):
        S = nc.scalar

        def step(b, s, following):
            act.wait_ge(n_turned, b + 1)
            S.copy(actT_hi[s][:], ps_xT[:, 0:KT]).then_inc(n_hi, 1)
            S.copy(rows[:, bass.ds(b, 1), 0:D], xn[s][:].unsqueeze(1)).then_inc(n_kept, 1)

        act.wait_ge(proj_read[2], A_OVER)
        over_elements(act, step)

    def router_vector(dve):
        V = nc.vector

        def normalise(b, s):
            V.tensor_scalar(xn[s][:].unsqueeze(1), tokens[:, bass.ds(b, 1), :], all_moments[:, bass.ds(b, 1), 0:1],
                            all_rstd[:, bass.ds(b, 1)], ALU.subtract, ALU.mult).then_inc(n_xn, 1)

        def keep_logits(b, s):
            dve.wait_ge(n_routed, b + 1)
            V.tensor_copy(logits[:, bass.ds(b, 1), :], ps_gu[s][:, 0, 0:EXPERTS].unsqueeze(1)).then_inc(n_logits, 1)

        def step(b, s, following):
            dve.wait_ge(n_hi, b + 1)
            V.tensor_tensor(actT_lo[s][:], ps_xT[:, 0:KT], actT_hi[s][:].bitcast(F32), ALU.subtract).then_inc(n_lo, 1)
            if following == 2:
                dve.wait_ge(n_kept, b + 1)
                normalise(b + 2, s)
            if not (isinstance(b, int) and b == 0):
                keep_logits(b - 1, 1 - s)

        dve.nop().then_inc(n_logits, 2)
        dve.wait_ge(proj_read[2], A_OVER)
        for b in range(B):
            V.bn_stats(all_stats[:, b], tokens[:, b]).then_inc(n_stats, 1)
        for b in range(B):
            dve.wait_ge(n_stats, b + 1)
            V.bn_aggr(all_moments[:, b], all_stats[:, b]).then_inc(n_moments, 1)
        dve.wait_ge(n_rstd, 1)
        for b in range(2):
            normalise(b, b)
        over_elements(dve, step, 2)
        keep_logits(B - 1, 1)

    def router_pool(pool):
        G = nc.gpsimd
        pool.wait_ge(n_moments, B)
        G.tensor_scalar(all_rstd, all_moments[:, :, 1], EPS, None, ALU.add).then_inc(n_var, 1)
        pool.wait_ge(n_var, 1)
        G.tensor_tensor(all_rstd, all_rstd, minus_half[:], ALU.pow).then_inc(n_rstd, 1)

    def b_unit(b, c):
        return 2 * b + c

    def phase_b_tensor(pe):
        def turn(b, s):
            pe.wait_ge(b_xn, b + 1)
            pe.wait_ge(b_lo, b + 1)
            for t in range(KT):
                mm = pe.transpose(ps_xT[:, t], xn[s][:, t * P:(t + 1) * P], identity)
            mm.then_inc(b_turned, 1)

        def gate_up(b, s, c):
            pe.wait_ge(b_lo, b + 2)
            pe.wait_ge(b_gated, b_unit(b, c) + 1)
            for g in range(2):
                for t in range(KT):
                    mm = three_products(pe, ps_gu[c][:, g], actT_hi[s][:, t], actT_lo[s][:, t],
                                        wgu_hi[:, t, c, g], wgu_lo[:, t, c, g], t == 0, t == KT - 1)
            mm.then_inc(b_gu, 1)

        def turn_hidden(b, c):
            m = b_unit(b, c)
            pe.wait_ge(b_gated, m + 3)
            pe.wait_ge(b_hlo, m + 1)
            for t in range(FT):
                mm = pe.transpose(ps_hT[:, t], silu[c][:, t * P:(t + 1) * P], identity)
            mm.then_inc(b_hturned, 1)

        def down(b, c):
            m = b_unit(b, c)
            pe.wait_ge(b_hlo, m + 2)
            if c == 0:
                pe.wait_ge(b_added, b + 1)
            for t in range(FT):
                mm = three_products(pe, ps_y[:, 0:D], hT_hi[c][:, t], hT_lo[c][:, t],
                                    wd_hi[:, c, t], wd_lo[:, c, t], c == 0 and t == 0, c == 1 and t == FT - 1)
            if c == 1:
                mm.then_inc(b_down, 1)

        def step(b, s, following):
            turn_hidden(b, 0)
            gate_up(b, s, 1)
            if following:
                turn(b + 1, 1 - s)
            down(b, 0)
            if isinstance(b, int) and b == 1:
                routing_tensor(pe)
            turn_hidden(b, 1)
            if following:
                gate_up(b + 1, 1 - s, 0)
            down(b, 1)

        pe.wait_ge(shared_lo, 2 * B)
        turn(0, 0)
        gate_up(0, 0, 0)
        over_elements(pe, step, BESIDE_ROUTING)

    def phase_b_scalar(act):
        S = nc.scalar

        def take_row(b, s):
            S.copy(xn[s][:].unsqueeze(1), rows[:, bass.ds(b, 1), 0:D]).then_inc(b_xn, 1)

        def act_hi(b, s):
            act.wait_ge(b_turned, b + 1)
            S.copy(actT_hi[s][:], ps_xT[:, 0:KT]).then_inc(b_hi, 1)

        def gate(b, c):
            act.wait_ge(b_gu, b_unit(b, c) + 1)
            S.activation(silu[c][:], ps_gu[c][:, 0], ACT.Silu).then_inc(b_silu, 1)

        def hidden_hi(b, c):
            act.wait_ge(b_hturned, b_unit(b, c) + 1)
            S.copy(hT_hi[c][:], ps_hT[:]).then_inc(b_hhi, 1)

        def step(b, s, following):
            gate(b, 0)
            hidden_hi(b, 0)
            if following:
                act_hi(b + 1, 1 - s)
            gate(b, 1)
            hidden_hi(b, 1)
            if isinstance(b, int) and b == 1:
                routing_scalar(act)
            if following == 2:
                take_row(b + 2, s)

        act.wait_ge(n_kept, B)
        take_row(0, 0)
        take_row(1, 1)
        act.wait_ge(n_routed, B)
        act_hi(0, 0)
        over_elements(act, step, BESIDE_ROUTING)

    def phase_b_vector(dve, routing):
        V = nc.vector

        def act_lo(b, s):
            dve.wait_ge(b_hi, b + 1)
            V.tensor_tensor(actT_lo[s][:], ps_xT[:, 0:KT], actT_hi[s][:].bitcast(F32), ALU.subtract).then_inc(b_lo, 1)

        def gated(b, c):
            dve.wait_ge(b_silu, b_unit(b, c) + 1)
            V.tensor_tensor(silu[c][:], silu[c][:], ps_gu[c][:, 1], ALU.mult).then_inc(b_gated, 1)

        def hidden_lo(b, c):
            dve.wait_ge(b_hhi, b_unit(b, c) + 1)
            V.tensor_tensor(hT_lo[c][:], ps_hT[:], hT_hi[c][:].bitcast(F32), ALU.subtract).then_inc(b_hlo, 1)

        def add(b):
            dve.wait_ge(b_down, b + 1)
            V.tensor_tensor(tokens[:, bass.ds(b, 1), :], tokens[:, bass.ds(b, 1), :], ps_y[:, 0:D].unsqueeze(1),
                            ALU.add).then_inc(b_added, 1)

        def step(b, s, following):
            hidden_lo(b, 0)
            if following:
                act_lo(b + 1, 1 - s)
            if isinstance(b, int):
                routing(b, 0)
            gated(b, 1)
            hidden_lo(b, 1)
            if isinstance(b, int):
                routing(b, 1)
            if following:
                gated(b + 1, 0)
            add(b)

        for credit, n in ((b_lo, 1), (b_gated, 2), (b_hlo, 1), (b_added, 1)):
            dve.nop().then_inc(credit, n)
        act_lo(0, 0)
        gated(0, 0)
        over_elements(dve, step, BESIDE_ROUTING)

    def routing_vector(dve):
        V = nc.vector
        done = 0

        def then(ins):
            nonlocal done
            ins.then_inc(r_step, 1)
            done += 1
            dve.wait_ge(r_step, done)

        def over_experts(v):
            return v.unsqueeze(2).to_broadcast([P, B, EXPERTS])

        priority = lane[:, L_PRIORITY:L_FULL].unsqueeze(1).to_broadcast([P, B, EXPERTS])

        def choose(k):
            source = masked_logits if k else logits
            then(V.tensor_reduce(best[k][:], source[:], AX.X, ALU.max))
            then(V.tensor_tensor(hit[:], source[:], over_experts(best[k][:]), ALU.is_ge))
            then(V.tensor_tensor(hit[:], hit[:], priority, ALU.mult))
            then(V.tensor_reduce(top_priority[:], hit[:], AX.X, ALU.max))
            then(V.tensor_tensor(pick[k][:], hit[:], over_experts(top_priority[:]), ALU.is_ge))

        def first_choice():
            dve.wait_ge(n_logits, B + 2)
            dve.wait_ge(lane_loaded, 16)
            V.memset(ones_bf[:], 1.0).then_inc(ones_made, 1)
            then(V.tensor_copy(earlier_bf[:], earlier_fp))
            choose(0)

        def second_choice():
            then(V.scalar_tensor_tensor(masked_logits[:], pick[0][:], -3e38, logits[:], ALU.mult, ALU.add))
            choose(1)
            then(V.tensor_tensor(ratio[:], best[1][:], best[0][:], ALU.subtract))
            V.tensor_tensor(chosen[:], pick[0][:], pick[1][:], ALU.add).then_inc(r_in, 1)

        ranks = ps_router[:, 0:B * EXPERTS].rearrange("p (b e) -> p e b", e=EXPERTS)
        totals = ps_router[:, B * EXPERTS:2 * B * EXPERTS].rearrange("p (b e) -> p e b", e=EXPERTS)
        flat = lambda v: v.rearrange("p e b -> p (e b)")
        full = lane[:, L_FULL:L_IOTA].unsqueeze(1).to_broadcast([P, EXPERTS, B])

        def weights_and_counts():
            dve.wait_ge(r_exp, 1)
            then(V.tensor_scalar(weight[0][:], ratio[:], 1.0, None, ALU.add))
            then(V.reciprocal(weight[0][:], weight[0][:]))
            then(V.tensor_tensor(weight[1][:], ratio[:], weight[0][:], ALU.mult))
            dve.wait_ge(r_ranked, 1)
            then(V.tensor_copy(place, totals))
            then(V.tensor_tensor_scan(flat(upto), lane[:, L_CARRY:L_ONES], flat(place), 0.0, ALU.mult, ALU.add))

        def tiles_of_experts():
            then(V.tensor_tensor(begun, upto[:, :, B - 1:B].to_broadcast([P, EXPERTS, B]), full, ALU.is_gt))
            then(V.tensor_reduce(n_tiles[:], begun, AX.X, ALU.add))
            then(V.tensor_scalar(n_tiles[:], n_tiles[:], 1.0, None, ALU.max))
            then(V.tensor_tensor_scan(end_tile[:], lane[:, L_ONES:], n_tiles[:], 0.0, ALU.mult, ALU.add))
            then(V.tensor_tensor(start_row[:], end_tile[:], n_tiles[:], ALU.subtract))
            then(V.tensor_scalar(start_row[:], start_row[:], float(P), None, ALU.mult))

        def places():
            then(V.tensor_tensor(place, upto, place, ALU.subtract))
            then(V.tensor_tensor(place, place, ranks, ALU.add))
            then(V.tensor_tensor(place, place, start_row[:].unsqueeze(2).to_broadcast([P, EXPERTS, B]), ALU.add))

        def places_of_choice(k):
            then(V.tensor_tensor(hit[:], pick[k][:], place.rearrange("p e b -> p b e"), ALU.mult))
            then(V.tensor_reduce(where_fp[k][:], hit[:], AX.X, ALU.add))
            V.tensor_copy(where[k][:], where_fp[k][:]).then_inc(r_placed, 1)

        def expert_of_tiles():
            ends = end_tile[:].unsqueeze(1).to_broadcast([P, TILES, EXPERTS])
            tiles = lane[:, L_IOTA:L_CARRY].unsqueeze(2).to_broadcast([P, TILES, EXPERTS])
            then(V.tensor_tensor(passed, ends, tiles, ALU.is_le))
            then(V.tensor_reduce(tile_expert_fp[:], passed, AX.X, ALU.add))
            then(V.tensor_scalar(tile_expert_fp[:], tile_expert_fp[:], float(EXPERTS - 1), None, ALU.min))
            V.tensor_copy(tile_expert[:], tile_expert_fp[:]).then_inc(r_ready, 1)

        def routing(b, point):
            if (b, point) == (0, 0):
                first_choice()
            elif (b, point) == (0, 1):
                second_choice()
            elif (b, point) == (2, 0):
                weights_and_counts()
            elif (b, point) == (2, 1):
                tiles_of_experts()
            elif (b, point) == (3, 0):
                places()
                places_of_choice(0)
            elif (b, point) == (3, 1):
                places_of_choice(1)
                expert_of_tiles()

        return routing

    def routing_tensor(pe):
        pe.wait_ge(r_in, 1)
        m = chosen[:].rearrange("p b e -> p (b e)")
        pe.matmul(ps_router[:, 0:B * EXPERTS], earlier_bf[:], m, start=True, stop=True)
        pe.matmul(ps_router[:, B * EXPERTS:2 * B * EXPERTS], ones_bf[:], m, start=True, stop=True).then_inc(r_ranked, 1)

    def routing_scalar(act):
        act.wait_ge(r_step, 13)
        nc.scalar.activation(ratio[:], ratio[:], ACT.Exp).then_inc(r_exp, 1)

    def routing_pool(pool):
        G = nc.gpsimd
        pool.wait_ge(emptied, 16)
        pool.wait_ge(ids_loaded, 16)
        pool.wait_ge(n_kept, B)
        for k in range(TOPK):
            pool.wait_ge(r_placed, k + 1)
            if k > 0:
                pool.wait_ge(r_sent, 16 * B)
            G.tensor_copy(rows[:, :, WEIGHT], weight[k][:])
            G.tensor_copy(rows[:, :, ROW_ID].bitcast(I32), row_id_sb[:, k]).then_inc(r_meta, 1)
            pool.wait_ge(r_meta, k + 1)
            for b in range(B):
                pool.indirect_dma_start(dispatched, bass.IndirectOffsetOnAxis(ap=where[k][:, b:b + 1], axis=0),
                                        rows[:, b], None, bounds_check=TILES * P - 1, oob_is_err=False).then_inc(r_sent, 16)

    def over_tiles(engine, step, registers=None):
        def experts_from(i):
            return registers(i) if registers else [None] * (FLIGHT + 1)

        with engine.Fori(0, TILES // FLIGHT - 1) as it:
            e = experts_from(FLIGHT * it)
            for u in range(FLIGHT):
                step(FLIGHT * it + u, u, it, e[u:], 2)
        e = experts_from(TILES - FLIGHT)
        for u in range(FLIGHT):
            step(TILES - FLIGHT + u, u, TILES // FLIGHT - 1, e[u:], min(2, FLIGHT - 1 - u))

    def phase_c_sync(sp):
        sp.wait_ge(r_sent, 16 * B * TOPK)
        for u in range(FLIGHT):
            sp.dma_start(tile_in[u][:], dispatched[u * P:(u + 1) * P, :]).then_inc(c_loaded[u], 16)
        with sp.Fori(1, TILES // FLIGHT) as it:
            for u in range(FLIGHT):
                sp.wait_ge(c_stored[u], 16 * it)
                sp.dma_start(tile_in[u][:], dispatched[bass.ds((FLIGHT * it + u) * P, P), :]).then_inc(c_loaded[u], 16)

    def phase_c_tensor(pe):
        def turn(i, u, loads):
            pe.wait_ge(c_loaded[u], 16 * loads)
            pe.wait_ge(c_kept, i + 1)
            for t in range(KT):
                mm = pe.transpose(ps_xT[:, t], tile_in[u][:, t * P:(t + 1) * P], identity)
            mm.then_inc(c_turned, 1)

        def gate_up(i, u, e):
            v = u % 2
            pe.wait_ge(c_kept, i + 2)
            pe.wait_ge(c_gated, i + 1)
            for g in range(2):
                for t in range(KT):
                    mm = pe.matmul(ps_gu[v][:, g], xT_fp[v][:, t], w1_sb[:, bass.ds(e, 1), t, g],
                                   start=t == 0, stop=t == KT - 1)
            mm.then_inc(c_gu, 1)

        def turn_hidden(i, u):
            v = u % 2
            pe.wait_ge(c_gated, i + 3)
            pe.wait_ge(c_hkept, i + 1)
            for t in range(FT):
                mm = pe.transpose(ps_hT[:, t], silu[v][:, t * P:(t + 1) * P], identity)
            mm.then_inc(c_hturned, 1)

        def down(i, u, e):
            v = u % 2
            pe.wait_ge(c_hkept, i + 2)
            pe.wait_ge(c_scaled, i + 1)
            for t in range(FT):
                mm = pe.matmul(ps_y[:, 0:D], hT_fp[v][:, t], w2_sb[:, bass.ds(e, 1), t], start=t == 0, stop=t == FT - 1)
            mm.then_inc(c_down, 1)

        def registers(i):
            n = FLIGHT + 1 if not isinstance(i, int) else FLIGHT
            return [pe.value_load(tile_expert[0:1, bass.ds(i + j, 1)], min_val=0, max_val=EXPERTS - 1) for j in range(n)]

        def step(i, u, r, e, following):
            turn_hidden(i, u)
            if following:
                gate_up(i + 1, u + 1, e[1])
            if following == 2:
                turn(i + 2, (u + 2) % FLIGHT, r + (u + 2) // FLIGHT + 1)
            down(i, u, e[0])

        pe.wait_ge(r_ready, 1)
        pe.wait_ge(experts_loaded, 16 * 2 * EXPERTS)
        first = registers(0)[0]
        turn(0, 0, 1)
        gate_up(0, 0, first)
        turn(1, 1, 1)
        over_tiles(pe, step, registers)

    def phase_c_scalar(act):
        S = nc.scalar

        def step(i, u, r, e, following):
            act.wait_ge(c_gu, i + 1)
            S.activation(silu[u % 2][:], ps_gu[u % 2][:, 0], ACT.Silu).then_inc(c_silu, 1)

        over_tiles(act, step)

    def phase_c_vector(dve):
        V = nc.vector
        for credit, n in ((c_kept, 1), (c_hkept, 1), (c_gated, 2), (c_scaled, 1)):
            dve.nop().then_inc(credit, n)

        def keep_x(i, u):
            dve.wait_ge(c_turned, i + 1)
            V.tensor_copy(xT_fp[u % 2][:], ps_xT[:, 0:KT]).then_inc(c_kept, 1)

        def gated(i, u):
            dve.wait_ge(c_silu, i + 1)
            V.tensor_tensor(silu[u % 2][:], silu[u % 2][:], ps_gu[u % 2][:, 1], ALU.mult).then_inc(c_gated, 1)

        def keep_h(i, u):
            dve.wait_ge(c_hturned, i + 1)
            V.tensor_copy(hT_fp[u % 2][:], ps_hT[:]).then_inc(c_hkept, 1)

        def scale(i, u):
            dve.wait_ge(c_down, i + 1)
            V.tensor_scalar(tile_out[u][:], ps_y[:, 0:D], tile_in[u][:, WEIGHT:WEIGHT + 1], None, ALU.mult).then_inc(c_scaled, 1)

        def step(i, u, r, e, following):
            keep_h(i, u)
            if following == 2:
                keep_x(i + 2, u + 2)
            if following:
                gated(i + 1, u + 1)
            scale(i, u)

        keep_x(0, 0)
        gated(0, 0)
        keep_x(1, 1)
        over_tiles(dve, step)
        for c in range(QUARTERS):
            dve.wait_ge(pairs_loaded[c], 16)
            for k in range(TOPK):
                mine = tokens[:, c * QB:(c + 1) * QB]
                V.tensor_tensor(mine, mine, products[:, c, :, k], ALU.add).then_inc(pairs_added, 1)
                dve.wait_ge(pairs_added, TOPK * c + k + 1)

    def phase_c_pool(pool):
        last_row = pool.to_reg(CHOICES - 1)
        with pool.Fori(0, TILES // FLIGHT) as it:
            for u in range(FLIGHT):
                wait_alone(pool, c_scaled, FLIGHT * it + u + 2)
                pool.indirect_dma_start(combined, bass.IndirectOffsetOnAxis(ap=tile_in[u][:, ROW_ID:ROW].bitcast(I32), axis=0),
                                        tile_out[u][:], None, bounds_check=last_row, oob_is_err=False).then_inc(c_stored[u], 16)

    def exists(element):
        return 0 <= element < B

    def over_iterations(engine, iteration):
        for nb in range(-1, 3):
            iteration(nb, nb)
        with engine.Fori(0, (B - 4) // 2) as it:
            for j in range(2):
                iteration(2 * it + 3 + j, 3 + j)
        for nb in range(B - 1, B + 3):
            iteration(nb, nb)

    def unit_at(b, nb, i):
        if i < 0:
            b, nb, i = b - 1, nb - 1, i + 4
        a = i // 2
        return (a, b - 2 * a, nb - 2 * a, i % 2) if exists(nb - 2 * a) else None

    def unit_before(b, nb, i):
        for back in range(1, 4):
            if unit_at(b, nb, i - back):
                return unit_at(b, nb, i - back)
        return None

    def wait_unit(engine, semaphores, unit):
        if unit:
            a, e, _, u = unit
            engine.wait_ge(semaphores[a], 2 * e + u + 1)

    STACKS = [(0, 0, 2), (1, -2, 0), (1, -2, 1), (1, -2, 2), (0, 1, 0), (0, 1, 1)]
    PROJECTIONS = [(1, -1), (0, 1), (2, -3)]

    def user_before(order, now, b, nb):
        i = order.index(now)
        for back in range(1, 2 * len(order)):
            who = order[(i - back) % len(order)]
            turns = -((i - back) // len(order))
            if exists(nb - turns + who[1]):
                return who, b - turns + who[1]
        return None, None

    flat_gu = [w[:].rearrange("p k u g n -> p (k u g n)") for w in (wgu_hi, wgu_lo)]
    flat_d = [w[:].rearrange("p u k n -> p (u k n)") for w in (wd_hi, wd_lo)]
    n_gu, n_d = KT * 2 * SHARED // B, FT * 2 * D // B
    SHARES = [(flat_gu[0], raw_gu, n_gu), (flat_d[0], raw_d, n_d)]
    LOW_SHARES = [(flat_gu[1], flat_gu[0], raw_gu, n_gu), (flat_d[1], flat_d[0], raw_d, n_d)]

    @block.sync
    def _(sp):
        sp.dma_start(squares[:], a["squares"]).then_inc(squares_loaded, 16)
        sp.dma_start(tokens[:, 0:2], x[0:2].rearrange("b t d -> t b d")).then_inc(x_loaded, 16)
        for w, c0, n in (("wq", 0, D), ("wk", D, KVD), ("wv", D + KVD, KVD)):
            sp.dma_start(raw_qkv[:, :, c0:c0 + n], a[w].rearrange("(k p) n -> p k n", p=P)).then_inc(qkv_loaded, 16)
        sp.dma_start(ctx_sb[:], ctx_512.rearrange("b t d -> t b d")).then_inc(ctx_loaded, 16)
        sp.dma_start(rope[:], a["rope"]).then_inc(consts_loaded, 16)
        sp.dma_start(norm_w[:, 0:D], a["q_norm"].partition_broadcast(P)).then_inc(consts_loaded, 16)
        sp.dma_start(norm_w[:, D:], a["k_norm"].partition_broadcast(P)).then_inc(consts_loaded, 16)
        for i, w in enumerate(("wo", "w_out_t")):
            sp.dma_start(raw_proj[:, i], a[w].rearrange("(k p) n -> p k n", p=P)).then_inc(attn_loaded, 16)
        sp.dma_start(raw_bias[:], a["bo"].partition_broadcast(P)).then_inc(attn_loaded, 16)
        sp.dma_start(raw_router[:], a["router"].rearrange("(k p) n -> p k n", p=P)).then_inc(attn_loaded, 16)
        sp.dma_start(tokens[:, 2:], x[2:].rearrange("b t d -> t b d")).then_inc(rest_loaded, 16)
        sp.dma_start(lane[:], a["lanes"]).then_inc(lane_loaded, 16)
        sp.wait_ge(empty_made, 2)
        sp.dma_start(dispatched.rearrange("(t p) n -> p t n", p=P),
                     empty_rows[:].unsqueeze(1).to_broadcast([P, TILES, ROW])).then_inc(emptied, 16)
        sp.wait_ge(kv_l, 1)
        gu = raw_gu.rearrange("p (k u g n) -> p k u g n", k=KT, u=2, g=2)
        for k in range(KT):
            for g, w in enumerate(("w_gate", "w_up")):
                sp.dma_start(gu[:, k, :, g], a[w][k * P:(k + 1) * P].rearrange("p (u n) -> p u n", u=2)).then_inc(shared_loaded, 16)
        sp.dma_start(raw_d.rearrange("p (k n) -> p k n", n=D), a["w_down"].rearrange("(k p) n -> p k n", p=P)).then_inc(shared_loaded, 16)
        sp.wait_ge(proj_read[2], A_OVER)
        sp.wait_ge(shared_lo, 2 * B)
        sp.dma_start(row_id_sb[:], a["row_ids"]).then_inc(ids_loaded, 16)
        for e in range(EXPERTS):
            sp.dma_start(w1_sb[:, e], a["w1"][e].rearrange("(k p) (g n) -> p k g n", p=P, g=2)).then_inc(experts_loaded, 16)
            sp.dma_start(w2_sb[:, e], a["w2"][e].rearrange("(k p) n -> p k n", p=P)).then_inc(experts_loaded, 16)
        sp.wait_ge(b_added, B_OVER)
        phase_c_sync(sp)
        for u in range(FLIGHT):
            sp.wait_ge(c_stored[u], 16 * (TILES // FLIGHT))
        for c in range(QUARTERS):
            sp.dma_start(products[:, c].rearrange("p b k n -> p b (k n)"), combined.rearrange("(c b p k) n -> c p b (k n)", c=QUARTERS, p=P, k=TOPK)[c]).then_inc(pairs_loaded[c], 16)
        for c in range(QUARTERS):
            sp.wait_ge(pairs_added, TOPK * (c + 1))
            sp.dma_start(out[c * QB:(c + 1) * QB].rearrange("b t d -> t b d"), tokens[:, c * QB:(c + 1) * QB]).then_inc(result_stored, 16)
        sp.wait_ge(result_stored, 16 * QUARTERS)

    def three_products(pe, dst, xh, xl, wh, wl, start, stop):
        pe.matmul(dst, xh, wh, start=start, stop=False)
        pe.matmul(dst, xh, wl, start=False, stop=False)
        return pe.matmul(dst, xl, wh, start=False, stop=stop)

    @block.tensor
    def _(pe):
        def turn(k, src):
            for t in range(KT):
                mm = pe.transpose(ps_actT[:, t], src[:, t * P:(t + 1) * P], identity)
            mm.then_inc(act_turned[k], 1)

        def turn_heads(k, e):
            pe.wait_ge(mixed_done[k - 1], e + 1)
            turn(k, mixed[k - 1][:].rearrange("p h d -> p (h d)"))

        def turn_tokens(e):
            pe.wait_ge(xn_done[0], e + 1)
            turn(0, xn[0])

        def project(k, b, nb):
            now = [p for p in PROJECTIONS if p[0] == k][0]
            before, e_before = user_before(PROJECTIONS, now, b, nb)
            pe.wait_ge(act_lo_done[k], b + now[1] + 1)
            if before:
                pe.wait_ge(proj_read[before[0]], e_before + 1)
            s = k % 2
            if k == 0:
                for t in range(KT):
                    mm = three_products(pe, ps_proj[:, 0:QKV], actT_hi[s][:, t], actT_lo[s][:, t],
                                        wqkv_hi[:, t], wqkv_lo[:, t], t == 0, t == KT - 1)
            else:
                if k == 1:
                    pe.matmul(ps_proj[:, 0:D], first_row[:], bias_hi[:], start=True, stop=False)
                    pe.matmul(ps_proj[:, 0:D], first_row[:], bias_lo[:], start=False, stop=False)
                for t in range(KT):
                    mm = three_products(pe, ps_proj[:, 0:D], actT_hi[s][:, t], actT_lo[s][:, t],
                                        wproj_hi[:, k - 1, t], wproj_lo[:, k - 1, t],
                                        k == 2 and t == 0, t == KT - 1)
            mm.then_inc(projected[k], 1)

        def turn_stack(a, offset, g, b, nb):
            if not exists(nb + offset):
                return
            e = b + offset
            before, e_before = user_before(STACKS, (a, offset, g), b, nb)
            if a == 0 or g > 0:
                pe.wait_ge(parts_l[a], e + 1)
            if before:
                pe.wait_ge(stack_kept[before[0]], 3 * e_before + before[2] + 1)
            first, n = ((HEADS, GROUPS), (0, HALF), (HALF, HALF))[g]
            for h in range(n):
                if a == 0:
                    src = stack[(nb + offset) % 2][:, first + h, 2:BLOCK]
                elif g == 0:
                    src = cross_kv[:, bass.ds(e, 1), h, 2:BLOCK]
                else:
                    src = cross_stack[:, first + h, 2:BLOCK]
                mm = pe.transpose(ps_stack[0:STACK, h], src, ident_bf[:])
            mm.then_inc(stack_turned[a], 1)

        def score(b, nb, i):
            unit = unit_at(b, nb, i)
            if not unit:
                return
            a, e, _, u = unit
            pe.wait_ge(stack_kept[a], 3 * e + u + 2)
            wait_unit(pe, shifted, unit_before(b, nb, i))
            for j in range(2):
                pe.matmul(ps_scores[:, 4 * j:4 * j + 4], ident_bf[:], mask_bf[:], start=True, stop=False,
                          skip_group_check=True)
                for n in range(4):
                    h = HALF * u + 4 * j + n
                    mm = pe.matmul(ps_scores[:, 4 * j + n], qT[a][0:STACK, h], kT[a][0:STACK, h // 4],
                                   start=False, stop=n == 3, skip_group_check=True)
            mm.then_inc(scored[a], 1)

        def turn_probs(b, nb, i):
            unit = unit_at(b, nb, i)
            if not unit:
                return
            a, _, _, u = unit
            wait_unit(pe, exp_done, unit)
            wait_unit(pe, prob_lo_done, unit_before(b, nb, i))
            for n in range(HALF):
                mm = pe.transpose(ps_probs[:, n], prob[u][:, n], identity)
            mm.then_inc(probs_turned[a], 1)

        def mix(b, nb, i):
            unit = unit_at(b, nb, i)
            if not unit:
                return
            a, e, ne, u = unit
            wait_unit(pe, prob_lo_done, unit)
            wait_unit(pe, heads_read, unit_before(b, nb, i))
            for n in range(HALF):
                group = GROUPS + (HALF * u + n) // 4
                v = stack[ne % 2][:, HEADS + group, 1:1 + VCOLS] if a == 0 else cross_kv[:, bass.ds(e, 1), group, 1:1 + VCOLS]
                dst = ps_heads[:, n * VCOLS:(n + 1) * VCOLS]
                pe.matmul(dst, prob_hi[u][:, n], v, start=True, stop=False)
                mm = pe.matmul(dst, prob_lo[u][:, n], v, start=False, stop=True)
            mm.then_inc(heads_done[a], 1)

        def iteration(b, nb):
            if nb == 1:
                pe.wait_ge(lo_made, 4)
            if nb == 2:
                pe.wait_ge(kv_l, 1)
            score(b, nb, 0)
            turn_stack(0, 0, 2, b, nb)
            turn_probs(b, nb, -1)
            if exists(nb - 1):
                turn_heads(1, b - 1)
            mix(b, nb, -2)
            turn_stack(1, -2, 0, b, nb)
            score(b, nb, 1)
            turn_probs(b, nb, 0)
            if exists(nb - 1):
                project(1, b, nb)
            if exists(nb + 1):
                turn_tokens(b + 1)
            mix(b, nb, -1)
            turn_stack(1, -2, 1, b, nb)
            if exists(nb + 1):
                project(0, b, nb)
            score(b, nb, 2)
            turn_probs(b, nb, 1)
            turn_stack(1, -2, 2, b, nb)
            if exists(nb - 3):
                turn_heads(2, b - 3)
            mix(b, nb, 0)
            score(b, nb, 3)
            turn_probs(b, nb, 2)
            if exists(nb - 3):
                project(2, b, nb)
            turn_stack(0, 1, 0, b, nb)
            mix(b, nb, 1)
            turn_stack(0, 1, 1, b, nb)

        pe.wait_ge(squares_loaded, 16)
        pe.wait_ge(lo_made, 1)
        pe.wait_ge(filled, 6)
        pe.wait_ge(filled_act, 3)
        over_iterations(pe, iteration)
        router_tensor(pe)
        phase_b_tensor(pe)
        phase_c_tensor(pe)

    @block.vector
    def _(dve):
        V = nc.vector

        V.memset(minus_half[:], -0.5).then_inc(filled, 1)
        V.memset(empty_rows[:, 0:ROW_ID], 0.0).then_inc(empty_made, 1)
        V.memset(empty_rows[:, ROW_ID:ROW].bitcast(I32), NO_ROW).then_inc(empty_made, 1)
        V.memset(cross_kv[:, :, :, 0:2], 1.0).then_inc(filled, 1)
        for s in range(2):
            V.memset(stack[s][:, :, 0:2], 1.0).then_inc(filled, 1)
        V.memset(rt_hi[:].bitcast(F32), 0.0).then_inc(filled, 1)
        V.memset(rt_lo[:].bitcast(F32), 0.0).then_inc(filled, 1)
        dve.wait_ge(filled, 6)
        dve.wait_ge(hi_made, 1)
        V.tensor_tensor(wqkv_lo[:], raw_qkv[:], wqkv_hi[:].bitcast(F32), ALU.subtract).then_inc(lo_made, 1)

        def ctx_squares():
            dve.wait_ge(ctx_loaded, 16)
            V.tensor_tensor(kv_a[:, :, 0:KVD], ctx_sb[:], ctx_sb[:], ALU.mult).then_inc(kv_step, 1)
            dve.wait_ge(kv_step, 1)
            V.tensor_reduce(k_rstd[:], kv_a[:, :, 0:KVD], AX.X, ALU.add).then_inc(kv_var, 1)

        def rotary_weights():
            dve.wait_ge(consts_loaded, 16 * 3)
            w_view = norm_w[:].rearrange("p (h n) -> p h n", n=HD)
            w_swap = norm_w[:].rearrange("p (h t e) -> p h t e", t=2, e=HD // 2)[:, :, ::-1, :]
            n_heads = HEADS + GROUPS
            V.tensor_tensor(cos_w[:].rearrange("p (h n) -> p h n", n=HD), w_view,
                            rope[:, 0:1, :].to_broadcast([P, n_heads, HD]), ALU.mult).then_inc(kv_step, 1)
            V.tensor_tensor(sin_w[:].rearrange("p (h t e) -> p h t e", t=2, e=HD // 2), w_swap,
                            rope[:, 1:2, :].rearrange("p o (t e) -> p o t e", t=2).to_broadcast([P, n_heads, 2, HD // 2]),
                            ALU.mult).then_inc(kv_step, 1)

        def low_weights():
            dve.wait_ge(hi_made, 4)
            V.tensor_tensor(wproj_lo[:], raw_proj[:], wproj_hi[:].bitcast(F32), ALU.subtract).then_inc(lo_made, 1)
            V.tensor_tensor(bias_lo[:], raw_bias[:], bias_hi[:].bitcast(F32), ALU.subtract).then_inc(lo_made, 1)
            V.tensor_tensor(rt_lo[:, :, 0:EXPERTS], raw_router[:], rt_hi[:, :, 0:EXPERTS].bitcast(F32), ALU.subtract).then_inc(lo_made, 1)

        def ctx_cosines():
            dve.wait_ge(kv_pow, 2)
            dve.wait_ge(kv_step, 3)
            V.tensor_tensor(kv_b[:, :, 0:KVD], ctx_sb[:], k_rstd[:].unsqueeze(2).to_broadcast([P, B, KVD]), ALU.mult).then_inc(kv_step, 1)
            dve.wait_ge(kv_step, 4)
            ck = cos_w[:, D:].unsqueeze(1).to_broadcast([P, B, KVD])
            V.tensor_tensor(kv_a[:, :, 0:KVD], kv_b[:, :, 0:KVD], ck, ALU.mult).then_inc(kv_step, 1)

        def ctx_sines():
            swapped = kv_b[:, :, 0:KVD].rearrange("p b (g t e) -> p b g t e", g=GROUPS, t=2)[:, :, :, ::-1, :]
            for g in range(GROUPS):
                sk = sin_w[:, D + g * HD:D + (g + 1) * HD].rearrange("p (t e) -> p t e", t=2)
                V.tensor_tensor(kv_a[:, :, KVD + g * HD:KVD + (g + 1) * HD].rearrange("p b (t e) -> p b t e", t=2),
                                swapped[:, :, g], sk.unsqueeze(1).to_broadcast([P, B, 2, HD // 2]),
                                ALU.mult).then_inc(kv_step, 1)
            dve.wait_ge(kv_step, 9)
            V.tensor_tensor(kv_fp[:, :, 0:KVD], kv_a[:, :, 0:KVD], kv_a[:, :, KVD:], ALU.add).then_inc(kv_src, 1)

        blocks = cross_kv[:].rearrange("p b g n -> p (b g) n")
        rest = kv_b.rearrange("p b (g n) -> p (b g) n", n=HD)

        def ctx_rest():
            dve.wait_ge(kv_h, 1)
            V.tensor_tensor(rest, kv_fp.rearrange("p b (g n) -> p (b g) n", n=HD), blocks[:, :, 2:2 + HD], ALU.subtract).then_inc(kv_r, 1)

        def ctx_last():
            dve.wait_ge(kv_m, 1)
            V.tensor_tensor(blocks[:, :, 2 + 2 * HD:2 + 3 * HD], rest, blocks[:, :, 2 + HD:2 + 2 * HD], ALU.subtract).then_inc(kv_l, 1)

        def setup_beside(nb, slot):
            if (nb, slot) == (-1, 1):
                ctx_squares()
            elif (nb, slot) == (-1, 3):
                rotary_weights()
                low_weights()
            elif (nb, slot) == (0, 0):
                dve.wait_ge(rest_loaded, 16)
                ctx_cosines()
            elif (nb, slot) == (0, 1):
                ctx_sines()
            elif (nb, slot) == (0, 3):
                ctx_rest()
            elif (nb, slot) == (1, 2):
                ctx_last()

        def norm_stats(a, e):
            V.bn_stats(bstats[:, a], tokens[:, bass.ds(e, 1), :]).then_inc(stats_done[a], 1)

        def norm_moments(a, e):
            wait_alone(dve, stats_done[a], e + 1)
            V.bn_aggr(moments[:, a], bstats[:, a]).then_inc(moments_done[a], 1)

        def normalise(a, e):
            dve.wait_ge(rstd_done[a], e + 1)
            V.tensor_scalar(xn[a][:].unsqueeze(1), tokens[:, bass.ds(e, 1), :], moments[:, a, 0:1], rstd[:, a],
                            ALU.subtract, ALU.mult).then_inc(xn_done[a], 1)

        def act_lo(k, e):
            dve.wait_ge(act_hi_done[k], e + 1)
            V.tensor_tensor(actT_lo[k % 2][:], ps_actT[:, 0:KT], actT_hi[k % 2][:].bitcast(F32), ALU.subtract).then_inc(act_lo_done[k], 1)

        def add_projected(k, e):
            dve.wait_ge(projected[k], e + 1)
            mine = tokens[:, bass.ds(e, 1), :]
            V.tensor_tensor(mine, mine, ps_proj[:, 0:D].unsqueeze(1), ALU.add).then_inc(proj_read[k], 1)

        def take_remainder(e, s):
            dve.wait_ge(parts_h[0], e + 1)
            V.tensor_tensor(remainder[0][:].rearrange("p (h n) -> p h n", n=HD),
                            ps_proj[:, 0:QKV].rearrange("p (h n) -> p h n", n=HD),
                            stack[s][:, :, 2:2 + HD], ALU.subtract).then_inc(proj_read[0], 1)

        def shift(b, nb, i):
            unit = unit_at(b, nb, i)
            if not unit:
                return
            a, _, _, u = unit
            wait_unit(dve, scored, unit)
            V.tensor_reduce(row_max[u][:], ps_scores[:], AX.X, ALU.max).then_inc(max_done[a], 1)
            wait_unit(dve, max_done, unit)
            V.tensor_tensor(prob[u][:], ps_scores[:], row_max[u][:].unsqueeze(2).to_broadcast([P, HALF, P]),
                            ALU.subtract).then_inc(shifted[a], 1)

        def probs_lo(b, nb, i):
            unit = unit_at(b, nb, i)
            if not unit:
                return
            a, _, _, u = unit
            wait_unit(dve, prob_hi_done, unit)
            V.tensor_tensor(prob_lo[u][:], ps_probs[:], prob_hi[u][:], ALU.subtract).then_inc(prob_lo_done[a], 1)

        def sum_parts(b, nb, i):
            unit = unit_at(b, nb, i)
            if not unit:
                return
            a, e, _, u = unit
            wait_unit(dve, heads_done, unit)
            o = ps_heads[:, 0:HALF * VCOLS].rearrange("p (h c) -> p h c", c=VCOLS)
            V.tensor_reduce(heads[a][:, HALF * u:HALF * (u + 1)],
                            o[:, :, 1:].rearrange("p h (c d) -> p h d c", c=3), AX.X, ALU.add).then_inc(heads_summed[a], 1)
            V.reciprocal(denom[a][:, HALF * u:HALF * (u + 1)], o[:, :, 0]).then_inc(heads_read[a], 1)

        def finish_heads(a, e):
            dve.wait_ge(heads_summed[a], 2 * e + 2)
            dve.wait_ge(heads_read[a], 2 * e + 2)
            V.tensor_tensor(mixed[a][:], heads[a][:], denom[a][:].unsqueeze(2).to_broadcast([P, HEADS, HD]),
                            ALU.mult).then_inc(mixed_done[a], 1)

        def iteration(b, nb):
            if exists(nb + 1):
                norm_stats(0, b + 1)
            shift(b, nb, 0)
            if exists(nb + 1):
                norm_moments(0, b + 1)
            probs_lo(b, nb, -1)
            if exists(nb - 1):
                act_lo(1, b - 1)
            sum_parts(b, nb, -2)
            if exists(nb + 1):
                normalise(0, b + 1)
            setup_beside(nb, 0)
            shift(b, nb, 1)
            if exists(nb - 1):
                add_projected(1, b - 1)
            if exists(nb + 1):
                act_lo(0, b + 1)
            if exists(nb - 1):
                wait_alone(dve, proj_read[1], b)
                norm_stats(1, b - 1)
            probs_lo(b, nb, 0)
            if exists(nb - 1):
                norm_moments(1, b - 1)
            sum_parts(b, nb, -1)
            setup_beside(nb, 1)
            shift(b, nb, 2)
            if exists(nb - 3):
                finish_heads(1, b - 3)
            if exists(nb + 1):
                take_remainder(b + 1, (nb + 1) % 2)
            probs_lo(b, nb, 1)
            if exists(nb - 1):
                normalise(1, b - 1)
            sum_parts(b, nb, 0)
            if exists(nb - 3):
                act_lo(2, b - 3)
            setup_beside(nb, 2)
            shift(b, nb, 3)
            probs_lo(b, nb, 2)
            sum_parts(b, nb, 1)
            if exists(nb - 3):
                add_projected(2, b - 3)
            if exists(nb):
                finish_heads(0, b)
            setup_beside(nb, 3)

        dve.wait_ge(x_loaded, 16)
        over_iterations(dve, iteration)
        router_vector(dve)
        phase_b_vector(dve, routing_vector(dve))
        phase_c_vector(dve)

    @block.scalar
    def _(act):
        S = nc.scalar
        act.wait_ge(squares_loaded, 16)
        S.copy(ident_bf[:], identity).then_inc(filled_act, 1)
        S.copy(mask_bf[:], squares[:, 1:2].to_broadcast([P, 4, P])).then_inc(filled_act, 1)
        S.copy(first_row[:], squares[:, 3]).then_inc(filled_act, 1)
        act.wait_ge(qkv_loaded, 16 * 3)
        S.copy(wqkv_hi[:], raw_qkv[:]).then_inc(hi_made, 1)

        def high_weights():
            act.wait_ge(attn_loaded, 16 * 4)
            S.copy(wproj_hi[:], raw_proj[:]).then_inc(hi_made, 1)
            S.copy(bias_hi[:], raw_bias[:]).then_inc(hi_made, 1)
            act.wait_ge(filled, 6)
            S.copy(rt_hi[:, :, 0:EXPERTS], raw_router[:]).then_inc(hi_made, 1)

        fp = kv_fp.rearrange("p b (g n) -> p (b g) n", n=HD)
        rest = kv_b.rearrange("p b (g n) -> p (b g) n", n=HD)
        slots = cross_kv[:].rearrange("p b g n -> p (b g) n")[:, :, 2:].rearrange("p r (c n) -> p r c n", n=HD)
        two = lambda v: v.unsqueeze(2).to_broadcast([P, B * KV, 2, HD])

        def ctx_values():
            act.wait_ge(ctx_loaded, 16)
            S.copy(kv_fp[:, :, KVD:], ctx_sb[:]).then_inc(kv_src, 1)

        def ctx_high():
            act.wait_ge(kv_src, 2)
            S.copy(slots[:, :, 0::3], two(fp))
            S.copy(slots[:, :, 5], fp).then_inc(kv_h, 1)

        def ctx_middle():
            act.wait_ge(kv_r, 1)
            S.copy(slots[:, :, 1::3], two(rest)).then_inc(kv_m, 1)

        def setup_beside(nb, slot):
            if (nb, slot) == (-1, 2):
                high_weights()
                ctx_values()
            elif (nb, slot) == (0, 2):
                ctx_high()
            elif (nb, slot) == (1, 1):
                ctx_middle()

        def act_hi(k, e):
            act.wait_ge(act_turned[k], e + 1)
            S.copy(actT_hi[k % 2][:], ps_actT[:, 0:KT]).then_inc(act_hi_done[k], 1)

        def in_slots(blocks):
            return blocks[:, :, 2:].rearrange("p h (c n) -> p h c n", n=HD)

        def high_parts_self(e, s):
            act.wait_ge(projected[0], e + 1)
            q = ps_proj[:, 0:D].rearrange("p (h n) -> p h n", n=HD)
            kv = ps_proj[:, D:QKV].rearrange("p (h n) -> p h n", n=HD)
            in_kv, in_q = in_slots(stack[s][:, HEADS:]), in_slots(stack[s][:, 0:HEADS])
            S.copy(in_kv[:, :, 0::3], kv.unsqueeze(2).to_broadcast([P, KV, 2, HD]))
            S.copy(in_kv[:, :, 5], kv)
            S.copy(in_q[:, :, 0:3], q.unsqueeze(2).to_broadcast([P, HEADS, 3, HD])).then_inc(parts_h[0], 1)

        def middle_parts_self(e, s):
            act.wait_ge(proj_read[0], e + 1)
            r = remainder[0][:].rearrange("p (h n) -> p h n", n=HD)
            in_kv, in_q = in_slots(stack[s][:, HEADS:]), in_slots(stack[s][:, 0:HEADS])
            S.copy(in_kv[:, :, 1::3], r[:, HEADS:].unsqueeze(2).to_broadcast([P, KV, 2, HD]))
            S.copy(in_q[:, :, 3:5], r[:, 0:HEADS].unsqueeze(2).to_broadcast([P, HEADS, 2, HD])).then_inc(parts_m[0], 1)

        def high_parts_cross(e):
            act.wait_ge(q_done, e + 1)
            q = q_fp[:].rearrange("p (h n) -> p h n", n=HD)
            S.copy(in_slots(cross_stack)[:, :, 0:3], q.unsqueeze(2).to_broadcast([P, HEADS, 3, HD])).then_inc(parts_h[1], 1)

        def middle_parts_cross(e):
            act.wait_ge(q_rest, e + 1)
            r = remainder[1][:, 0:D].rearrange("p (h n) -> p h n", n=HD)
            S.copy(in_slots(cross_stack)[:, :, 3:5], r.unsqueeze(2).to_broadcast([P, HEADS, 2, HD])).then_inc(parts_m[1], 1)

        def keep_stack(a, offset, g, b, nb):
            if not exists(nb + offset):
                return
            act.wait_ge(stack_turned[a], 3 * (b + offset) + g + 1)
            if g == 0:
                S.copy(kT[a][0:STACK], ps_stack[0:STACK, 0:GROUPS]).then_inc(stack_kept[a], 1)
            else:
                S.copy(qT[a][0:STACK, HALF * (g - 1):HALF * g], ps_stack[0:STACK]).then_inc(stack_kept[a], 1)

        def exponentials(b, nb, i):
            unit = unit_at(b, nb, i)
            if not unit:
                return
            a, _, _, u = unit
            wait_unit(act, shifted, unit)
            S.activation(prob[u][:], prob[u][:], ACT.Exp, scale=SCALE).then_inc(exp_done[a], 1)

        def probs_hi(b, nb, i):
            unit = unit_at(b, nb, i)
            if not unit:
                return
            a, _, _, u = unit
            wait_unit(act, probs_turned, unit)
            S.copy(prob_hi[u][:], ps_probs[:]).then_inc(prob_hi_done[a], 1)

        def share(b, nb):
            if nb == 0:
                act.wait_ge(shared_loaded, 16 * 5)
            for hi, src, n in SHARES:
                S.copy(hi[:, bass.ds(n * b, n)], src[:, bass.ds(n * b, n)]).then_inc(shared_hi, 1)

        def iteration(b, nb):
            keep_stack(0, 0, 2, b, nb)
            probs_hi(b, nb, -1)
            if exists(nb - 1):
                act_hi(1, b - 1)
            exponentials(b, nb, 0)
            keep_stack(1, -2, 0, b, nb)
            if exists(nb - 2):
                middle_parts_cross(b - 2)
            if exists(nb - 3):
                share(b - 3, nb - 3)
            setup_beside(nb, 0)
            probs_hi(b, nb, 0)
            if exists(nb + 1):
                act_hi(0, b + 1)
            keep_stack(1, -2, 1, b, nb)
            exponentials(b, nb, 1)
            setup_beside(nb, 1)
            if exists(nb + 1):
                high_parts_self(b + 1, (nb + 1) % 2)
            probs_hi(b, nb, 1)
            keep_stack(1, -2, 2, b, nb)
            exponentials(b, nb, 2)
            if exists(nb - 3):
                act_hi(2, b - 3)
            if exists(nb + 1):
                middle_parts_self(b + 1, (nb + 1) % 2)
            setup_beside(nb, 2)
            keep_stack(0, 1, 0, b, nb)
            probs_hi(b, nb, 2)
            keep_stack(0, 1, 1, b, nb)
            exponentials(b, nb, 3)
            if exists(nb - 1):
                high_parts_cross(b - 1)

        over_iterations(act, iteration)
        router_scalar(act)
        phase_b_scalar(act)
        phase_c_scalar(act)

    @block.gpsimd
    def _(pool):
        G = nc.gpsimd
        pool.wait_ge(filled, 6)

        def ctx_scale():
            pool.wait_ge(kv_var, 1)
            G.tensor_scalar(k_rstd[:], k_rstd[:], 1.0 / KVD, EPS, ALU.mult, ALU.add).then_inc(kv_pow, 1)
            pool.wait_ge(kv_pow, 1)
            G.tensor_tensor(k_rstd[:], k_rstd[:], minus_half[:], ALU.pow).then_inc(kv_pow, 1)

        def norm_scale(a, e, mul, add):
            wait_alone(pool, moments_done[a], e + 1)
            G.tensor_scalar(variance[:, a], moments[:, a, 1:2], mul, add, ALU.mult, ALU.add).then_inc(var_eps[a], 1)
            pool.wait_ge(var_eps[a], e + 1)
            G.tensor_tensor(rstd[:, a], variance[:, a], minus_half[:, 0:1], ALU.pow).then_inc(rstd_done[a], 1)

        def low_parts(a, e, blocks):
            pool.wait_ge(parts_m[a], e + 1)
            r = remainder[a][:].rearrange("p (h n) -> p h n", n=HD)
            if a == 0:
                kv = blocks[:, HEADS:]
                G.tensor_tensor(kv[:, :, 2 + 2 * HD:2 + 3 * HD], r[:, HEADS:], kv[:, :, 2 + 4 * HD:2 + 5 * HD], ALU.subtract)
            q = blocks[:, 0:HEADS]
            G.tensor_tensor(q[:, :, 2 + 5 * HD:2 + 6 * HD], r[:, 0:HEADS], q[:, :, 2 + 4 * HD:2 + 5 * HD], ALU.subtract).then_inc(parts_l[a], 1)

        def rotate(e):
            pool.wait_ge(xn_done[1], e + 1)
            G.tensor_tensor(q_fp[:], xn[1][:], cos_w[:, 0:D], ALU.mult).then_inc(rope_step, 1)
            half = lambda v: v.rearrange("p (h t e) -> p h t e", t=2, e=HD // 2)
            G.tensor_tensor(half(q_sin[:]), half(xn[1][:])[:, :, ::-1, :], half(sin_w[:, 0:D]), ALU.mult).then_inc(rope_step, 1)
            pool.wait_ge(rope_step, 2 * e + 2)
            G.tensor_tensor(q_fp[:], q_fp[:], q_sin[:], ALU.add).then_inc(q_done, 1)

        def rest_of_q(e):
            pool.wait_ge(parts_h[1], e + 1)
            G.tensor_tensor(remainder[1][:, 0:D].rearrange("p (h n) -> p h n", n=HD),
                            q_fp[:].rearrange("p (h n) -> p h n", n=HD),
                            cross_stack[:, :, 2:2 + HD], ALU.subtract).then_inc(q_rest, 1)

        def share(b):
            pool.wait_ge(shared_hi, 2 * b + 2)
            for lo, hi, src, n in LOW_SHARES:
                G.tensor_tensor(lo[:, bass.ds(n * b, n)], src[:, bass.ds(n * b, n)],
                                hi[:, bass.ds(n * b, n)].bitcast(F32), ALU.subtract).then_inc(shared_lo, 1)

        def iteration(b, nb):
            if exists(nb + 1):
                norm_scale(0, b + 1, 1.0, EPS)
            if exists(nb - 2):
                low_parts(1, b - 2, cross_stack)
            if exists(nb - 3):
                share(b - 3)
            if exists(nb - 1):
                norm_scale(1, b - 1, 1.0 + EPS, EPS * EPS)
            if exists(nb + 1):
                low_parts(0, b + 1, stack[(nb + 1) % 2])
            if nb == -1:
                ctx_scale()
            if nb == 1:
                pool.wait_ge(kv_step, 3)
            if exists(nb - 1):
                rotate(b - 1)
                rest_of_q(b - 1)

        over_iterations(pool, iteration)
        router_pool(pool)
        routing_pool(pool)
        phase_c_pool(pool)

    block.__exit__(None, None, None)
    sems.close()
    top.close()


_INS = {"x": "x", "ctx_512": "ctx_512", "wq": "L0_attn_Wq", "wk": "L0_attn_Wk", "wv": "L0_attn_Wv", "wo": "L0_attn_Wo",
        "bo": "L0_attn_bo", "q_norm": "L0_xattn_q_norm_w", "k_norm": "L0_xattn_k_norm_w",
        "w_out_t": "L0_xattn_w_out", "router": "L0_ffn_router_w", "w1": "L0_ffn_w1", "w2": "L0_ffn_w2",
        "w_gate": "L0_ffn_w_gate", "w_up": "L0_ffn_w_up", "w_down": "L0_ffn_w_down"}


def kernel(**inputs):
    import concourse.bacc as bacc
    from concourse.bass_utils import run_bass_kernel_spmd

    arrays = {}
    for name, source in _INS.items():
        w = np.asarray(inputs[source])
        arrays[name] = np.ascontiguousarray(w.T if name == "w_out_t" else w)
    B = arrays["x"].shape[0]
    tiles = B * TOPK + EXPERTS
    arrays["squares"], arrays["rope"], arrays["lanes"], arrays["row_ids"] = constants(B, tiles)
    nc = bacc.Bacc("TRN2", target_bir_lowering=False, num_devices=1)
    aps = {name: nc.dram_tensor(f"in_{name}", v.shape, mybir.dt.from_np(v.dtype), kind="ExternalInput").ap()
           for name, v in arrays.items()}
    out = nc.dram_tensor("out", arrays["x"].shape, F32, kind="ExternalOutput").ap()
    decoder_layer(nc, aps, out)
    ran = run_bass_kernel_spmd(nc, [{f"in_{name}": v for name, v in arrays.items()}], core_ids=[0])
    return ran.results[0]["out"]
```

```python
from contextlib import ExitStack

import numpy as np
import concourse.bass as bass
from concourse import mybir

ALU = mybir.AluOpType
ACT = mybir.ActivationFunctionType
AX = mybir.AxisListType
F32 = mybir.dt.float32
F32R = mybir.dt.float32r
BF16 = mybir.dt.bfloat16
F16 = mybir.dt.float16
I32 = mybir.dt.int32

P = 128
D = 256
HEADS, GROUPS, HD = 16, 4, 16
KVD = GROUPS * HD
QKV = D + 2 * KVD
EPS = 1e-5
SCALE = 1.0 / HD ** 0.5
MASKED = -1e30
EXPERTS, INTER, TOPK = 8, 512, 2
SHARED = 2 * INTER
KT = D // P
FT = INTER // P
FLIGHT = 4
UNITS = SHARED // P
UNITS_IN_FLIGHT = 4
BESIDE_ROUTING = 2

SLOTS = 6
STACK = SLOTS * HD
BLOCK = 2 + STACK
VCOLS = 1 + 3 * HD
KV = 2 * GROUPS
HALF = HEADS // 2

WEIGHT, ROW_ID, ROW = D, D + 1, D + 2

L_PRIORITY = 0
L_FULL = L_PRIORITY + EXPERTS


def constants(B, TILES):
    t = np.arange(P)
    ident = np.eye(P)
    causal = np.where(t[:, None] < t[None, :], MASKED, 0.0)
    earlier = (t[:, None] < t[None, :]) * 1.0
    first = (t[:, None] == 0) * np.ones((1, P))
    squares = np.stack([ident, causal, earlier, first], 1).astype(np.float32)
    freq = np.outer(t.astype(np.float32), (1.0 / 10000.0 ** (np.arange(0, HD, 2, dtype=np.float32) / HD)).astype(np.float32))
    cos = np.concatenate([np.cos(freq), np.cos(freq)], 1)
    sin = np.concatenate([-np.sin(freq), np.sin(freq)], 1)
    rope = np.stack([cos, sin], 1).astype(np.float32)
    row = np.concatenate([
        EXPERTS - np.arange(EXPERTS), 128.0 * np.arange(B), np.arange(TILES),
        np.tile((np.arange(B) > 0) * 1.0, EXPERTS), np.ones(EXPERTS)]).astype(np.float32)
    lanes = np.broadcast_to(row, (P, row.size)).copy()
    token = P * np.arange(B)[None, :] + t[:, None]
    row_ids = (TOPK * token[:, None, :] + np.arange(TOPK)[None, :, None]).astype(np.int32)
    return squares, rope, lanes, row_ids


def decoder_layer(nc, a, out):
    x, ctx_512 = a["x"], a["ctx_512"]
    B = x.shape[0]
    PAIRS = B // 2
    CHOICES = B * P * TOPK
    TILES = CHOICES // P + EXPERTS
    assert TILES % FLIGHT == 0 and B % 2 == 0 and EXPERTS == UNITS
    NO_ROW = CHOICES
    dispatched = nc.dram_tensor("dispatched", (TILES * P, ROW), F32, kind="Internal").ap()
    combined = nc.dram_tensor("combined", (CHOICES, D), F32, kind="Internal").ap()

    L_IOTA = L_FULL + B
    L_CARRY = L_IOTA + TILES
    L_ONES = L_CARRY + EXPERTS * B

    top = ExitStack()

    def maker(scope):
        def sb(name, shape, dt):
            return scope.enter_context(nc.sbuf_tensor(name, shape, dt))
        return sb

    sb = maker(top)
    tokens = sb("tokens", [P, B, D], F32)
    over_shared = [nc.sbuf_base]
    wgu_hi = sb("wgu_hi", [P, KT, 2, 2, INTER], F32R)
    wgu_lo = sb("wgu_lo", [P, KT, 2, 2, INTER], F32R)
    wd_hi = sb("wd_hi", [P, 2, FT, D], F32R)
    wd_lo = sb("wd_lo", [P, 2, FT, D], F32R)
    rt_hi = sb("rt_hi", [P, KT, D], F32R)
    rt_lo = sb("rt_lo", [P, KT, D], F32R)
    squares = sb("squares", [P, 4, P], F32)
    identity, earlier_fp = squares[:, 0], squares[:, 2]
    lane = sb("lane", [P, L_ONES + EXPERTS], F32)
    bstats = sb("bstats", [P, 2, 6], F32)
    moments = sb("moments", [P, 2, 2], F32)
    variance = sb("variance", [P, 2, 1], F32)
    rstd = sb("rstd", [P, 2, 1], F32)
    minus_half = sb("minus_half", [P, B], F32)
    xn = [sb(f"xn{s}", [P, D], F32) for s in range(2)]
    pair_at = nc.sbuf_base
    pair_hi = sb("pair_hi", [P, KT, 2, P], F32R)
    pair_lo = sb("pair_lo", [P, KT, 2, P], F32R)
    actT_hi = [pair_hi[:, :, s] for s in range(2)]
    actT_lo = [pair_lo[:, :, s] for s in range(2)]

    phase_a = ExitStack()
    sb = maker(phase_a)
    wqkv_hi = sb("wqkv_hi", [P, KT, QKV], F32R)
    wqkv_lo = sb("wqkv_lo", [P, KT, QKV], F32R)
    wproj_hi = sb("wproj_hi", [P, 2, KT, D], F32R)
    wproj_lo = sb("wproj_lo", [P, 2, KT, D], F32R)
    bias_hi = sb("bias_hi", [P, D], F32R)
    bias_lo = sb("bias_lo", [P, D], F32R)
    first_row = sb("first_row", [P, P], F32R)
    raw = sb("raw", [P, KT * 2 * SHARED + FT * 2 * D], F32)
    raw_qkv = sb("raw_qkv", [P, KT, QKV], F32)
    raw_proj = sb("raw_proj", [P, 2, KT, D], F32)
    raw_bias = sb("raw_bias", [P, D], F32)
    raw_router = sb("raw_router", [P, KT, EXPERTS], F32)
    mask_bf = sb("mask_bf", [P, 4, P], BF16)
    ident_bf = sb("ident_bf", [P, P], BF16)
    rope = sb("rope", [P, 2, HD], F32)
    norm_w = sb("norm_w", [P, D + KVD], F32)
    cos_w = sb("cos_w", [P, D + KVD], F32)
    sin_w = sb("sin_w", [P, D + KVD], F32)
    cross_kv = sb("cross_kv", [P, B, KV, BLOCK], BF16)
    stack = [sb(f"stack{s}", [P, HEADS + KV, BLOCK], BF16) for s in range(2)]
    remainder = [sb(f"remainder{a}", [P, QKV], F32) for a in range(2)]
    cross_stack = sb("cross_stack", [P, HEADS, BLOCK], BF16)
    q_fp = sb("q_fp", [P, D], F32)
    q_sin = sb("q_sin", [P, D], F32)
    qT = [sb(f"qT{a}", [P, HEADS, P], BF16) for a in range(2)]
    kT = [sb(f"kT{a}", [P, GROUPS, P], BF16) for a in range(2)]
    row_max = [sb(f"row_max{u}", [P, HALF], F32) for u in range(2)]
    prob = [sb(f"prob{u}", [P, HALF, P], F32) for u in range(2)]
    prob_hi = [sb(f"prob_hi{u}", [P, HALF, P], F16) for u in range(2)]
    prob_lo = [sb(f"prob_lo{u}", [P, HALF, P], F16) for u in range(2)]
    heads = [sb(f"heads{a}", [P, HEADS, HD], F32) for a in range(2)]
    denom = [sb(f"denom{a}", [P, HEADS], F32) for a in range(2)]
    mixed = [sb(f"mixed{a}", [P, HEADS, HD], F32) for a in range(2)]
    ctx_sb = sb("ctx_sb", [P, B, KVD], F32)
    k_rstd = sb("k_rstd", [P, B], F32)
    empty_rows = sb("empty_rows", [P, ROW], F32)
    phase_a.close()
    kv_fp = raw[:, 0:B * 2 * KVD].rearrange("p (b n) -> p b n", b=B)
    kv_a = raw[:, B * 2 * KVD:2 * B * 2 * KVD].rearrange("p (b n) -> p b n", b=B)
    kv_b = raw[:, 2 * B * 2 * KVD:3 * B * 2 * KVD].rearrange("p (b n) -> p b n", b=B)
    raw_gu = raw[:, 0:KT * 2 * SHARED]
    raw_d = raw[:, KT * 2 * SHARED:]

    phase_c = ExitStack()
    sb = maker(phase_c)
    rows_at = nc.sbuf_base
    rows = sb("rows", [P, B, ROW], F32)
    w1_at = nc.sbuf_base
    w1_sb = sb("w1_sb", [P, EXPERTS, KT, 2, INTER], F32)
    w2_at = nc.sbuf_base
    w2_sb = sb("w2_sb", [P, EXPERTS, FT, D], F32)
    logits = sb("logits", [P, B, EXPERTS], F32)
    silu_all = sb("silu_all", [P, UNITS_IN_FLIGHT, 2 * P], F32)
    silu = [silu_all[:, 2 * u:2 * u + 2].rearrange("p a n -> p (a n)") for u in range(2)]
    hidden_hi = sb("hidden_hi", [P, UNITS_IN_FLIGHT, 2, P], F32R)
    hidden_lo = sb("hidden_lo", [P, UNITS_IN_FLIGHT, 2, P], F32R)
    best = [sb(f"best{k}", [P, B], F32) for k in range(2)]
    hit = sb("hit", [P, B, EXPERTS], F32)
    pick = [sb(f"pick{k}", [P, B, EXPERTS], F32) for k in range(2)]
    top_priority = sb("top_priority", [P, B], F32)
    masked_logits = sb("masked_logits", [P, B, EXPERTS], F32)
    weight = [sb(f"weight{k}", [P, B], F32) for k in range(2)]
    ratio = sb("ratio", [P, B], F32)
    chosen = sb("chosen", [P, B, EXPERTS], BF16)
    ones_bf = sb("ones_bf", [P, P], BF16)
    earlier_bf = sb("earlier_bf", [P, P], BF16)
    counts = sb("counts", [P, 3, EXPERTS, B], F32)
    upto, begun, place = (counts[:, i] for i in range(3))
    n_tiles = sb("n_tiles", [P, EXPERTS], F32)
    end_tile = sb("end_tile", [P, EXPERTS], F32)
    start_row = sb("start_row", [P, EXPERTS], F32)
    where_fp = [sb(f"where_fp{k}", [P, B], F32) for k in range(2)]
    where = [sb(f"where{k}", [P, B], I32) for k in range(2)]
    assert TILES <= 3 * B
    passed = counts[:].rearrange("p i e b -> p (i e b)")[:, 0:TILES * EXPERTS].rearrange("p (t e) -> p t e", e=EXPERTS)
    tile_expert_fp = sb("tile_expert_fp", [P, TILES], F32)
    tile_expert = sb("tile_expert", [P, TILES], I32)
    row_id_sb = sb("row_id_sb", [P, TOPK, B], I32)
    phase_c.close()

    def over(name, shape, dt):
        words = int(np.prod(shape[1:]))
        t = nc.alloc_sbuf_tensor_at(name, shape, dt, offset=over_shared[0])
        over_shared[0] += -(-words * mybir.dt.size(dt) // 32) * 32
        return t

    w2_hi = over("w2_hi", [P, EXPERTS, FT, D], F32R)
    w1_hi = [over("w1_gate_hi", [P, EXPERTS, INTER], F32R),
             nc.alloc_sbuf_tensor_at("w1_up_hi", [P, EXPERTS, INTER], F32R, offset=rows_at)]
    w1_lo = nc.alloc_sbuf_tensor_at("w1_lo", [P, EXPERTS, KT, 2, INTER], F32R, offset=w1_at)
    w2_lo = nc.alloc_sbuf_tensor_at("w2_lo", [P, EXPERTS, FT, D], F32R, offset=w2_at)
    tile_in = [over(f"tile_in{u}", [P, ROW], F32)[:] for u in range(FLIGHT - 1)]
    tile_in.append(counts[:].rearrange("p i e b -> p (i e b)")[:, 0:ROW])
    tile_out = xn
    xT_whole = nc.alloc_sbuf_tensor_at("xT_whole", [P, 2, P], F32, offset=pair_at)
    xT_fp = [xT_whole[:, v] for v in range(2)]
    xT_hi = [pair_hi[:, 1, v] for v in range(2)]
    xT_lo = [pair_lo[:, 1, v] for v in range(2)]
    hT_hi = [hidden_hi[:, 2 * v:2 * v + 2].rearrange("p a s n -> p (a s) n") for v in range(2)]
    hT_lo = [hidden_lo[:, 2 * v:2 * v + 2].rearrange("p a s n -> p (a s) n") for v in range(2)]
    QUARTERS, QB = 4, B // 4
    products = w1_sb[:].rearrange("p e k g n -> p (e k g n)")[:, 0:B * TOPK * D].rearrange(
        "p (c b k n) -> p c b k n", c=QUARTERS, b=QB, k=TOPK)

    psum_a = ExitStack()
    ps_scores = psum_a.enter_context(nc.psum_tensor("ps_scores", [P, HALF, P], F32))
    ps_probs = psum_a.enter_context(nc.psum_tensor("ps_probs", [P, HALF, P], F32))
    ps_stack = psum_a.enter_context(nc.psum_tensor("ps_stack", [P, HALF, P], BF16))
    ps_heads = psum_a.enter_context(nc.psum_tensor("ps_heads", [P, 512], F32))
    ps_proj = psum_a.enter_context(nc.psum_tensor("ps_proj", [P, 512], F32))
    ps_actT = psum_a.enter_context(nc.psum_tensor("ps_actT", [P, 4, P], F32))
    psum_a.close()
    psum_c = ExitStack()
    ps_gu = [psum_c.enter_context(nc.psum_tensor(f"ps_gu{u}", [P, 2, INTER], F32)) for u in range(2)]
    ps_hT = psum_c.enter_context(nc.psum_tensor("ps_hT", [P, FT, P], F32))
    ps_y = psum_c.enter_context(nc.psum_tensor("ps_y", [P, 512], F32))
    ps_router = psum_c.enter_context(nc.psum_tensor("ps_router", [P, 512], F32))
    ps_xT = psum_c.enter_context(nc.psum_tensor("ps_xT", [P, 4, P], F32))
    psum_c.close()

    sems = ExitStack()

    def sem(name):
        return sems.enter_context(nc.semaphore(name))

    lane_loaded, squares_loaded, x_loaded, rest_loaded, qkv_loaded, consts_loaded, attn_loaded, ctx_loaded, shared_loaded = map(
        sem, ["lane_loaded", "squares_loaded", "x_loaded", "rest_loaded", "qkv_loaded", "consts_loaded", "attn_loaded", "ctx_loaded", "shared_loaded"])
    empty_made, emptied = sem("empty_made"), sem("emptied")
    filled_act, unread = sem("filled_act"), sem("unread")
    filled, hi_made, lo_made, kv_step, kv_var, kv_pow, kv_src, kv_h, kv_r, kv_m, kv_l = map(sem, [
        "filled", "hi_made", "lo_made", "kv_step", "kv_var", "kv_pow", "kv_src", "kv_h", "kv_r", "kv_m", "kv_l"])
    shared_hi, shared_lo, a_ends, b_ends = map(sem, ["shared_hi", "shared_lo", "a_ends", "b_ends"])
    def each(names, n):
        return [[sem(f"{name}{i}") for i in range(n)] for name in names]

    stats_done, moments_done, var_eps, rstd_done, xn_done = each(
        ["stats_done", "moments_done", "var_eps", "rstd_done", "xn_done"], 2)
    act_turned, act_hi_done, act_lo_done, projected, proj_read = each([
        "act_turned", "act_hi_done", "act_lo_done", "projected", "proj_read"], 3)
    parts_h, parts_m, parts_l, stack_turned, stack_kept = each([
        "parts_h", "parts_m", "parts_l", "stack_turned", "stack_kept"], 2)
    q_rest, rope_step, q_done = map(sem, ["q_rest", "rope_step", "q_done"])
    scored, max_done, shifted, exp_done, probs_turned, prob_hi_done, prob_lo_done = each([
        "scored", "max_done", "shifted", "exp_done", "probs_turned", "prob_hi_done", "prob_lo_done"], 2)
    heads_done, heads_summed, heads_read, mixed_done = each([
        "heads_done", "heads_summed", "heads_read", "mixed_done"], 2)

    n_stats, n_moments, n_var, n_rstd, n_xn, n_kept = map(sem, ["n_stats", "n_moments", "n_var", "n_rstd", "n_xn", "n_kept"])
    n_turned, n_hi, n_lo, n_routed, n_logits = map(sem, ["n_turned", "n_hi", "n_lo", "n_routed", "n_logits"])
    b_xn, b_turned, b_hi, b_lo = map(sem, ["b_xn", "b_turned", "b_hi", "b_lo"])
    b_gu, b_silu, b_gated, b_hhi, b_hlo, b_down, b_added = map(
        sem, ["b_gu", "b_silu", "b_gated", "b_hhi", "b_hlo", "b_down", "b_added"])
    ones_made, r_step, r_exp, r_in, r_ranked, r_ready, r_meta, r_placed = map(
        sem, ["ones_made", "r_step", "r_exp", "r_in", "r_ranked", "r_ready", "r_meta", "r_placed"])
    r_sent, experts_loaded, ids_loaded = map(sem, ["r_sent", "experts_loaded", "ids_loaded"])
    c_loaded = [sem(f"c_loaded{u}") for u in range(FLIGHT)]
    c_stored = [sem(f"c_stored{u}") for u in range(FLIGHT)]
    w2_high, w2_low, w_up_hi, w_up_lo, w_hi, w_lo, c_xhi, c_hhi = map(sem, ["w2_high", "w2_low", "w_up_hi", "w_up_lo", "w_hi", "w_lo", "c_xhi", "c_hhi"])
    c_turned, c_kept, c_gu, c_silu, c_gated, c_hturned, c_hkept, c_down, c_scaled = map(sem, [
        "c_turned", "c_kept", "c_gu", "c_silu", "c_gated", "c_hturned", "c_hkept", "c_down", "c_scaled"])
    pairs_loaded = [sem(f"pairs_loaded{c}") for c in range(QUARTERS)]
    pairs_added, result_stored = sem("pairs_added"), sem("result_stored")

    A_OVER = B
    B_OVER = B + 1

    block = nc.Block()
    block.__enter__()

    def wait_alone(engine, semaphore, value):
        engine.wait_ge(semaphore, value)
        engine.sem_inc(unread, 1)

    def over_elements(engine, step, first=0):
        for b in range(first):
            step(b, b % 2, 2)
        with engine.Fori(first // 2, PAIRS - 1) as it:
            for s in range(2):
                step(2 * it + s, s, 2)
        step(B - 2, 0, 1)
        step(B - 1, 1, 0)

    all_stats = silu[0][:, 0:6 * B].rearrange("p (b n) -> p b n", n=6)
    all_moments = silu[0][:, 6 * B:8 * B].rearrange("p (b n) -> p b n", n=2)
    all_rstd = silu[0][:, 8 * B:9 * B]

    ps_rows = [ps_xT, ps_hT]

    def router_tensor(pe):
        def turn(b, s):
            pe.wait_ge(n_xn, b + 1)
            for t in range(KT):
                mm = pe.transpose(ps_rows[s][:, t], xn[s][:, t * P:(t + 1) * P], identity)
            mm.then_inc(n_turned, 1)

        def step(b, s, following):
            if following:
                turn(b + 1, 1 - s)
            pe.wait_ge(n_lo, b + 1)
            pe.wait_ge(n_logits, b + 1)
            for t in range(KT):
                mm = three_products(pe, ps_gu[s][:, 0, 0:D], actT_hi[s][:, t], actT_lo[s][:, t],
                                    rt_hi[:, t], rt_lo[:, t], t == 0, t == KT - 1)
            mm.then_inc(n_routed, 1)

        pe.wait_ge(proj_read[2], A_OVER)
        turn(0, 0)
        over_elements(pe, step)

    def router_scalar(act):
        S = nc.scalar

        def step(b, s, following):
            act.wait_ge(n_turned, b + 1)
            S.copy(actT_hi[s][:], ps_rows[s][:, 0:KT]).then_inc(n_hi, 1)
            S.copy(rows[:, bass.ds(b, 1), 0:D], xn[s][:].unsqueeze(1)).then_inc(n_kept, 1)

        act.wait_ge(proj_read[2], A_OVER)
        over_elements(act, step)

    def router_vector(dve):
        V = nc.vector

        def normalise(b, s):
            V.tensor_scalar(xn[s][:].unsqueeze(1), tokens[:, bass.ds(b, 1), :], all_moments[:, bass.ds(b, 1), 0:1],
                            all_rstd[:, bass.ds(b, 1)], ALU.subtract, ALU.mult).then_inc(n_xn, 1)

        def keep_logits(b, s):
            dve.wait_ge(n_routed, b + 1)
            V.tensor_copy(logits[:, bass.ds(b, 1), :], ps_gu[s][:, 0, 0:EXPERTS].unsqueeze(1)).then_inc(n_logits, 1)

        def step(b, s, following):
            dve.wait_ge(n_hi, b + 1)
            V.tensor_tensor(actT_lo[s][:], ps_rows[s][:, 0:KT], actT_hi[s][:].bitcast(F32), ALU.subtract).then_inc(n_lo, 1)
            if following == 2:
                dve.wait_ge(n_kept, b + 1)
                normalise(b + 2, s)
            if not (isinstance(b, int) and b == 0):
                keep_logits(b - 1, 1 - s)

        dve.nop().then_inc(n_logits, 2)
        dve.wait_ge(proj_read[2], A_OVER)
        for b in range(B):
            V.bn_stats(all_stats[:, b], tokens[:, b]).then_inc(n_stats, 1)
        for b in range(B):
            dve.wait_ge(n_stats, b + 1)
            V.bn_aggr(all_moments[:, b], all_stats[:, b]).then_inc(n_moments, 1)
        dve.wait_ge(n_rstd, 1)
        for b in range(2):
            normalise(b, b)
        over_elements(dve, step, 2)
        keep_logits(B - 1, 1)

    def router_pool(pool):
        G = nc.gpsimd
        pool.wait_ge(n_moments, B)
        G.tensor_scalar(all_rstd, all_moments[:, :, 1], EPS, None, ALU.add).then_inc(n_var, 1)
        pool.wait_ge(n_var, 1)
        G.tensor_tensor(all_rstd, all_rstd, minus_half[:], ALU.pow).then_inc(n_rstd, 1)

    ps_unit = [ps_gu[v // 2][:, v % 2] for v in range(UNITS_IN_FLIGHT)]
    ps_down = [ps_y, ps_hT[:].rearrange("p t n -> p (t n)")]

    def over_pairs(engine, step):
        for p in range(BESIDE_ROUTING):
            step(p, p, True)
        with engine.Fori(BESIDE_ROUTING, PAIRS - 1) as p:
            step(p, None, True)
        step(PAIRS - 1, PAIRS - 1, False)

    def phase_b_tensor(pe):
        def turn(p):
            pe.wait_ge(b_xn, 2 * p + 2)
            for s in range(2):
                for t in range(KT):
                    mm = pe.transpose(ps_xT[:, KT * s + t], xn[s][:, t * P:(t + 1) * P], identity)
            mm.then_inc(b_turned, 1)

        def gate_up(p, j):
            pe.wait_ge(b_lo, p + 1)
            pe.wait_ge(b_gated, UNITS * p + j + 1)
            c, f = divmod(j, FT)
            cols = slice(f * P, (f + 1) * P)
            for g in range(2):
                dst = ps_unit[j % UNITS_IN_FLIGHT][:, g * 2 * P:(g + 1) * 2 * P]
                for t in range(KT):
                    mm = three_products(pe, dst, wgu_hi[:, t, c, g, cols], wgu_lo[:, t, c, g, cols],
                                        pair_hi[:, t], pair_lo[:, t], t == 0, t == KT - 1)
            mm.then_inc(b_gu, 1)

        def down(p, j):
            pe.wait_ge(b_hlo, UNITS * p + j + 1)
            if j == 0:
                pe.wait_ge(b_added, 2 * p + 1)
            c, f = divmod(j, FT)
            v = j % UNITS_IN_FLIGHT
            for s in range(2):
                mm = three_products(pe, ps_down[s][:, 0:D], hidden_hi[:, v, s], hidden_lo[:, v, s],
                                    wd_hi[:, c, f], wd_lo[:, c, f], j == 0, j == UNITS - 1)
            if j == UNITS - 1:
                mm.then_inc(b_down, 1)

        def step(p, known, following):
            for j in range(UNITS - 2):
                gate_up(p, j + 2)
                down(p, j)
                if j == 2 and following:
                    turn(p + 1)
            down(p, UNITS - 2)
            if following:
                gate_up(p + 1, 0)
            down(p, UNITS - 1)
            if following:
                gate_up(p + 1, 1)
            if known == 0:
                routing_tensor(pe)

        pe.wait_ge(shared_lo, 2 * B)
        turn(0)
        gate_up(0, 0)
        gate_up(0, 1)
        over_pairs(pe, step)

    def phase_b_scalar(act):
        S = nc.scalar

        def take_rows(p):
            for s in range(2):
                S.copy(xn[s][:].unsqueeze(1), rows[:, bass.ds(2 * p + s, 1), 0:D]).then_inc(b_xn, 1)

        def act_hi(p):
            act.wait_ge(b_turned, p + 1)
            S.copy(pair_hi[:].rearrange("p t s n -> p s t n"), ps_xT[:].rearrange("p (s t) n -> p s t n", s=2)).then_inc(b_hi, 1)

        def gate(p, j):
            v = j % UNITS_IN_FLIGHT
            act.wait_ge(b_gu, UNITS * p + j + 1)
            S.activation(silu_all[:, v], ps_unit[v][:, 0:2 * P], ACT.Silu).then_inc(b_silu, 1)

        def keep_hi(p, j):
            v = j % UNITS_IN_FLIGHT
            act.wait_ge(b_gated, UNITS * p + j + UNITS_IN_FLIGHT + 1)
            S.copy(hidden_hi[:, v].rearrange("p s n -> p (s n)"), silu_all[:, v]).then_inc(b_hhi, 1)

        def step(p, known, following):
            for j in range(UNITS):
                if j == UNITS - 1 and following:
                    act.wait_ge(b_gu, UNITS * p + UNITS)
                    act_hi(p + 1)
                gate(p, j)
                keep_hi(p, j)
                if not following:
                    act.wait_ge(r_sent, 16 * B * TOPK)
                    act.wait_ge(experts_loaded, 16 * 2 * EXPERTS)
                    split_up_hi(act, j)
                if j == 0 and following:
                    take_rows(p + 1)
                if known == 1 and j == 0:
                    routing_scalar(act)

        act.wait_ge(n_kept, B)
        take_rows(0)
        act.wait_ge(n_routed, B)
        act_hi(0)
        over_pairs(act, step)

    def phase_b_vector(dve, routing):
        V = nc.vector

        def act_lo(p):
            dve.wait_ge(b_hi, p + 1)
            V.tensor_tensor(pair_lo[:].rearrange("p t s n -> p s t n"), ps_xT[:].rearrange("p (s t) n -> p s t n", s=2),
                            pair_hi[:].bitcast(F32).rearrange("p t s n -> p s t n"), ALU.subtract).then_inc(b_lo, 1)

        def gated(p, j):
            v = j % UNITS_IN_FLIGHT
            dve.wait_ge(b_silu, UNITS * p + j + 1)
            V.tensor_tensor(silu_all[:, v], silu_all[:, v], ps_unit[v][:, 2 * P:4 * P], ALU.mult).then_inc(b_gated, 1)

        def keep_lo(p, j):
            v = j % UNITS_IN_FLIGHT
            dve.wait_ge(b_hhi, UNITS * p + j + 1)
            V.tensor_tensor(hidden_lo[:, v].rearrange("p s n -> p (s n)"), silu_all[:, v],
                            hidden_hi[:, v].bitcast(F32).rearrange("p s n -> p (s n)"), ALU.subtract).then_inc(b_hlo, 1)

        def add(p):
            dve.wait_ge(b_down, p + 1)
            for s in range(2):
                mine = tokens[:, bass.ds(2 * p + s, 1), :]
                V.tensor_tensor(mine, mine, ps_down[s][:, 0:D].unsqueeze(1), ALU.add).then_inc(b_added, 1)

        def step(p, known, following):
            for j in range(UNITS):
                if j == UNITS - 1 and following:
                    act_lo(p + 1)
                gated(p, j)
                keep_lo(p, j)
                if not following:
                    split_up_lo(dve, j)
                if j == 0 and known != 0:
                    add(p - 1)
                if known is not None and following:
                    routing(known, j)

        for credit, n in ((b_gated, UNITS_IN_FLIGHT), (b_added, 1)):
            dve.nop().then_inc(credit, n)
        act_lo(0)
        over_pairs(dve, step)
        add(PAIRS - 1)

    def routing_vector(dve):
        V = nc.vector
        done = 0

        def then(ins):
            nonlocal done
            ins.then_inc(r_step, 1)
            done += 1
            dve.wait_ge(r_step, done)

        def over_experts(v):
            return v.unsqueeze(2).to_broadcast([P, B, EXPERTS])

        priority = lane[:, L_PRIORITY:L_FULL].unsqueeze(1).to_broadcast([P, B, EXPERTS])

        def choose(k, step):
            source = masked_logits if k else logits
            if step == 0 and k == 0:
                dve.wait_ge(n_logits, B + 2)
                dve.wait_ge(lane_loaded, 16)
                V.memset(ones_bf[:], 1.0).then_inc(ones_made, 1)
                then(V.tensor_copy(earlier_bf[:], earlier_fp))
            elif step == 0:
                then(V.scalar_tensor_tensor(masked_logits[:], pick[0][:], -3e38, logits[:], ALU.mult, ALU.add))
            if step == 0:
                then(V.tensor_reduce(best[k][:], source[:], AX.X, ALU.max))
            elif step == 1:
                then(V.tensor_tensor(hit[:], source[:], over_experts(best[k][:]), ALU.is_ge))
                then(V.tensor_tensor(hit[:], hit[:], priority, ALU.mult))
            else:
                then(V.tensor_reduce(top_priority[:], hit[:], AX.X, ALU.max))
                then(V.tensor_tensor(pick[k][:], hit[:], over_experts(top_priority[:]), ALU.is_ge))
            if step == 2 and k == 1:
                then(V.tensor_tensor(ratio[:], best[1][:], best[0][:], ALU.subtract))
                V.tensor_tensor(chosen[:], pick[0][:], pick[1][:], ALU.add).then_inc(r_in, 1)

        ranks = ps_router[:, 0:B * EXPERTS].rearrange("p (b e) -> p e b", e=EXPERTS)
        totals = ps_router[:, B * EXPERTS:2 * B * EXPERTS].rearrange("p (b e) -> p e b", e=EXPERTS)
        flat = lambda v: v.rearrange("p e b -> p (e b)")
        full = lane[:, L_FULL:L_IOTA].unsqueeze(1).to_broadcast([P, EXPERTS, B])

        def weights_and_counts():
            dve.wait_ge(r_exp, 1)
            then(V.tensor_scalar(weight[0][:], ratio[:], 1.0, None, ALU.add))
            then(V.reciprocal(weight[0][:], weight[0][:]))
            then(V.tensor_tensor(weight[1][:], ratio[:], weight[0][:], ALU.mult))
            dve.wait_ge(r_ranked, 1)
            then(V.tensor_copy(place, totals))
            then(V.tensor_tensor_scan(flat(upto), lane[:, L_CARRY:L_ONES], flat(place), 0.0, ALU.mult, ALU.add))

        def tiles_of_experts():
            then(V.tensor_tensor(begun, upto[:, :, B - 1:B].to_broadcast([P, EXPERTS, B]), full, ALU.is_gt))
            then(V.tensor_reduce(n_tiles[:], begun, AX.X, ALU.add))
            then(V.tensor_scalar(n_tiles[:], n_tiles[:], 1.0, None, ALU.max))
            then(V.tensor_tensor_scan(end_tile[:], lane[:, L_ONES:], n_tiles[:], 0.0, ALU.mult, ALU.add))
            then(V.tensor_tensor(start_row[:], end_tile[:], n_tiles[:], ALU.subtract))
            then(V.tensor_scalar(start_row[:], start_row[:], float(P), None, ALU.mult))

        def places():
            then(V.tensor_tensor(place, upto, place, ALU.subtract))
            then(V.tensor_tensor(place, place, ranks, ALU.add))
            then(V.tensor_tensor(place, place, start_row[:].unsqueeze(2).to_broadcast([P, EXPERTS, B]), ALU.add))

        def places_of_choice(k):
            then(V.tensor_tensor(hit[:], pick[k][:], place.rearrange("p e b -> p b e"), ALU.mult))
            then(V.tensor_reduce(where_fp[k][:], hit[:], AX.X, ALU.add))
            V.tensor_copy(where[k][:], where_fp[k][:]).then_inc(r_placed, 1)

        def expert_of_tiles():
            ends = end_tile[:].unsqueeze(1).to_broadcast([P, TILES, EXPERTS])
            tiles = lane[:, L_IOTA:L_CARRY].unsqueeze(2).to_broadcast([P, TILES, EXPERTS])
            then(V.tensor_tensor(passed, ends, tiles, ALU.is_le))
            then(V.tensor_reduce(tile_expert_fp[:], passed, AX.X, ALU.add))
            then(V.tensor_scalar(tile_expert_fp[:], tile_expert_fp[:], float(EXPERTS - 1), None, ALU.min))
            V.tensor_copy(tile_expert[:], tile_expert_fp[:]).then_inc(r_ready, 1)

        def routing(p, j):
            for k in range(TOPK):
                for step in range(3):
                    if (p, j) == (0, 1 + 3 * k + step):
                        choose(k, step)
            if (p, j) == (1, 2):
                weights_and_counts()
            elif (p, j) == (1, 3):
                tiles_of_experts()
            elif (p, j) == (1, 4):
                places()
            elif (p, j) == (1, 5):
                places_of_choice(0)
            elif (p, j) == (1, 6):
                places_of_choice(1)
            elif (p, j) == (1, 7):
                expert_of_tiles()

        return routing

    def routing_tensor(pe):
        pe.wait_ge(r_in, 1)
        m = chosen[:].rearrange("p b e -> p (b e)")
        pe.matmul(ps_router[:, 0:B * EXPERTS], earlier_bf[:], m, start=True, stop=True)
        pe.matmul(ps_router[:, B * EXPERTS:2 * B * EXPERTS], ones_bf[:], m, start=True, stop=True).then_inc(r_ranked, 1)

    def routing_scalar(act):
        act.wait_ge(r_step, 13)
        nc.scalar.activation(ratio[:], ratio[:], ACT.Exp).then_inc(r_exp, 1)

    def routing_pool(pool):
        G = nc.gpsimd
        pool.wait_ge(emptied, 16)
        pool.wait_ge(ids_loaded, 16)
        pool.wait_ge(n_kept, B)
        for k in range(TOPK):
            pool.wait_ge(r_placed, k + 1)
            if k > 0:
                pool.wait_ge(r_sent, 16 * B)
            G.tensor_copy(rows[:, :, WEIGHT], weight[k][:])
            G.tensor_copy(rows[:, :, ROW_ID].bitcast(I32), row_id_sb[:, k]).then_inc(r_meta, 1)
            pool.wait_ge(r_meta, k + 1)
            for b in range(B):
                pool.indirect_dma_start(dispatched, bass.IndirectOffsetOnAxis(ap=where[k][:, b:b + 1], axis=0),
                                        rows[:, b], None, bounds_check=TILES * P - 1, oob_is_err=False).then_inc(r_sent, 16)

    def over_tiles(engine, step):
        first = FLIGHT * (-(-EXPERTS // FLIGHT))
        for i in range(first):
            step(i, i % FLIGHT, i // FLIGHT, 2)
        with engine.Fori(first // FLIGHT, TILES // FLIGHT - 1) as it:
            for u in range(FLIGHT):
                step(FLIGHT * it + u, u, it, 2)
        for u in range(FLIGHT):
            step(TILES - FLIGHT + u, u, TILES // FLIGHT - 1, min(2, FLIGHT - 1 - u))

    def split_up_hi(act, e):
        nc.scalar.copy(w1_hi[1][:, e], w1_sb[:, e, 1, 1]).then_inc(w_up_hi, 1)

    def split_up_lo(dve, e):
        dve.wait_ge(w_up_hi, e + 1)
        nc.vector.tensor_tensor(w1_lo[:, e, 1, 1], w1_sb[:, e, 1, 1], w1_hi[1][:, e].bitcast(F32), ALU.subtract).then_inc(w_up_lo, 1)

    def split_hi(act, e):
        nc.scalar.copy(w2_hi[:, e], w2_sb[:, e]).then_inc(w2_high, 1)
        if e == 0:
            act.wait_ge(b_down, PAIRS)
        nc.scalar.copy(w1_hi[0][:, e], w1_sb[:, e, 1, 0]).then_inc(w_hi, 1)

    def split_lo(dve, e):
        dve.wait_ge(w2_high, e + 1)
        nc.vector.tensor_tensor(w2_lo[:, e], w2_sb[:, e], w2_hi[:, e].bitcast(F32), ALU.subtract).then_inc(w2_low, 1)
        dve.wait_ge(w_hi, e + 1)
        nc.vector.tensor_tensor(w1_lo[:, e, 1, 0], w1_sb[:, e, 1, 0], w1_hi[0][:, e].bitcast(F32), ALU.subtract).then_inc(w_lo, 1)

    def phase_c_sync(sp):
        sp.wait_ge(r_sent, 16 * B * TOPK)
        sp.wait_ge(r_ready, 1)
        sp.wait_ge(n_routed, B)
        for u in range(FLIGHT):
            sp.dma_start(tile_in[u], dispatched[u * P:(u + 1) * P, :]).then_inc(c_loaded[u], 16)
        with sp.Fori(1, TILES // FLIGHT) as it:
            for u in range(FLIGHT):
                sp.wait_ge(c_stored[u], 16 * it)
                sp.dma_start(tile_in[u], dispatched[bass.ds((FLIGHT * it + u) * P, P), :]).then_inc(c_loaded[u], 16)

    def phase_c_tensor(pe):
        def turn(i, u, loads):
            pe.wait_ge(c_loaded[u], 16 * loads)
            pe.wait_ge(c_kept, i + 1)
            for t in range(KT):
                mm = pe.transpose(ps_xT[:, t], tile_in[u][:, t * P:(t + 1) * P], identity)
            mm.then_inc(c_turned, 1)

        def gate_up(i, u, e):
            v = u % 2
            pe.wait_ge(c_kept, i + 2)
            pe.wait_ge(c_gated, i + 1)
            if isinstance(i, int) and i < EXPERTS:
                pe.wait_ge(w_lo, i + 1)
                pe.wait_ge(w2_low, i + 1)
            expert = bass.ds(e, 1)
            for g in range(2):
                three_products(pe, ps_gu[v][:, g], xT_hi[v], xT_lo[v],
                               w1_hi[g][:, expert], w1_lo[:, expert, 1, g], True, False)
            for g in range(2):
                mm = pe.matmul(ps_gu[v][:, g], xT_fp[v], w1_sb[:, expert, 0, g], start=False, stop=True)
            mm.then_inc(c_gu, 1)

        def turn_hidden(i, u):
            v = u % 2
            pe.wait_ge(c_gated, i + 3)
            pe.wait_ge(c_hkept, i + 1)
            for t in range(FT):
                mm = pe.transpose(ps_hT[:, t], silu[v][:, t * P:(t + 1) * P], identity)
            mm.then_inc(c_hturned, 1)

        def down(i, u, e):
            v = u % 2
            pe.wait_ge(c_hkept, i + 2)
            pe.wait_ge(c_scaled, i + 1)
            for t in range(FT):
                mm = three_products(pe, ps_y[:, 0:D], hT_hi[v][:, t], hT_lo[v][:, t], w2_hi[:, bass.ds(e, 1), t],
                                    w2_lo[:, bass.ds(e, 1), t], t == 0, t == FT - 1)
            mm.then_inc(c_down, 1)

        def expert_of(i):
            return pe.value_load(tile_expert[0:1, bass.ds(i, 1)], min_val=0, max_val=EXPERTS - 1)

        def step(i, u, r, following):
            if u == 0:
                experts[:] = [expert_of(i), expert_of(i + 1)]
            mine = experts.pop(0)
            turn_hidden(i, u)
            if following:
                gate_up(i + 1, u + 1, experts[0])
            if u < FLIGHT - 1 and following == 2:
                experts.append(expert_of(i + 2))
            if following == 2:
                turn(i + 2, (u + 2) % FLIGHT, r + (u + 2) // FLIGHT + 1)
            down(i, u, mine)

        pe.wait_ge(r_ready, 1)
        pe.wait_ge(experts_loaded, 16 * 2 * EXPERTS)
        pe.wait_ge(w_up_lo, EXPERTS)
        experts = [expert_of(0)]
        turn(0, 0, 1)
        gate_up(0, 0, experts[0])
        turn(1, 1, 1)
        over_tiles(pe, step)

    def phase_c_scalar(act):
        S = nc.scalar

        def gate(i, u):
            act.wait_ge(c_gu, i + 1)
            S.activation(silu[u % 2][:], ps_gu[u % 2][:, 0], ACT.Silu).then_inc(c_silu, 1)

        def keep_x(i, u):
            act.wait_ge(c_turned, i + 1)
            S.copy(xT_fp[u % 2], ps_xT[:, 0])
            S.copy(xT_hi[u % 2], ps_xT[:, 1]).then_inc(c_xhi, 1)

        def h_hi(i, u):
            act.wait_ge(c_hturned, i + 1)
            S.copy(hT_hi[u % 2], ps_hT[:]).then_inc(c_hhi, 1)

        def step(i, u, r, following):
            if following:
                gate(i + 1, u + 1)
            if following == 2:
                keep_x(i + 2, u)
            if following:
                h_hi(i + 1, u + 1)
            if isinstance(i, int) and i + 3 < EXPERTS:
                split_hi(act, i + 3)

        act.wait_ge(b_gu, UNITS * PAIRS)
        split_hi(act, 0)
        keep_x(0, 0)
        split_hi(act, 1)
        split_hi(act, 2)
        gate(0, 0)
        keep_x(1, 1)
        h_hi(0, 0)
        over_tiles(act, step)

    def phase_c_vector(dve):
        V = nc.vector
        for credit, n in ((c_kept, 1), (c_hkept, 1), (c_gated, 2), (c_scaled, 1)):
            dve.nop().then_inc(credit, n)

        def keep_x(i, u):
            dve.wait_ge(c_xhi, i + 1)
            V.tensor_tensor(xT_lo[u % 2], ps_xT[:, 1], xT_hi[u % 2].bitcast(F32), ALU.subtract).then_inc(c_kept, 1)

        def gated(i, u):
            dve.wait_ge(c_silu, i + 1)
            V.tensor_tensor(silu[u % 2][:], silu[u % 2][:], ps_gu[u % 2][:, 1], ALU.mult).then_inc(c_gated, 1)

        def keep_h(i, u):
            dve.wait_ge(c_hhi, i + 1)
            V.tensor_tensor(hT_lo[u % 2], ps_hT[:], hT_hi[u % 2].bitcast(F32), ALU.subtract).then_inc(c_hkept, 1)

        def scale(i, u, r):
            dve.wait_ge(c_down, i + 1)
            if not (isinstance(i, int) and i < 2):
                dve.wait_ge(c_stored[(u + 2) % FLIGHT], 16 * (r + u // 2))
            V.tensor_scalar(tile_out[u % 2][:], ps_y[:, 0:D], tile_in[u][:, WEIGHT:WEIGHT + 1], None, ALU.mult).then_inc(c_scaled, 1)

        def step(i, u, r, following):
            keep_h(i, u)
            if isinstance(i, int) and i + 2 < EXPERTS:
                split_lo(dve, i + 2)
            if following:
                gated(i + 1, u + 1)
            if following == 2:
                keep_x(i + 2, u + 2)
            scale(i, u, r)

        split_lo(dve, 0)
        keep_x(0, 0)
        split_lo(dve, 1)
        gated(0, 0)
        keep_x(1, 1)
        over_tiles(dve, step)
        for c in range(QUARTERS):
            dve.wait_ge(pairs_loaded[c], 16)
            for k in range(TOPK):
                mine = tokens[:, c * QB:(c + 1) * QB]
                V.tensor_tensor(mine, mine, products[:, c, :, k], ALU.add).then_inc(pairs_added, 1)
                dve.wait_ge(pairs_added, TOPK * c + k + 1)

    def phase_c_pool(pool):
        last_row = pool.to_reg(CHOICES - 1)
        with pool.Fori(0, TILES // FLIGHT) as it:
            for u in range(FLIGHT):
                wait_alone(pool, c_scaled, FLIGHT * it + u + 2)
                pool.indirect_dma_start(combined, bass.IndirectOffsetOnAxis(ap=tile_in[u][:, ROW_ID:ROW].bitcast(I32), axis=0),
                                        tile_out[u % 2][:], None, bounds_check=last_row, oob_is_err=False).then_inc(c_stored[u], 16)

    def exists(element):
        return 0 <= element < B

    def over_iterations(engine, iteration):
        for nb in range(-1, 3):
            iteration(nb, nb)
        with engine.Fori(0, (B - 4) // 2) as it:
            for j in range(2):
                iteration(2 * it + 3 + j, 3 + j)
        for nb in range(B - 1, B + 3):
            iteration(nb, nb)

    def unit_at(b, nb, i):
        if i < 0:
            b, nb, i = b - 1, nb - 1, i + 4
        a = i // 2
        return (a, b - 2 * a, nb - 2 * a, i % 2) if exists(nb - 2 * a) else None

    def unit_before(b, nb, i):
        for back in range(1, 4):
            if unit_at(b, nb, i - back):
                return unit_at(b, nb, i - back)
        return None

    def wait_unit(engine, semaphores, unit):
        if unit:
            a, e, _, u = unit
            engine.wait_ge(semaphores[a], 2 * e + u + 1)

    STACKS = [(0, 0, 2), (1, -2, 0), (1, -2, 1), (1, -2, 2), (0, 1, 0), (0, 1, 1)]
    PROJECTIONS = [(1, -1), (0, 1), (2, -3)]

    def user_before(order, now, b, nb):
        i = order.index(now)
        for back in range(1, 2 * len(order)):
            who = order[(i - back) % len(order)]
            turns = -((i - back) // len(order))
            if exists(nb - turns + who[1]):
                return who, b - turns + who[1]
        return None, None

    flat_gu = [w[:].rearrange("p k u g n -> p (k u g n)") for w in (wgu_hi, wgu_lo)]
    flat_d = [w[:].rearrange("p u k n -> p (u k n)") for w in (wd_hi, wd_lo)]
    n_gu, n_d = KT * 2 * SHARED // B, FT * 2 * D // B
    SHARES = [(flat_gu[0], raw_gu, n_gu), (flat_d[0], raw_d, n_d)]
    LOW_SHARES = [(flat_gu[1], flat_gu[0], raw_gu, n_gu), (flat_d[1], flat_d[0], raw_d, n_d)]

    @block.sync
    def _(sp):
        sp.dma_start(squares[:], a["squares"]).then_inc(squares_loaded, 16)
        sp.dma_start(tokens[:, 0:2], x[0:2].rearrange("b t d -> t b d")).then_inc(x_loaded, 16)
        for w, c0, n in (("wq", 0, D), ("wk", D, KVD), ("wv", D + KVD, KVD)):
            sp.dma_start(raw_qkv[:, :, c0:c0 + n], a[w].rearrange("(k p) n -> p k n", p=P)).then_inc(qkv_loaded, 16)
        sp.dma_start(ctx_sb[:], ctx_512.rearrange("b t d -> t b d")).then_inc(ctx_loaded, 16)
        sp.dma_start(rope[:], a["rope"]).then_inc(consts_loaded, 16)
        sp.dma_start(norm_w[:, 0:D], a["q_norm"].partition_broadcast(P)).then_inc(consts_loaded, 16)
        sp.dma_start(norm_w[:, D:], a["k_norm"].partition_broadcast(P)).then_inc(consts_loaded, 16)
        for i, w in enumerate(("wo", "w_out_t")):
            sp.dma_start(raw_proj[:, i], a[w].rearrange("(k p) n -> p k n", p=P)).then_inc(attn_loaded, 16)
        sp.dma_start(raw_bias[:], a["bo"].partition_broadcast(P)).then_inc(attn_loaded, 16)
        sp.dma_start(raw_router[:], a["router"].rearrange("(k p) n -> p k n", p=P)).then_inc(attn_loaded, 16)
        sp.dma_start(tokens[:, 2:], x[2:].rearrange("b t d -> t b d")).then_inc(rest_loaded, 16)
        sp.dma_start(lane[:], a["lanes"]).then_inc(lane_loaded, 16)
        sp.wait_ge(empty_made, 2)
        sp.dma_start(dispatched.rearrange("(t p) n -> p t n", p=P),
                     empty_rows[:].unsqueeze(1).to_broadcast([P, TILES, ROW])).then_inc(emptied, 16)
        sp.wait_ge(kv_l, 1)
        gu = raw_gu.rearrange("p (k u g n) -> p k u g n", k=KT, u=2, g=2)
        for k in range(KT):
            for g, w in enumerate(("w_gate", "w_up")):
                sp.dma_start(gu[:, k, :, g], a[w][k * P:(k + 1) * P].rearrange("p (u n) -> p u n", u=2)).then_inc(shared_loaded, 16)
        sp.dma_start(raw_d.rearrange("p (k n) -> p k n", n=D), a["w_down"].rearrange("(k p) n -> p k n", p=P)).then_inc(shared_loaded, 16)
        sp.wait_ge(proj_read[2], A_OVER)
        sp.wait_ge(shared_lo, 2 * B)
        sp.dma_start(row_id_sb[:], a["row_ids"]).then_inc(ids_loaded, 16)
        for e in range(EXPERTS):
            sp.dma_start(w1_sb[:, e], a["w1"][e].rearrange("(k p) (g n) -> p k g n", p=P, g=2)).then_inc(experts_loaded, 16)
            sp.dma_start(w2_sb[:, e], a["w2"][e].rearrange("(k p) n -> p k n", p=P)).then_inc(experts_loaded, 16)
        phase_c_sync(sp)
        for u in range(FLIGHT):
            sp.wait_ge(c_stored[u], 16 * (TILES // FLIGHT))
        for c in range(QUARTERS):
            sp.dma_start(products[:, c].rearrange("p b k n -> p b (k n)"), combined.rearrange("(c b p k) n -> c p b (k n)", c=QUARTERS, p=P, k=TOPK)[c]).then_inc(pairs_loaded[c], 16)
        for c in range(QUARTERS):
            sp.wait_ge(pairs_added, TOPK * (c + 1))
            sp.dma_start(out[c * QB:(c + 1) * QB].rearrange("b t d -> t b d"), tokens[:, c * QB:(c + 1) * QB]).then_inc(result_stored, 16)
        sp.wait_ge(result_stored, 16 * QUARTERS)

    def three_products(pe, dst, xh, xl, wh, wl, start, stop):
        pe.matmul(dst, xh, wh, start=start, stop=False)
        pe.matmul(dst, xh, wl, start=False, stop=False)
        return pe.matmul(dst, xl, wh, start=False, stop=stop)

    @block.tensor
    def _(pe):
        def turn(k, src):
            for t in range(KT):
                mm = pe.transpose(ps_actT[:, t], src[:, t * P:(t + 1) * P], identity)
            mm.then_inc(act_turned[k], 1)

        def turn_heads(k, e):
            pe.wait_ge(mixed_done[k - 1], e + 1)
            turn(k, mixed[k - 1][:].rearrange("p h d -> p (h d)"))

        def turn_tokens(e):
            pe.wait_ge(xn_done[0], e + 1)
            turn(0, xn[0])

        def project(k, b, nb):
            now = [p for p in PROJECTIONS if p[0] == k][0]
            before, e_before = user_before(PROJECTIONS, now, b, nb)
            pe.wait_ge(act_lo_done[k], b + now[1] + 1)
            if before:
                pe.wait_ge(proj_read[before[0]], e_before + 1)
            s = k % 2
            if k == 0:
                for t in range(KT):
                    mm = three_products(pe, ps_proj[:, 0:QKV], actT_hi[s][:, t], actT_lo[s][:, t],
                                        wqkv_hi[:, t], wqkv_lo[:, t], t == 0, t == KT - 1)
            else:
                if k == 1:
                    pe.matmul(ps_proj[:, 0:D], first_row[:], bias_hi[:], start=True, stop=False)
                    pe.matmul(ps_proj[:, 0:D], first_row[:], bias_lo[:], start=False, stop=False)
                for t in range(KT):
                    mm = three_products(pe, ps_proj[:, 0:D], actT_hi[s][:, t], actT_lo[s][:, t],
                                        wproj_hi[:, k - 1, t], wproj_lo[:, k - 1, t],
                                        k == 2 and t == 0, t == KT - 1)
            mm.then_inc(projected[k], 1)

        def turn_stack(a, offset, g, b, nb):
            if not exists(nb + offset):
                return
            e = b + offset
            before, e_before = user_before(STACKS, (a, offset, g), b, nb)
            if a == 0 or g > 0:
                pe.wait_ge(parts_l[a], e + 1)
            if before:
                pe.wait_ge(stack_kept[before[0]], 3 * e_before + before[2] + 1)
            first, n = ((HEADS, GROUPS), (0, HALF), (HALF, HALF))[g]
            for h in range(n):
                if a == 0:
                    src = stack[(nb + offset) % 2][:, first + h, 2:BLOCK]
                elif g == 0:
                    src = cross_kv[:, bass.ds(e, 1), h, 2:BLOCK]
                else:
                    src = cross_stack[:, first + h, 2:BLOCK]
                mm = pe.transpose(ps_stack[0:STACK, h], src, ident_bf[:])
            mm.then_inc(stack_turned[a], 1)

        def score(b, nb, i):
            unit = unit_at(b, nb, i)
            if not unit:
                return
            a, e, _, u = unit
            pe.wait_ge(stack_kept[a], 3 * e + u + 2)
            wait_unit(pe, shifted, unit_before(b, nb, i))
            for j in range(2):
                pe.matmul(ps_scores[:, 4 * j:4 * j + 4], ident_bf[:], mask_bf[:], start=True, stop=False,
                          skip_group_check=True)
                for n in range(4):
                    h = HALF * u + 4 * j + n
                    mm = pe.matmul(ps_scores[:, 4 * j + n], qT[a][0:STACK, h], kT[a][0:STACK, h // 4],
                                   start=False, stop=n == 3, skip_group_check=True)
            mm.then_inc(scored[a], 1)

        def turn_probs(b, nb, i):
            unit = unit_at(b, nb, i)
            if not unit:
                return
            a, _, _, u = unit
            wait_unit(pe, exp_done, unit)
            wait_unit(pe, prob_lo_done, unit_before(b, nb, i))
            for n in range(HALF):
                mm = pe.transpose(ps_probs[:, n], prob[u][:, n], identity)
            mm.then_inc(probs_turned[a], 1)

        def mix(b, nb, i):
            unit = unit_at(b, nb, i)
            if not unit:
                return
            a, e, ne, u = unit
            wait_unit(pe, prob_lo_done, unit)
            wait_unit(pe, heads_read, unit_before(b, nb, i))
            for n in range(HALF):
                group = GROUPS + (HALF * u + n) // 4
                v = stack[ne % 2][:, HEADS + group, 1:1 + VCOLS] if a == 0 else cross_kv[:, bass.ds(e, 1), group, 1:1 + VCOLS]
                dst = ps_heads[:, n * VCOLS:(n + 1) * VCOLS]
                pe.matmul(dst, prob_hi[u][:, n], v, start=True, stop=False)
                mm = pe.matmul(dst, prob_lo[u][:, n], v, start=False, stop=True)
            mm.then_inc(heads_done[a], 1)

        def iteration(b, nb):
            if nb == 1:
                pe.wait_ge(lo_made, 4)
            if nb == 2:
                pe.wait_ge(kv_l, 1)
            score(b, nb, 0)
            turn_stack(0, 0, 2, b, nb)
            turn_probs(b, nb, -1)
            if exists(nb - 1):
                turn_heads(1, b - 1)
            mix(b, nb, -2)
            turn_stack(1, -2, 0, b, nb)
            score(b, nb, 1)
            turn_probs(b, nb, 0)
            if exists(nb - 1):
                project(1, b, nb)
            if exists(nb + 1):
                turn_tokens(b + 1)
            mix(b, nb, -1)
            turn_stack(1, -2, 1, b, nb)
            if exists(nb + 1):
                project(0, b, nb)
            score(b, nb, 2)
            turn_probs(b, nb, 1)
            turn_stack(1, -2, 2, b, nb)
            if exists(nb - 3):
                turn_heads(2, b - 3)
            mix(b, nb, 0)
            score(b, nb, 3)
            turn_probs(b, nb, 2)
            if exists(nb - 3):
                project(2, b, nb)
            turn_stack(0, 1, 0, b, nb)
            mix(b, nb, 1)
            turn_stack(0, 1, 1, b, nb)

        pe.wait_ge(squares_loaded, 16)
        pe.wait_ge(lo_made, 1)
        pe.wait_ge(filled, 6)
        pe.wait_ge(filled_act, 3)
        over_iterations(pe, iteration)
        router_tensor(pe)
        phase_b_tensor(pe)
        phase_c_tensor(pe)

    @block.vector
    def _(dve):
        V = nc.vector

        V.memset(minus_half[:], -0.5).then_inc(filled, 1)
        V.memset(empty_rows[:, 0:ROW_ID], 0.0).then_inc(empty_made, 1)
        V.memset(empty_rows[:, ROW_ID:ROW].bitcast(I32), NO_ROW).then_inc(empty_made, 1)
        V.memset(cross_kv[:, :, :, 0:2], 1.0).then_inc(filled, 1)
        for s in range(2):
            V.memset(stack[s][:, :, 0:2], 1.0).then_inc(filled, 1)
        V.memset(rt_hi[:].bitcast(F32), 0.0).then_inc(filled, 1)
        V.memset(rt_lo[:].bitcast(F32), 0.0).then_inc(filled, 1)
        dve.wait_ge(filled, 6)
        dve.wait_ge(hi_made, 1)
        V.tensor_tensor(wqkv_lo[:], raw_qkv[:], wqkv_hi[:].bitcast(F32), ALU.subtract).then_inc(lo_made, 1)

        def ctx_squares():
            dve.wait_ge(ctx_loaded, 16)
            V.tensor_tensor(kv_a[:, :, 0:KVD], ctx_sb[:], ctx_sb[:], ALU.mult).then_inc(kv_step, 1)
            dve.wait_ge(kv_step, 1)
            V.tensor_reduce(k_rstd[:], kv_a[:, :, 0:KVD], AX.X, ALU.add).then_inc(kv_var, 1)

        def rotary_weights():
            dve.wait_ge(consts_loaded, 16 * 3)
            w_view = norm_w[:].rearrange("p (h n) -> p h n", n=HD)
            w_swap = norm_w[:].rearrange("p (h t e) -> p h t e", t=2, e=HD // 2)[:, :, ::-1, :]
            n_heads = HEADS + GROUPS
            V.tensor_tensor(cos_w[:].rearrange("p (h n) -> p h n", n=HD), w_view,
                            rope[:, 0:1, :].to_broadcast([P, n_heads, HD]), ALU.mult).then_inc(kv_step, 1)
            V.tensor_tensor(sin_w[:].rearrange("p (h t e) -> p h t e", t=2, e=HD // 2), w_swap,
                            rope[:, 1:2, :].rearrange("p o (t e) -> p o t e", t=2).to_broadcast([P, n_heads, 2, HD // 2]),
                            ALU.mult).then_inc(kv_step, 1)

        def low_weights():
            dve.wait_ge(hi_made, 4)
            V.tensor_tensor(wproj_lo[:], raw_proj[:], wproj_hi[:].bitcast(F32), ALU.subtract).then_inc(lo_made, 1)
            V.tensor_tensor(bias_lo[:], raw_bias[:], bias_hi[:].bitcast(F32), ALU.subtract).then_inc(lo_made, 1)
            V.tensor_tensor(rt_lo[:, :, 0:EXPERTS], raw_router[:], rt_hi[:, :, 0:EXPERTS].bitcast(F32), ALU.subtract).then_inc(lo_made, 1)

        def ctx_cosines():
            dve.wait_ge(kv_pow, 2)
            dve.wait_ge(kv_step, 3)
            V.tensor_tensor(kv_b[:, :, 0:KVD], ctx_sb[:], k_rstd[:].unsqueeze(2).to_broadcast([P, B, KVD]), ALU.mult).then_inc(kv_step, 1)
            dve.wait_ge(kv_step, 4)
            ck = cos_w[:, D:].unsqueeze(1).to_broadcast([P, B, KVD])
            V.tensor_tensor(kv_a[:, :, 0:KVD], kv_b[:, :, 0:KVD], ck, ALU.mult).then_inc(kv_step, 1)

        def ctx_sines():
            swapped = kv_b[:, :, 0:KVD].rearrange("p b (g t e) -> p b g t e", g=GROUPS, t=2)[:, :, :, ::-1, :]
            for g in range(GROUPS):
                sk = sin_w[:, D + g * HD:D + (g + 1) * HD].rearrange("p (t e) -> p t e", t=2)
                V.tensor_tensor(kv_a[:, :, KVD + g * HD:KVD + (g + 1) * HD].rearrange("p b (t e) -> p b t e", t=2),
                                swapped[:, :, g], sk.unsqueeze(1).to_broadcast([P, B, 2, HD // 2]),
                                ALU.mult).then_inc(kv_step, 1)
            dve.wait_ge(kv_step, 9)
            V.tensor_tensor(kv_fp[:, :, 0:KVD], kv_a[:, :, 0:KVD], kv_a[:, :, KVD:], ALU.add).then_inc(kv_src, 1)

        blocks = cross_kv[:].rearrange("p b g n -> p (b g) n")
        rest = kv_b.rearrange("p b (g n) -> p (b g) n", n=HD)

        def ctx_rest():
            dve.wait_ge(kv_h, 1)
            V.tensor_tensor(rest, kv_fp.rearrange("p b (g n) -> p (b g) n", n=HD), blocks[:, :, 2:2 + HD], ALU.subtract).then_inc(kv_r, 1)

        def ctx_last():
            dve.wait_ge(kv_m, 1)
            V.tensor_tensor(blocks[:, :, 2 + 2 * HD:2 + 3 * HD], rest, blocks[:, :, 2 + HD:2 + 2 * HD], ALU.subtract).then_inc(kv_l, 1)

        def setup_beside(nb, slot):
            if (nb, slot) == (-1, 1):
                ctx_squares()
            elif (nb, slot) == (-1, 3):
                rotary_weights()
                low_weights()
            elif (nb, slot) == (0, 0):
                dve.wait_ge(rest_loaded, 16)
                ctx_cosines()
            elif (nb, slot) == (0, 1):
                ctx_sines()
            elif (nb, slot) == (0, 3):
                ctx_rest()
            elif (nb, slot) == (1, 2):
                ctx_last()

        def norm_stats(a, e):
            V.bn_stats(bstats[:, a], tokens[:, bass.ds(e, 1), :]).then_inc(stats_done[a], 1)

        def norm_moments(a, e):
            wait_alone(dve, stats_done[a], e + 1)
            V.bn_aggr(moments[:, a], bstats[:, a]).then_inc(moments_done[a], 1)

        def normalise(a, e):
            dve.wait_ge(rstd_done[a], e + 1)
            V.tensor_scalar(xn[a][:].unsqueeze(1), tokens[:, bass.ds(e, 1), :], moments[:, a, 0:1], rstd[:, a],
                            ALU.subtract, ALU.mult).then_inc(xn_done[a], 1)

        def act_lo(k, e):
            dve.wait_ge(act_hi_done[k], e + 1)
            V.tensor_tensor(actT_lo[k % 2][:], ps_actT[:, 0:KT], actT_hi[k % 2][:].bitcast(F32), ALU.subtract).then_inc(act_lo_done[k], 1)

        def add_projected(k, e):
            dve.wait_ge(projected[k], e + 1)
            mine = tokens[:, bass.ds(e, 1), :]
            V.tensor_tensor(mine, mine, ps_proj[:, 0:D].unsqueeze(1), ALU.add).then_inc(proj_read[k], 1)

        def take_remainder(e, s):
            dve.wait_ge(parts_h[0], e + 1)
            V.tensor_tensor(remainder[0][:].rearrange("p (h n) -> p h n", n=HD),
                            ps_proj[:, 0:QKV].rearrange("p (h n) -> p h n", n=HD),
                            stack[s][:, :, 2:2 + HD], ALU.subtract).then_inc(proj_read[0], 1)

        def shift(b, nb, i):
            unit = unit_at(b, nb, i)
            if not unit:
                return
            a, _, _, u = unit
            wait_unit(dve, scored, unit)
            V.tensor_reduce(row_max[u][:], ps_scores[:], AX.X, ALU.max).then_inc(max_done[a], 1)
            wait_unit(dve, max_done, unit)
            V.tensor_tensor(prob[u][:], ps_scores[:], row_max[u][:].unsqueeze(2).to_broadcast([P, HALF, P]),
                            ALU.subtract).then_inc(shifted[a], 1)

        def probs_lo(b, nb, i):
            unit = unit_at(b, nb, i)
            if not unit:
                return
            a, _, _, u = unit
            wait_unit(dve, prob_hi_done, unit)
            V.tensor_tensor(prob_lo[u][:], ps_probs[:], prob_hi[u][:], ALU.subtract).then_inc(prob_lo_done[a], 1)

        def sum_parts(b, nb, i):
            unit = unit_at(b, nb, i)
            if not unit:
                return
            a, e, _, u = unit
            wait_unit(dve, heads_done, unit)
            o = ps_heads[:, 0:HALF * VCOLS].rearrange("p (h c) -> p h c", c=VCOLS)
            V.tensor_reduce(heads[a][:, HALF * u:HALF * (u + 1)],
                            o[:, :, 1:].rearrange("p h (c d) -> p h d c", c=3), AX.X, ALU.add).then_inc(heads_summed[a], 1)
            V.reciprocal(denom[a][:, HALF * u:HALF * (u + 1)], o[:, :, 0]).then_inc(heads_read[a], 1)

        def iteration(b, nb):
            if exists(nb + 1):
                norm_stats(0, b + 1)
            shift(b, nb, 0)
            if exists(nb + 1):
                norm_moments(0, b + 1)
            probs_lo(b, nb, -1)
            if exists(nb - 1):
                act_lo(1, b - 1)
            sum_parts(b, nb, -2)
            if exists(nb + 1):
                normalise(0, b + 1)
            setup_beside(nb, 0)
            shift(b, nb, 1)
            if exists(nb - 1):
                add_projected(1, b - 1)
            if exists(nb + 1):
                act_lo(0, b + 1)
            if exists(nb - 1):
                wait_alone(dve, proj_read[1], b)
                norm_stats(1, b - 1)
            probs_lo(b, nb, 0)
            if exists(nb - 1):
                norm_moments(1, b - 1)
            sum_parts(b, nb, -1)
            setup_beside(nb, 1)
            shift(b, nb, 2)
            if exists(nb + 1):
                take_remainder(b + 1, (nb + 1) % 2)
            probs_lo(b, nb, 1)
            if exists(nb - 1):
                normalise(1, b - 1)
            sum_parts(b, nb, 0)
            if exists(nb - 3):
                act_lo(2, b - 3)
            setup_beside(nb, 2)
            shift(b, nb, 3)
            probs_lo(b, nb, 2)
            sum_parts(b, nb, 1)
            if exists(nb - 3):
                add_projected(2, b - 3)
            setup_beside(nb, 3)

        dve.wait_ge(x_loaded, 16)
        over_iterations(dve, iteration)
        router_vector(dve)
        phase_b_vector(dve, routing_vector(dve))
        phase_c_vector(dve)

    @block.scalar
    def _(act):
        S = nc.scalar
        act.wait_ge(squares_loaded, 16)
        S.copy(ident_bf[:], identity).then_inc(filled_act, 1)
        S.copy(mask_bf[:], squares[:, 1:2].to_broadcast([P, 4, P])).then_inc(filled_act, 1)
        S.copy(first_row[:], squares[:, 3]).then_inc(filled_act, 1)
        act.wait_ge(qkv_loaded, 16 * 3)
        S.copy(wqkv_hi[:], raw_qkv[:]).then_inc(hi_made, 1)

        def high_weights():
            act.wait_ge(attn_loaded, 16 * 4)
            S.copy(wproj_hi[:], raw_proj[:]).then_inc(hi_made, 1)
            S.copy(bias_hi[:], raw_bias[:]).then_inc(hi_made, 1)
            act.wait_ge(filled, 6)
            S.copy(rt_hi[:, :, 0:EXPERTS], raw_router[:]).then_inc(hi_made, 1)

        fp = kv_fp.rearrange("p b (g n) -> p (b g) n", n=HD)
        rest = kv_b.rearrange("p b (g n) -> p (b g) n", n=HD)
        slots = cross_kv[:].rearrange("p b g n -> p (b g) n")[:, :, 2:].rearrange("p r (c n) -> p r c n", n=HD)
        two = lambda v: v.unsqueeze(2).to_broadcast([P, B * KV, 2, HD])

        def ctx_values():
            act.wait_ge(ctx_loaded, 16)
            S.copy(kv_fp[:, :, KVD:], ctx_sb[:]).then_inc(kv_src, 1)

        def ctx_high():
            act.wait_ge(kv_src, 2)
            S.copy(slots[:, :, 0::3], two(fp))
            S.copy(slots[:, :, 5], fp).then_inc(kv_h, 1)

        def ctx_middle():
            act.wait_ge(kv_r, 1)
            S.copy(slots[:, :, 1::3], two(rest)).then_inc(kv_m, 1)

        def setup_beside(nb, slot):
            if (nb, slot) == (-1, 2):
                high_weights()
                ctx_values()
            elif (nb, slot) == (0, 2):
                ctx_high()
            elif (nb, slot) == (1, 1):
                ctx_middle()

        def act_hi(k, e):
            act.wait_ge(act_turned[k], e + 1)
            S.copy(actT_hi[k % 2][:], ps_actT[:, 0:KT]).then_inc(act_hi_done[k], 1)

        def in_slots(blocks):
            return blocks[:, :, 2:].rearrange("p h (c n) -> p h c n", n=HD)

        def high_parts_self(e, s):
            act.wait_ge(projected[0], e + 1)
            q = ps_proj[:, 0:D].rearrange("p (h n) -> p h n", n=HD)
            kv = ps_proj[:, D:QKV].rearrange("p (h n) -> p h n", n=HD)
            in_kv, in_q = in_slots(stack[s][:, HEADS:]), in_slots(stack[s][:, 0:HEADS])
            S.copy(in_kv[:, :, 0::3], kv.unsqueeze(2).to_broadcast([P, KV, 2, HD]))
            S.copy(in_kv[:, :, 5], kv)
            S.copy(in_q[:, :, 0:3], q.unsqueeze(2).to_broadcast([P, HEADS, 3, HD])).then_inc(parts_h[0], 1)

        def middle_parts_self(e, s):
            act.wait_ge(proj_read[0], e + 1)
            r = remainder[0][:].rearrange("p (h n) -> p h n", n=HD)
            in_kv, in_q = in_slots(stack[s][:, HEADS:]), in_slots(stack[s][:, 0:HEADS])
            S.copy(in_kv[:, :, 1::3], r[:, HEADS:].unsqueeze(2).to_broadcast([P, KV, 2, HD]))
            S.copy(in_q[:, :, 3:5], r[:, 0:HEADS].unsqueeze(2).to_broadcast([P, HEADS, 2, HD])).then_inc(parts_m[0], 1)

        def high_parts_cross(e):
            act.wait_ge(q_done, e + 1)
            q = q_fp[:].rearrange("p (h n) -> p h n", n=HD)
            S.copy(in_slots(cross_stack)[:, :, 0:3], q.unsqueeze(2).to_broadcast([P, HEADS, 3, HD])).then_inc(parts_h[1], 1)

        def middle_parts_cross(e):
            act.wait_ge(q_rest, e + 1)
            r = remainder[1][:, 0:D].rearrange("p (h n) -> p h n", n=HD)
            S.copy(in_slots(cross_stack)[:, :, 3:5], r.unsqueeze(2).to_broadcast([P, HEADS, 2, HD])).then_inc(parts_m[1], 1)

        def keep_stack(a, offset, g, b, nb):
            if not exists(nb + offset):
                return
            act.wait_ge(stack_turned[a], 3 * (b + offset) + g + 1)
            if g == 0:
                S.copy(kT[a][0:STACK], ps_stack[0:STACK, 0:GROUPS]).then_inc(stack_kept[a], 1)
            else:
                S.copy(qT[a][0:STACK, HALF * (g - 1):HALF * g], ps_stack[0:STACK]).then_inc(stack_kept[a], 1)

        def exponentials(b, nb, i):
            unit = unit_at(b, nb, i)
            if not unit:
                return
            a, _, _, u = unit
            wait_unit(act, shifted, unit)
            S.activation(prob[u][:], prob[u][:], ACT.Exp, scale=SCALE).then_inc(exp_done[a], 1)

        def probs_hi(b, nb, i):
            unit = unit_at(b, nb, i)
            if not unit:
                return
            a, _, _, u = unit
            wait_unit(act, probs_turned, unit)
            S.copy(prob_hi[u][:], ps_probs[:]).then_inc(prob_hi_done[a], 1)

        def share(b, nb):
            if nb == 0:
                act.wait_ge(shared_loaded, 16 * 5)
            for hi, src, n in SHARES:
                S.copy(hi[:, bass.ds(n * b, n)], src[:, bass.ds(n * b, n)]).then_inc(shared_hi, 1)

        def iteration(b, nb):
            keep_stack(0, 0, 2, b, nb)
            probs_hi(b, nb, -1)
            if exists(nb - 1):
                act_hi(1, b - 1)
            exponentials(b, nb, 0)
            keep_stack(1, -2, 0, b, nb)
            if exists(nb - 2):
                middle_parts_cross(b - 2)
            if exists(nb - 3):
                share(b - 3, nb - 3)
            setup_beside(nb, 0)
            probs_hi(b, nb, 0)
            if exists(nb + 1):
                act_hi(0, b + 1)
            keep_stack(1, -2, 1, b, nb)
            exponentials(b, nb, 1)
            setup_beside(nb, 1)
            if exists(nb + 1):
                high_parts_self(b + 1, (nb + 1) % 2)
            probs_hi(b, nb, 1)
            keep_stack(1, -2, 2, b, nb)
            exponentials(b, nb, 2)
            if exists(nb - 3):
                act_hi(2, b - 3)
            if exists(nb + 1):
                middle_parts_self(b + 1, (nb + 1) % 2)
            setup_beside(nb, 2)
            keep_stack(0, 1, 0, b, nb)
            probs_hi(b, nb, 2)
            keep_stack(0, 1, 1, b, nb)
            exponentials(b, nb, 3)
            if exists(nb - 1):
                high_parts_cross(b - 1)

        over_iterations(act, iteration)
        router_scalar(act)
        phase_b_scalar(act)
        phase_c_scalar(act)

    @block.gpsimd
    def _(pool):
        G = nc.gpsimd
        pool.wait_ge(filled, 6)

        def ctx_scale():
            pool.wait_ge(kv_var, 1)
            G.tensor_scalar(k_rstd[:], k_rstd[:], 1.0 / KVD, EPS, ALU.mult, ALU.add).then_inc(kv_pow, 1)
            pool.wait_ge(kv_pow, 1)
            G.tensor_tensor(k_rstd[:], k_rstd[:], minus_half[:], ALU.pow).then_inc(kv_pow, 1)

        def finish_heads(a, e):
            pool.wait_ge(heads_summed[a], 2 * e + 2)
            pool.wait_ge(heads_read[a], 2 * e + 2)
            G.tensor_tensor(mixed[a][:], heads[a][:], denom[a][:].unsqueeze(2).to_broadcast([P, HEADS, HD]),
                            ALU.mult).then_inc(mixed_done[a], 1)

        def norm_scale(a, e, mul, add):
            wait_alone(pool, moments_done[a], e + 1)
            G.tensor_scalar(variance[:, a], moments[:, a, 1:2], mul, add, ALU.mult, ALU.add).then_inc(var_eps[a], 1)
            pool.wait_ge(var_eps[a], e + 1)
            G.tensor_tensor(rstd[:, a], variance[:, a], minus_half[:, 0:1], ALU.pow).then_inc(rstd_done[a], 1)

        def low_parts(a, e, blocks):
            pool.wait_ge(parts_m[a], e + 1)
            r = remainder[a][:].rearrange("p (h n) -> p h n", n=HD)
            if a == 0:
                kv = blocks[:, HEADS:]
                G.tensor_tensor(kv[:, :, 2 + 2 * HD:2 + 3 * HD], r[:, HEADS:], kv[:, :, 2 + 4 * HD:2 + 5 * HD], ALU.subtract)
            q = blocks[:, 0:HEADS]
            G.tensor_tensor(q[:, :, 2 + 5 * HD:2 + 6 * HD], r[:, 0:HEADS], q[:, :, 2 + 4 * HD:2 + 5 * HD], ALU.subtract).then_inc(parts_l[a], 1)

        def rotate(e):
            pool.wait_ge(xn_done[1], e + 1)
            G.tensor_tensor(q_fp[:], xn[1][:], cos_w[:, 0:D], ALU.mult).then_inc(rope_step, 1)
            half = lambda v: v.rearrange("p (h t e) -> p h t e", t=2, e=HD // 2)
            G.tensor_tensor(half(q_sin[:]), half(xn[1][:])[:, :, ::-1, :], half(sin_w[:, 0:D]), ALU.mult).then_inc(rope_step, 1)
            pool.wait_ge(rope_step, 2 * e + 2)
            G.tensor_tensor(q_fp[:], q_fp[:], q_sin[:], ALU.add).then_inc(q_done, 1)

        def rest_of_q(e):
            pool.wait_ge(parts_h[1], e + 1)
            G.tensor_tensor(remainder[1][:, 0:D].rearrange("p (h n) -> p h n", n=HD),
                            q_fp[:].rearrange("p (h n) -> p h n", n=HD),
                            cross_stack[:, :, 2:2 + HD], ALU.subtract).then_inc(q_rest, 1)

        def share(b):
            pool.wait_ge(shared_hi, 2 * b + 2)
            for lo, hi, src, n in LOW_SHARES:
                G.tensor_tensor(lo[:, bass.ds(n * b, n)], src[:, bass.ds(n * b, n)],
                                hi[:, bass.ds(n * b, n)].bitcast(F32), ALU.subtract).then_inc(shared_lo, 1)

        def iteration(b, nb):
            if exists(nb + 1):
                norm_scale(0, b + 1, 1.0, EPS)
            if exists(nb - 2):
                low_parts(1, b - 2, cross_stack)
            if exists(nb - 3):
                share(b - 3)
            if exists(nb - 1):
                norm_scale(1, b - 1, 1.0 + EPS, EPS * EPS)
            if exists(nb - 3):
                finish_heads(1, b - 3)
            if exists(nb + 1):
                low_parts(0, b + 1, stack[(nb + 1) % 2])
            if nb == -1:
                ctx_scale()
            if nb == 1:
                pool.wait_ge(kv_step, 3)
            if exists(nb - 1):
                rotate(b - 1)
                rest_of_q(b - 1)
            if exists(nb):
                finish_heads(0, b)

        over_iterations(pool, iteration)
        router_pool(pool)
        routing_pool(pool)
        phase_c_pool(pool)

    block.__exit__(None, None, None)
    sems.close()
    top.close()


_INS = {"x": "x", "ctx_512": "ctx_512", "wq": "L0_attn_Wq", "wk": "L0_attn_Wk", "wv": "L0_attn_Wv", "wo": "L0_attn_Wo",
        "bo": "L0_attn_bo", "q_norm": "L0_xattn_q_norm_w", "k_norm": "L0_xattn_k_norm_w",
        "w_out_t": "L0_xattn_w_out", "router": "L0_ffn_router_w", "w1": "L0_ffn_w1", "w2": "L0_ffn_w2",
        "w_gate": "L0_ffn_w_gate", "w_up": "L0_ffn_w_up", "w_down": "L0_ffn_w_down"}


def kernel(**inputs):
    import concourse.bacc as bacc
    from concourse.bass_utils import run_bass_kernel_spmd

    arrays = {}
    for name, source in _INS.items():
        w = np.asarray(inputs[source])
        arrays[name] = np.ascontiguousarray(w.T if name == "w_out_t" else w)
    B = arrays["x"].shape[0]
    tiles = B * TOPK + EXPERTS
    arrays["squares"], arrays["rope"], arrays["lanes"], arrays["row_ids"] = constants(B, tiles)
    nc = bacc.Bacc("TRN2", target_bir_lowering=False, num_devices=1)
    aps = {name: nc.dram_tensor(f"in_{name}", v.shape, mybir.dt.from_np(v.dtype), kind="ExternalInput").ap()
           for name, v in arrays.items()}
    out = nc.dram_tensor("out", arrays["x"].shape, F32, kind="ExternalOutput").ap()
    decoder_layer(nc, aps, out)
    ran = run_bass_kernel_spmd(nc, [{f"in_{name}": v for name, v in arrays.items()}], core_ids=[0])
    return ran.results[0]["out"]
```
